# Optimizing a Trainium2 kernel written in Bass

```python
import numpy as np
import jax
import jax.numpy as jnp

def _softmax(x, axis=-1):
    return jax.nn.softmax(x, axis=axis)

def _gelu(x):
    return jax.nn.gelu(x, approximate=True)

def _silu(x):
    return jax.nn.silu(x)

def _sigmoid(x):
    return jax.nn.sigmoid(x)

def _layernorm(x, axis=-1, eps=1e-05):
    m = jnp.mean(x, axis=axis, keepdims=True)
    v = jnp.var(x, axis=axis, keepdims=True)
    return (x - m) / jnp.sqrt(v + eps)

def _scatter_add(tgt, idx, src, axis=0):
    return tgt.at[idx].add(src)

def _segment_sum(src, seg, n):
    return jax.ops.segment_sum(src, seg, n)
kernel_name = 'mk_pixart_seq_d2_seqx_r4_8fe15a'

def setup_inputs(seed: int=0):
    np.random.seed(seed)
    _w = jnp.asarray

    def _rec_inputs():
        import jax
        import jax.numpy as jnp
        _rk = jax.random.key(seed)
        x = -0.0003929 + 0.9999 * jax.random.normal(jax.random.fold_in(_rk, 1), (4, 1024, 256), jnp.float32)
        _lenS = 1024 - jax.random.randint(jax.random.fold_in(_rk, 7), (4,), 0, max(1, 1024 // 4) + 1, jnp.int32)
        _lenS2 = 77 - jax.random.randint(jax.random.fold_in(_rk, 8), (4,), 0, max(1, 77 // 4) + 1, jnp.int32)
        _ctx_1024P = jax.random.normal(jax.random.fold_in(_rk, 11), (4, 16, 256), jnp.float32)
        _ctx_1024c = jax.random.dirichlet(jax.random.fold_in(_rk, 511), 0.3 * jnp.ones((16,), jnp.float32), (4, 77))
        _ctx_1024t = jnp.einsum('bsk,bkd->bsd', _ctx_1024c, _ctx_1024P)
        _ctx_1024t = _ctx_1024t * jax.lax.rsqrt(jnp.mean(jnp.square(_ctx_1024t)) + 1e-12) * 0.953939
        ctx_1024 = -1.39393e-06 + 0.999914 * (_ctx_1024t + 0.3 * jax.random.normal(jax.random.fold_in(_rk, 611), (4, 77, 256), jnp.float32))
        cond_1024 = -0.00920427 + 1.00102 * jax.random.normal(jax.random.fold_in(_rk, 12), (4, 256), jnp.float32)
        _validS = jnp.arange(1024)[None, :] < _lenS[:, None]
        _validS2 = jnp.arange(77)[None, :] < _lenS2[:, None]
        _causal = jnp.tril(jnp.ones((1024, 1024), dtype=bool))
        mask_BxS2_bf1 = jnp.ones((4, 77), dtype=bool)
        mask_SxS_bk0 = jnp.logical_not(jnp.broadcast_to(_validS[0:1, :], (1024, 1024)))
        return (x, ctx_1024, cond_1024, mask_BxS2_bf1, mask_SxS_bk0)
    x, ctx_1024, cond_1024, mask_BxS2_bf1, mask_SxS_bk0 = _rec_inputs()

    def _L0_xcond_setup():
        import jax, jax.numpy as jnp
        import numpy as np
        EPS = 1e-05

        def _ada_ln(x, c, W_ss, b_ss):
            mu = jnp.mean(x, axis=-1, keepdims=True)
            var = jnp.mean((x - mu) ** 2, axis=-1, keepdims=True)
            h = (x - mu) / jnp.sqrt(var + EPS)
            ss = jax.nn.silu(c) @ W_ss + b_ss
            scale, bias = jnp.split(ss, 2, axis=-1)
            return (1.0 + scale)[:, None, :] * h + bias[:, None, :]
        key = jax.random.key(seed)
        ks = jax.random.split(key, 12)
        B, Lq, Lkv, H = (8, 512, 128, 256)
        s = 0.02
        return {'x_q': jax.random.normal(ks[0], (B, Lq, H), jnp.float32), 'x_kv': jax.random.normal(ks[1], (B, Lkv, H), jnp.float32), 't_vec': jax.random.normal(ks[2], (B, H), jnp.float32), 'Wq': jax.random.normal(ks[3], (H, H), jnp.float32) * s, 'bq': jnp.zeros((H,), jnp.float32), 'Wkv': jax.random.normal(ks[4], (H, 2 * H), jnp.float32) * s, 'bkv': jnp.zeros((2 * H,), jnp.float32), 'Wp': jax.random.normal(ks[5], (H, H), jnp.float32) * s, 'bp': jnp.zeros((H,), jnp.float32), 'Wss_q': jax.random.normal(ks[6], (H, 2 * H), jnp.float32) * s, 'bss_q': jnp.zeros((2 * H,), jnp.float32), 'Wss_kv': jax.random.normal(ks[7], (H, 2 * H), jnp.float32) * s, 'bss_kv': jnp.zeros((2 * H,), jnp.float32)}
    _L0_xcond_all = _L0_xcond_setup()
    _L0_xcond_in = {k: v for k, v in _L0_xcond_all.items() if k in ('Wq', 'bq', 'Wkv', 'bkv', 'Wp', 'bp', 'Wss_q', 'bss_q', 'Wss_kv', 'bss_kv')}
    del _L0_xcond_all

    def _L1_xcond_setup():
        import jax, jax.numpy as jnp
        import numpy as np
        B, N, D, H, LC = (2, 256, 256, 16, 77)
        HD = D // H
        BLOCK = 16
        ROPE_BASE = 10000.0
        EPS = 1e-05

        def _block_diff_mask(n, block_size):
            idx = np.arange(2 * n)
            q = idx[:, None]
            kv = idx[None, :]
            fq = q >= n
            fkv = kv >= n
            bq = np.where(fq, (q - n) // block_size, q // block_size)
            bkv = np.where(fkv, (kv - n) // block_size, kv // block_size)
            block_diagonal = (bq == bkv) & (fq == fkv)
            offset_block_causal = (bq > bkv) & fkv & ~fq
            block_causal = (bq >= bkv) & fq & fkv
            return jnp.asarray(block_diagonal | offset_block_causal | block_causal)

        def _rope_tables(n):
            inv_freq = 1.0 / ROPE_BASE ** (np.arange(0, HD, 2, dtype=np.float32) / HD)
            freqs = np.outer(np.arange(n, dtype=np.float32), inv_freq)
            emb = np.concatenate([freqs, freqs], axis=-1)
            cos = jnp.asarray(np.cos(emb), jnp.float32)[None, :, None, :]
            sin = jnp.asarray(np.sin(emb), jnp.float32)[None, :, None, :]
            return (cos, sin)

        def _ln(x, w):
            xf = x.astype(jnp.float32)
            mu = jnp.mean(xf, axis=-1, keepdims=True)
            var = jnp.mean(jnp.square(xf - mu), axis=-1, keepdims=True)
            y = (xf - mu) * jax.lax.rsqrt(var + EPS)
            return y * w[None, None, :]

        def _apply_rope(t, cos, sin):
            t1, t2 = jnp.split(t, 2, axis=-1)
            rot = jnp.concatenate([-t2, t1], axis=-1)
            return t * cos + rot * sin

        def _attn(q, k, v, mask):
            scale = 1.0 / np.sqrt(HD)
            s = jnp.einsum('bqhd,bkhd->bhqk', q, k) * scale
            s = jnp.where(mask, s, jnp.finfo(s.dtype).min)
            a = jax.nn.softmax(s, axis=-1)
            return jnp.einsum('bhqk,bkhd->bqhd', a, v)
        key = jax.random.key(seed)
        ks = jax.random.split(key, 16)
        w = lambda k, shp: jax.random.normal(k, shp, jnp.float32) * 0.02
        inp = {'x': jax.random.normal(ks[0], (B, 2 * N, D), jnp.float32), 'cond_global': jax.random.normal(ks[1], (B, D), jnp.float32), 'cond_tokens': jax.random.normal(ks[2], (B, LC, D), jnp.float32), 'adaLN_W': w(ks[3], (D, 9 * D)), 'adaLN_b': w(ks[4], (9 * D,)), 'norm1_w': jnp.ones((D,), jnp.float32), 'qkv_W': w(ks[5], (D, 3 * D)), 'attn_out_W': w(ks[6], (D, D)), 'normc_w': jnp.ones((D,), jnp.float32), 'cq_W': w(ks[7], (D, D)), 'ck_W': w(ks[8], (D, D)), 'cv_W': w(ks[9], (D, D)), 'co_W': w(ks[10], (D, D)), 'norm2_w': jnp.ones((D,), jnp.float32), 'mlp_W1': w(ks[11], (D, 4 * D)), 'mlp_b1': w(ks[12], (4 * D,)), 'mlp_W2': w(ks[13], (4 * D, D)), 'mlp_b2': w(ks[14], (D,)), 'cond_kv_mask': jnp.ones((B, LC), bool), 'attn_mask': _block_diff_mask(N, BLOCK)}
        return inp
    _L1_xcond_all = _L1_xcond_setup()
    _L1_xcond_in = {k: v for k, v in _L1_xcond_all.items() if k in ('adaLN_W', 'adaLN_b', 'norm1_w', 'qkv_W', 'attn_out_W', 'normc_w', 'cq_W', 'ck_W', 'cv_W', 'co_W', 'norm2_w', 'mlp_W1', 'mlp_b1', 'mlp_W2', 'mlp_b2')}
    del _L1_xcond_all
    return {'x': x, 'ctx_1024': ctx_1024, 'cond_1024': cond_1024, 'mask_BxS2_bf1': mask_BxS2_bf1, 'mask_SxS_bk0': mask_SxS_bk0, 'L0_xcond_Wq': _L0_xcond_in['Wq'], 'L0_xcond_bq': _L0_xcond_in['bq'], 'L0_xcond_Wkv': _L0_xcond_in['Wkv'], 'L0_xcond_bkv': _L0_xcond_in['bkv'], 'L0_xcond_Wp': _L0_xcond_in['Wp'], 'L0_xcond_bp': _L0_xcond_in['bp'], 'L0_xcond_Wss_q': _L0_xcond_in['Wss_q'], 'L0_xcond_bss_q': _L0_xcond_in['bss_q'], 'L0_xcond_Wss_kv': _L0_xcond_in['Wss_kv'], 'L0_xcond_bss_kv': _L0_xcond_in['bss_kv'], 'L1_xcond_adaLN_W': _L1_xcond_in['adaLN_W'], 'L1_xcond_adaLN_b': _L1_xcond_in['adaLN_b'], 'L1_xcond_norm1_w': _L1_xcond_in['norm1_w'], 'L1_xcond_qkv_W': _L1_xcond_in['qkv_W'], 'L1_xcond_attn_out_W': _L1_xcond_in['attn_out_W'], 'L1_xcond_normc_w': _L1_xcond_in['normc_w'], 'L1_xcond_cq_W': _L1_xcond_in['cq_W'], 'L1_xcond_ck_W': _L1_xcond_in['ck_W'], 'L1_xcond_cv_W': _L1_xcond_in['cv_W'], 'L1_xcond_co_W': _L1_xcond_in['co_W'], 'L1_xcond_norm2_w': _L1_xcond_in['norm2_w'], 'L1_xcond_mlp_W1': _L1_xcond_in['mlp_W1'], 'L1_xcond_mlp_b1': _L1_xcond_in['mlp_b1'], 'L1_xcond_mlp_W2': _L1_xcond_in['mlp_W2'], 'L1_xcond_mlp_b2': _L1_xcond_in['mlp_b2']}

def reference(x, ctx_1024, cond_1024, mask_BxS2_bf1, mask_SxS_bk0, L0_xcond_Wq, L0_xcond_bq, L0_xcond_Wkv, L0_xcond_bkv, L0_xcond_Wp, L0_xcond_bp, L0_xcond_Wss_q, L0_xcond_bss_q, L0_xcond_Wss_kv, L0_xcond_bss_kv, L1_xcond_adaLN_W, L1_xcond_adaLN_b, L1_xcond_norm1_w, L1_xcond_qkv_W, L1_xcond_attn_out_W, L1_xcond_normc_w, L1_xcond_cq_W, L1_xcond_ck_W, L1_xcond_cv_W, L1_xcond_co_W, L1_xcond_norm2_w, L1_xcond_mlp_W1, L1_xcond_mlp_b1, L1_xcond_mlp_W2, L1_xcond_mlp_b2):
    import jax
    import jax.numpy as jnp

    def _L0_xcond_ref(x_q, x_kv, t_vec, Wq, bq, Wkv, bkv, Wp, bp, Wss_q, bss_q, Wss_kv, bss_kv):
        import jax, jax.numpy as jnp
        import numpy as np
        EPS = 1e-05

        def _ada_ln(x, c, W_ss, b_ss):
            mu = jnp.mean(x, axis=-1, keepdims=True)
            var = jnp.mean((x - mu) ** 2, axis=-1, keepdims=True)
            h = (x - mu) / jnp.sqrt(var + EPS)
            ss = jax.nn.silu(c) @ W_ss + b_ss
            scale, bias = jnp.split(ss, 2, axis=-1)
            return (1.0 + scale)[:, None, :] * h + bias[:, None, :]
        B, Lq, H = x_q.shape
        Lkv = x_kv.shape[1]
        nh = 16
        dh = H // nh
        xq = _ada_ln(x_q, t_vec, Wss_q, bss_q)
        xkv = _ada_ln(x_kv, t_vec, Wss_kv, bss_kv)
        q = (xq @ Wq + bq).reshape(B, Lq, nh, dh)
        kv = (xkv @ Wkv + bkv).reshape(B, Lkv, 2, nh, dh)
        k = kv[:, :, 0]
        v = kv[:, :, 1]
        scores = jnp.einsum('bqhd,bkhd->bhqk', q, k) / jnp.sqrt(jnp.float32(dh))
        attn = jax.nn.softmax(scores, axis=-1)
        out = jnp.einsum('bhqk,bkhd->bqhd', attn, v).reshape(B, Lq, H)
        return x_q + (out @ Wp + bp)

    def _L1_xcond_ref(x, cond_global, cond_tokens, adaLN_W, adaLN_b, norm1_w, qkv_W, attn_out_W, normc_w, cq_W, ck_W, cv_W, co_W, norm2_w, mlp_W1, mlp_b1, mlp_W2, mlp_b2, cond_kv_mask, attn_mask):
        import jax, jax.numpy as jnp
        import numpy as np
        B, N, D, H, LC = (2, 256, 256, 16, 77)
        HD = D // H
        BLOCK = 16
        ROPE_BASE = 10000.0
        EPS = 1e-05

        def _block_diff_mask(n, block_size):
            idx = np.arange(2 * n)
            q = idx[:, None]
            kv = idx[None, :]
            fq = q >= n
            fkv = kv >= n
            bq = np.where(fq, (q - n) // block_size, q // block_size)
            bkv = np.where(fkv, (kv - n) // block_size, kv // block_size)
            block_diagonal = (bq == bkv) & (fq == fkv)
            offset_block_causal = (bq > bkv) & fkv & ~fq
            block_causal = (bq >= bkv) & fq & fkv
            return jnp.asarray(block_diagonal | offset_block_causal | block_causal)

        def _rope_tables(n):
            inv_freq = 1.0 / ROPE_BASE ** (np.arange(0, HD, 2, dtype=np.float32) / HD)
            freqs = np.outer(np.arange(n, dtype=np.float32), inv_freq)
            emb = np.concatenate([freqs, freqs], axis=-1)
            cos = jnp.asarray(np.cos(emb), jnp.float32)[None, :, None, :]
            sin = jnp.asarray(np.sin(emb), jnp.float32)[None, :, None, :]
            return (cos, sin)

        def _ln(x, w):
            xf = x.astype(jnp.float32)
            mu = jnp.mean(xf, axis=-1, keepdims=True)
            var = jnp.mean(jnp.square(xf - mu), axis=-1, keepdims=True)
            y = (xf - mu) * jax.lax.rsqrt(var + EPS)
            return y * w[None, None, :]

        def _apply_rope(t, cos, sin):
            t1, t2 = jnp.split(t, 2, axis=-1)
            rot = jnp.concatenate([-t2, t1], axis=-1)
            return t * cos + rot * sin

        def _attn(q, k, v, mask):
            scale = 1.0 / np.sqrt(HD)
            s = jnp.einsum('bqhd,bkhd->bhqk', q, k) * scale
            s = jnp.where(mask, s, jnp.finfo(s.dtype).min)
            a = jax.nn.softmax(s, axis=-1)
            return jnp.einsum('bhqk,bkhd->bqhd', a, v)
        b, s, d = x.shape
        n = s // 2
        mod = (cond_global @ adaLN_W + adaLN_b)[:, None, :]
        sh_msa, sc_msa, g_msa, sh_x, sc_x, g_x, sh_mlp, sc_mlp, g_mlp = jnp.split(mod, 9, axis=-1)
        x_norm = _ln(x, norm1_w) * (1 + sc_msa) + sh_msa
        cos, sin = _rope_tables(n)

        def qkv(h):
            t = (h @ qkv_W).reshape(b, n, 3, H, HD)
            q, k, v = (t[:, :, 0], t[:, :, 1], t[:, :, 2])
            return (_apply_rope(q, cos, sin), _apply_rope(k, cos, sin), v)
        q1, k1, v1 = qkv(x_norm[:, :n])
        q2, k2, v2 = qkv(x_norm[:, n:])
        q = jnp.concatenate([q1, q2], axis=1)
        k = jnp.concatenate([k1, k2], axis=1)
        v = jnp.concatenate([v1, v2], axis=1)
        self_out = _attn(q, k, v, attn_mask[None, None]).reshape(b, s, d) @ attn_out_W
        x = x + g_msa * self_out
        xc = _ln(x, normc_w) * (1 + sc_x) + sh_x
        qc = (xc @ cq_W).reshape(b, s, H, HD)
        kc = (cond_tokens @ ck_W).reshape(b, LC, H, HD)
        vc = (cond_tokens @ cv_W).reshape(b, LC, H, HD)
        cross = _attn(qc, kc, vc, cond_kv_mask[:, None, None, :]).reshape(b, s, d) @ co_W
        x = x + g_x * cross
        xm = _ln(x, norm2_w) * (1 + sc_mlp) + sh_mlp
        h = jax.nn.gelu(xm @ mlp_W1 + mlp_b1, approximate=True)
        mlp_out = h @ mlp_W2 + mlp_b2
        return x + g_mlp * mlp_out
    x = _L0_xcond_ref(x, ctx_1024, cond_1024, L0_xcond_Wq, L0_xcond_bq, L0_xcond_Wkv, L0_xcond_bkv, L0_xcond_Wp, L0_xcond_bp, L0_xcond_Wss_q, L0_xcond_bss_q, L0_xcond_Wss_kv, L0_xcond_bss_kv)
    x = _L1_xcond_ref(x, cond_1024, ctx_1024, L1_xcond_adaLN_W, L1_xcond_adaLN_b, L1_xcond_norm1_w, L1_xcond_qkv_W, L1_xcond_attn_out_W, L1_xcond_normc_w, L1_xcond_cq_W, L1_xcond_ck_W, L1_xcond_cv_W, L1_xcond_co_W, L1_xcond_norm2_w, L1_xcond_mlp_W1, L1_xcond_mlp_b1, L1_xcond_mlp_W2, L1_xcond_mlp_b2, mask_BxS2_bf1, mask_SxS_bk0)
    return x

_drawn_inputs = setup_inputs


def setup_inputs(seed=0):
    import zlib

    import numpy as np

    out = dict(_drawn_inputs(seed))
    spreads = {'L0_xcond_bq': (0.0, 2.0),
     'L0_xcond_bkv': (0.0, 0.1),
     'L0_xcond_bp': (0.0, 0.1),
     'L0_xcond_bss_q': (0.0, 0.8),
     'L0_xcond_bss_kv': (0.0, 0.649),
     'L1_xcond_norm1_w': (1.0, 0.6),
     'L1_xcond_normc_w': (1.0, 0.6),
     'L1_xcond_norm2_w': (1.0, 0.6)}
    factors = {'L0_xcond_Wq': 8.0,
     'L0_xcond_Wss_q': 8.0,
     'L1_xcond_adaLN_b': 8.0,
     'L1_xcond_qkv_W': 3.203,
     'L1_xcond_attn_out_W': 3.174,
     'L1_xcond_cq_W': 8.0,
     'L1_xcond_ck_W': 8.0,
     'L1_xcond_cv_W': 3.406,
     'L1_xcond_co_W': 3.347,
     'L1_xcond_mlp_b1': 26.587,
     'L1_xcond_mlp_b2': 8.0}
    for name, (base, spread) in spreads.items():
        noise = np.random.default_rng([zlib.crc32(name.encode()), seed]).standard_normal(out[name].shape)
        drawn = base * np.exp(spread * noise) if base else spread * noise
        out[name] = jnp.asarray(drawn.astype(out[name].dtype))
    for name, factor in factors.items():
        out[name] = (out[name] * factor).astype(out[name].dtype)
    return out
```

```python
from contextlib import ExitStack

import concourse.bass as bass
from concourse import mybir

F32 = mybir.dt.float32
BF16 = mybir.dt.bfloat16
U8 = mybir.dt.uint8
I32 = mybir.dt.int32
ALU = mybir.AluOpType
ACT = mybir.ActivationFunctionType
AX_X = mybir.AxisListType.X

P = 128
B, S, D = 4, 1024, 256
C = D // P
T = S // P
HALF = 512
NH, HD = 16, 16
LC = 77
HPC = P // HD
FF = 4 * D
EPS = 1e-5
SCALE = HD ** -0.5
MASKED = -1e30
N_SLOT = 6
Q_SLOTS = (0, 0, 1, 0, 2, 1)
K_SLOTS = (0, 1, 0, 2, 0, 1)
BIAS_ROW = N_SLOT * HD
MAX_ROWS = BIAS_ROW + 1
STACK = MAX_ROWS + 3

CONST_COLS = dict(ident=(0, P), cos=(P, S // 2), sin=(P + S // 2, S // 2),
                  before=(P + S, T), iota=(P + S + T, T), tile=(P + S + 2 * T, 1))
CONST_N = P + S + 2 * T + 1

VEC_ROWS = {}
_at = 0
for _name, _n in (("bss_q", 4), ("bss_kv", 4), ("adaLN_b", 18), ("bq", 2), ("bkv", 4), ("norm1_w", 2),
                  ("normc_w", 2), ("norm2_w", 2), ("mlp_b1", 8), ("bp", 2), ("mlp_b2", 2)):
    VEC_ROWS[_name] = (_at, _n)
    _at += _n
N_VEC = _at
N_MOD = 26
NORMS = dict(q0=(0, 2), kv0=(4, 6), n1=(10, 8), nc=(16, 14), n2=(22, 20))
GATES = dict(msa=12, x=18, mlp=24)


class Signal:

    def __init__(self, sem):
        self.sem, self.at = sem, 0

    def reserve(self, n):
        start = self.at
        self.at += n
        return start


def build(nc, a, out):
    ctx = ExitStack()
    with ctx:
        def sb(name, shape, dt=F32):
            return ctx.enter_context(nc.sbuf_tensor(name, shape, dt))

        const = sb("const", [P, CONST_N])

        def constant(name):
            at, n = CONST_COLS[name]
            return const[:, at:at + n]

        ident, cos_k, sin_k = constant("ident"), constant("cos"), constant("sin")
        ident_bf = sb("ident_bf", [P, P], BF16)
        rope_q = sb("rope_q", [P, 2, S])
        w_q = sb("w_q", [P, C, D])
        w_p = sb("w_p", [P, C, D])
        w_qkv = sb("w_qkv", [P, C, 3 * D])
        w_out = sb("w_out", [P, C, D])
        w_cq = sb("w_cq", [P, C, D])
        w_co = sb("w_co", [P, C, D])
        w_1 = sb("w_1", [P, C, FF])
        w_2 = sb("w_2", [P, FF // P, D])
        vec = sb("vec", [P, N_VEC])
        affine = sb("affine", [P, B, 5, 2, C])
        gates = sb("gates", [P, B, 4, C])
        affine_b = sb("affine_b", [P, 5, 2, C])
        gates_b = sb("gates_b", [P, 4, C])
        bp_row = sb("bp_row", [P, D])
        gb2_row = sb("gb2_row", [P, D])
        spread = sb("spread", [P, 2, P])
        x = sb("x", [P, T, D])
        xT = sb("xT", [P, C, S])
        sums = sb("sums", [P, C, S])
        arena_a = sb("arena_a", [P, 8192])
        arena_r = sb("arena_r", [P, 8192])
        k_parts = sb("k_parts", [P, 3, C, S], BF16)
        v_self = sb("v_self", [P, T, D])
        v_ctx = sb("v_ctx", [P, B, 2, D])
        v_pad = sb("v_pad", [P, NH, 2 * HD])
        ones_pad = sb("ones_pad", [P, 2, 2 * HD])
        k_ctx = sb("k_ctx", [P, NH, B * 2 * P], BF16)
        k_self = sb("k_self", [P, NH, P], BF16)
        mask_bias = sb("mask_bias", [P, T, S], BF16)
        ones_row = sb("ones_row", [NH, S], BF16)
        tile_list = sb("tile_list", [1, 1 + T], I32)
        stats = sb("stats", [P, T, 6])
        mean_var = sb("mean_var", [P, T, 2])
        var_eps = sb("var_eps", [P, T])
        rstd = sb("rstd", [P, T])
        minus_half = sb("minus_half", [P, T])
        neg_max = sb("neg_max", [P, T * NH])
        max_rest, tile_max = spread[:, 0, :], spread[:, 1, :]
        max_parts = sb("max_parts", [P, 3, P], BF16)

        q_stack = arena_a[:, :].bitcast(BF16).rearrange("p (h s) -> p h s", h=NH)
        xhat = arena_a[:, 0:T * D].rearrange("p (t d) -> p t d", t=T)
        hidden = arena_a[:, :].rearrange("p (f s) -> p f s", f=FF // P)
        probs = arena_r[:, :].rearrange("p (n s) -> p n s", n=8)
        part_rest = arena_r[:, 0:C * S].rearrange("p (c s) -> p c s", c=C)
        q_parts = arena_r[:, 2048:5120].bitcast(BF16).rearrange("p (i c s) -> p i c s", i=3, c=C)
        shuffled = arena_r[:, 6144:8192].rearrange("p (c s) -> p c s", c=C)
        w_gated = arena_r[:, 5120:7168].rearrange("p (c d) -> p c d", d=D)

        ps = ctx.enter_context(nc.psum_tensor("ps", [P, 8, HALF], F32))

        signals = []

        def signal(name):
            s = Signal(ctx.enter_context(nc.semaphore(name)))
            signals.append(s)
            return s

        loads = signal("loads")
        stored = signal("stored")
        stacked = signal("stacked")
        pe_done = signal("pe_done")
        act_done = signal("act_done")
        dve_done = signal("dve_done")
        pool_done = signal("pool_done")
        stats_ready = signal("stats_ready")
        var_ready = signal("var_ready")
        rstd_ready = signal("rstd_ready")
        xhat_ready = signal("xhat_ready")
        xT_transposed = signal("xT_transposed")
        xT_act = signal("xT_act")
        xT_dve = signal("xT_dve")
        product = signal("product")
        moved = signal("moved")
        high_ready = signal("high_ready")
        rest_ready = signal("rest_ready")
        middle_ready = signal("middle_ready")
        low_ready = signal("low_ready")
        rope_step = signal("rope_step")
        scores_ready = signal("scores_ready")
        max_taken = signal("max_taken")
        max_turned = signal("max_turned")
        max_high = signal("max_high")
        max_rest1 = signal("max_rest1")
        max_middle = signal("max_middle")
        max_low = signal("max_low")
        keyed_ready = signal("keyed_ready")
        exp_done = signal("exp_done")
        pv_done = signal("pv_done")
        recip_done = signal("recip_done")
        normed = signal("normed")
        v_padded = signal("v_padded")

        def clear_signals():
            for s in signals:
                nc.sync.sem_clear(s.sem)
                s.at = 0
            nc.all_engine_barrier()


        def vcol(name, i=0):
            at = VEC_ROWS[name][0] + i
            return vec[:, at:at + 1]

        def pad_v(dve, of):
            src = of.rearrange("p (g two d) -> p g two d", two=2, d=HD)
            dst = v_pad[:].rearrange("p (g two) (z d) -> p g two z d", two=2, z=2)
            nc.vector.tensor_copy(dst[:, :, 0, 0, :], src[:, :, 0, :])
            return nc.vector.tensor_copy(dst[:, :, 1, 1, :], src[:, :, 1, :])

        def norm_stage(x_tiles, n_tiles, norm_scale, norm_shift, dst, n_groups, group_cols):
            per_group = n_tiles // n_groups
            st0, va0, rs0 = stats_ready.reserve(2), var_ready.reserve(1), rstd_ready.reserve(1)
            xh0, xt0 = xhat_ready.reserve(n_tiles), xT_transposed.reserve(2 * n_groups)
            xa0, xd0 = xT_act.reserve(n_groups), xT_dve.reserve(n_groups)
            with nc.Block() as block:
                @block.vector
                def _(dve):
                    for t in range(n_tiles):
                        last = nc.vector.bn_stats(stats[:, t, :], x_tiles(t))
                    last.then_inc(stats_ready.sem, 1)
                    dve.wait_ge(stats_ready.sem, st0 + 1)
                    for t in range(n_tiles):
                        last = nc.vector.bn_aggr(mean_var[:, t, :], stats[:, t, :])
                    last.then_inc(stats_ready.sem, 1)
                    dve.wait_ge(stats_ready.sem, st0 + 2)
                    nc.vector.tensor_scalar(var_eps[:, 0:n_tiles], mean_var[:, 0:n_tiles, 1], EPS, None,
                                            ALU.add).then_inc(var_ready.sem, 1)
                    dve.wait_ge(rstd_ready.sem, rs0 + 1)
                    for t in range(n_tiles):
                        nc.vector.tensor_scalar(xhat[:, t, :], x_tiles(t), mean_var[:, t, 0:1],
                                                rstd[:, t:t + 1], ALU.subtract, ALU.mult)\
                            .then_inc(xhat_ready.sem, 1)
                    for g in range(n_groups):
                        dve.wait_ge(xT_transposed.sem, xt0 + 2 * g + 2)
                        nc.vector.tensor_scalar(dst[:, 1, g * group_cols:(g + 1) * group_cols],
                                                ps[:, 2 * g + 1, 0:group_cols], norm_scale(1, g),
                                                norm_shift(1, g), ALU.mult, ALU.add)\
                            .then_inc(xT_dve.sem, 1)

                @block.gpsimd
                def _(pool):
                    pool.wait_ge(var_ready.sem, va0 + 1)
                    nc.gpsimd.tensor_tensor(rstd[:, 0:n_tiles], var_eps[:, 0:n_tiles],
                                            minus_half[:, 0:n_tiles], ALU.pow).then_inc(rstd_ready.sem, 1)

                @block.tensor
                def _(pe):
                    for g in range(n_groups):
                        for c in range(C):
                            for t in range(per_group):
                                if c == 0:
                                    pe.wait_ge(xhat_ready.sem, xh0 + g * per_group + t + 1)
                                last = nc.tensor.transpose(ps[:, 2 * g + c, t * P:(t + 1) * P],
                                                           xhat[:, g * per_group + t, c * P:(c + 1) * P],
                                                           ident)
                            last.then_inc(xT_transposed.sem, 1)

                @block.scalar
                def _(act):
                    for g in range(n_groups):
                        act.wait_ge(xT_transposed.sem, xt0 + 2 * g + 1)
                        nc.scalar.activation(dst[:, 0, g * group_cols:(g + 1) * group_cols],
                                             ps[:, 2 * g, 0:group_cols], ACT.Identity,
                                             bias=norm_shift(0, g), scale=norm_scale(0, g))\
                            .then_inc(xT_act.sem, 1)

        def stack_dmas(sp, stack, parts, slot, part):
            for g in range(C):
                sp.dma_start(stack[slot * HD:(slot + 1) * HD, g * HPC:(g + 1) * HPC, :], parts(part, g))\
                    .then_inc(stacked.sem, 16)

        def attention_max(q_cols_keys, running, mask_tile):
            keys, k_of = q_cols_keys
            n = T * 2
            sc0, mt0 = scores_ready.reserve(n), max_taken.reserve(n + (1 if running else 0))
            view = ps[:].rearrange("p (u b) (h k) -> p u (b h) k", u=4, h=4)
            dst = tile_max if running else neg_max[:]
            with nc.Block() as block:
                @block.tensor
                def _(pe):
                    for u in range(n):
                        t, hh = u // 2, u % 2
                        if u >= 4:
                            pe.wait_ge(max_taken.sem, mt0 + u - 3)
                        for i in range(8):
                            h = hh * 8 + i
                            o = view[:, u % 4, i, 0:keys]
                            if mask_tile is not None:
                                nc.tensor.matmul(o, mask_tile(slice(t * P, (t + 1) * P)), ident_bf[:],
                                                 start=True, stop=False)
                            last = nc.tensor.matmul(o, q_stack[0:BIAS_ROW + 1, h, t * P:(t + 1) * P],
                                                    k_of(h, BIAS_ROW + 1), start=mask_tile is None,
                                                    stop=True)
                        last.then_inc(scores_ready.sem, 1)

                @block.vector
                def _(dve):
                    for u in range(n):
                        dve.wait_ge(scores_ready.sem, sc0 + u + 1)
                        nc.vector.tensor_reduce(dst.rearrange("p (h t) -> p h t", t=T)[:, u % 2 * 8:u % 2 * 8 + 8, u // 2],
                                                view[:, u % 4, :, 0:keys], AX_X,
                                                ALU.max, negate=True).then_inc(max_taken.sem, 1)
                    if running:
                        dve.wait_ge(max_taken.sem, mt0 + n)
                        nc.vector.tensor_tensor(neg_max[:], neg_max[:], tile_max, ALU.min)\
                            .then_inc(max_taken.sem, 1)

        def max_to_stack():
            tu0, hi0 = max_turned.reserve(1), max_high.reserve(1)
            re0, mi0, lo0, sk0 = max_rest1.reserve(1), max_middle.reserve(1), max_low.reserve(1), stacked.reserve(48)
            with nc.Block() as block:
                @block.tensor
                def _(pe):
                    nc.tensor.transpose(ps[:, 0, 0:P], neg_max[:], ident).then_inc(max_turned.sem, 1)

                @block.scalar
                def _(act):
                    act.wait_ge(max_turned.sem, tu0 + 1)
                    nc.scalar.activation(max_parts[:, 0, :], ps[:, 0, 0:P], ACT.Copy).then_inc(max_high.sem, 1)
                    act.wait_ge(max_rest1.sem, re0 + 1)
                    nc.scalar.activation(max_parts[:, 1, :], max_rest, ACT.Copy).then_inc(max_middle.sem, 1)

                @block.vector
                def _(dve):
                    dve.wait_ge(max_high.sem, hi0 + 1)
                    nc.vector.tensor_tensor(max_rest, ps[:, 0, 0:P], max_parts[:, 0, :], ALU.subtract)\
                        .then_inc(max_rest1.sem, 1)
                    dve.wait_ge(max_middle.sem, mi0 + 1)
                    nc.vector.tensor_tensor(max_parts[:, 2, :], max_rest, max_parts[:, 1, :],
                                            ALU.subtract).then_inc(max_low.sem, 1)

                @block.sync
                def _(sp):
                    for i, ready in enumerate(((max_high.sem, hi0 + 1), (max_middle.sem, mi0 + 1),
                                               (max_low.sem, lo0 + 1))):
                        sp.wait_ge(*ready)
                        row = q_stack[MAX_ROWS + i:MAX_ROWS + i + 1]
                        sp.dma_start(row.rearrange("o h (t q) -> o (h t) q", q=P), max_parts[:, i, :])\
                            .then_inc(stacked.sem, 16)
                    sp.wait_ge(stacked.sem, sk0 + 48)

        def attention_sum(k_of, mask_tile, add_to):
            ke0, ex0, pv0 = keyed_ready.reserve(NH), exp_done.reserve(NH), pv_done.reserve(4)
            rd0, no0 = recip_done.reserve(2), normed.reserve(2)
            with nc.Block() as block:
                @block.tensor
                def _(pe):
                    def products(quad):
                        g, sub = quad // 2, quad % 2
                        pe.wait_ge(exp_done.sem, ex0 + 4 * quad + 4)
                        if g == 1 and sub == 0:
                            pe.wait_ge(normed.sem, no0 + 1)
                        for what in range(2):
                            for half in range(2):
                                for j in range(4):
                                    n = 4 * quad + j
                                    h = 8 * g + 2 * j + sub
                                    w = v_pad[:, h, :] if what == 0 else ones_pad[:, sub, :]
                                    last = nc.tensor.matmul(
                                        ps[32 * j:32 * j + 32, 4 + 2 * what + half, :], w,
                                        probs[:, n % 8, half * HALF:(half + 1) * HALF],
                                        start=(sub == 0), stop=(sub == 1), skip_group_check=True)
                        last.then_inc(pv_done.sem, 1)

                    for n in range(NH):
                        quad, j = n // 4, n % 4
                        h = 8 * (quad // 2) + 2 * j + quad % 2
                        if n >= 2:
                            pe.wait_ge(exp_done.sem, ex0 + n - 1)
                        for half in range(2):
                            o = ps[:, 2 * (n % 2) + half, :]
                            cols = slice(half * HALF, (half + 1) * HALF)
                            if mask_tile is not None:
                                nc.tensor.matmul(o, ident_bf[:], mask_tile(cols),
                                                 start=True, stop=False)
                            last = nc.tensor.matmul(o, k_of(h, STACK), q_stack[0:STACK, h, cols],
                                                    start=mask_tile is None, stop=True)
                        last.then_inc(keyed_ready.sem, 1)
                        if j == 3 and quad >= 1:
                            products(quad - 1)
                    products(3)

                @block.scalar
                def _(act):
                    for n in range(NH):
                        act.wait_ge(keyed_ready.sem, ke0 + n + 1)
                        if n >= 8:
                            act.wait_ge(pv_done.sem, pv0 + n // 4 - 1)
                        nc.scalar.activation(
                            probs[:, n % 8, :],
                            ps[:, 2 * (n % 2):2 * (n % 2) + 2, :].rearrange("p a b -> p (a b)"),
                            ACT.Exp, scale=SCALE).then_inc(exp_done.sem, 1)

                @block.vector
                def _(dve):
                    for g in range(2):
                        dve.wait_ge(pv_done.sem, pv0 + 2 * g + 2)
                        o = ps[:, 4:6, :].rearrange("p a b -> p (a b)")
                        total = ps[:, 6:8, :].rearrange("p a b -> p (a b)")
                        if add_to:
                            nc.vector.tensor_tensor(sums[:, g, :], sums[:, g, :], total, ALU.add)\
                                .then_inc(recip_done.sem, 1)
                            nc.vector.tensor_tensor(xT[:, g, :], xT[:, g, :], o, ALU.add)\
                                .then_inc(normed.sem, 1)
                        else:
                            nc.vector.reciprocal(sums[:, g, :], total).then_inc(recip_done.sem, 1)
                            dve.wait_ge(recip_done.sem, rd0 + g + 1)
                            nc.vector.tensor_tensor(xT[:, g, :], o, sums[:, g, :], ALU.mult)\
                                .then_inc(normed.sem, 1)

        def query_stage(w, bias, rope):
            pr0, mo0 = product.reserve(4), moved.reserve(0 if rope else 4)
            hi0, re0, mi0, lo0 = (s.reserve(4) for s in (high_ready, rest_ready, middle_ready, low_ready))
            sk0 = stacked.reserve(16 * (1 + N_SLOT * C))
            ro0 = rope_step.reserve(8 if rope else 0)
            with nc.Block() as block:
                @block.tensor
                def _(pe):
                    for u in range(4):
                        m, half = u // 2, u % 2
                        for c in range(C):
                            last = nc.tensor.matmul(ps[:, u, :], w[:, c, m * P:(m + 1) * P],
                                                    xT[:, c, half * HALF:(half + 1) * HALF],
                                                    start=(c == 0), stop=(c == C - 1))
                        last.then_inc(product.sem, 1)

                @block.scalar
                def _(act):
                    for u in range(4):
                        m, cols = u // 2, slice(u % 2 * HALF, (u % 2 + 1) * HALF)
                        if not rope:
                            act.wait_ge(product.sem, pr0 + u + 1)
                            nc.scalar.activation(part_rest[:, m, cols], ps[:, u, :], ACT.Identity,
                                                 bias=bias(m)).then_inc(moved.sem, 1)
                            act.wait_ge(moved.sem, mo0 + u + 1)
                        else:
                            act.wait_ge(rope_step.sem, ro0 + 2 * u + 2)
                        nc.scalar.activation(q_parts[:, 0, m, cols], part_rest[:, m, cols], ACT.Copy)\
                            .then_inc(high_ready.sem, 1)
                    for u in range(4):
                        m, cols = u // 2, slice(u % 2 * HALF, (u % 2 + 1) * HALF)
                        act.wait_ge(rest_ready.sem, re0 + u + 1)
                        nc.scalar.activation(q_parts[:, 1, m, cols], part_rest[:, m, cols], ACT.Copy)\
                            .then_inc(middle_ready.sem, 1)

                @block.vector
                def _(dve):
                    for u in range(4):
                        m, cols = u // 2, slice(u % 2 * HALF, (u % 2 + 1) * HALF)
                        if rope:
                            dve.wait_ge(product.sem, pr0 + u + 1)
                            rope_unit(dve, ps[:, u, :], part_rest[:, m, cols], shuffled[:, m, cols],
                                      rope_q[:, 0, cols], rope_q[:, 1, cols], ro0 + 2 * u)
                    for u in range(4):
                        m, cols = u // 2, slice(u % 2 * HALF, (u % 2 + 1) * HALF)
                        dve.wait_ge(high_ready.sem, hi0 + u + 1)
                        nc.vector.tensor_tensor(part_rest[:, m, cols], part_rest[:, m, cols],
                                                q_parts[:, 0, m, cols], ALU.subtract)\
                            .then_inc(rest_ready.sem, 1)
                    for u in range(4):
                        m, cols = u // 2, slice(u % 2 * HALF, (u % 2 + 1) * HALF)
                        dve.wait_ge(middle_ready.sem, mi0 + u + 1)
                        dve.wait_ge(rest_ready.sem, re0 + u + 1)
                        nc.vector.tensor_tensor(q_parts[:, 2, m, cols], part_rest[:, m, cols],
                                                q_parts[:, 1, m, cols], ALU.subtract)\
                            .then_inc(low_ready.sem, 1)

                @block.sync
                def _(sp):
                    sp.dma_start(q_stack[BIAS_ROW:BIAS_ROW + 1], ones_row[:])\
                        .then_inc(stacked.sem, 16)
                    sp.wait_ge(high_ready.sem, hi0 + 4)
                    for part, ready in ((0, None), (1, (middle_ready.sem, mi0 + 4)), (2, (low_ready.sem, lo0 + 4))):
                        if ready:
                            sp.wait_ge(*ready)
                        for s in range(N_SLOT):
                            if Q_SLOTS[s] != part:
                                continue
                            stack_dmas(sp, q_stack, lambda i, g: q_parts[:, i, g, :], s, part)
                    sp.wait_ge(stacked.sem, sk0 + 16 * (1 + N_SLOT * C))

        def rope_unit(dve, of, dst, turned, cos, sin, start):
            lower, upper = slice(0, P // 2), slice(P // 2, P)
            nc.vector.tensor_tensor(dst, of, cos, ALU.mult)
            nc.vector.tensor_tensor(turned[lower], of[upper], sin[upper], ALU.mult)
            nc.vector.tensor_tensor(turned[upper], of[lower], sin[lower], ALU.mult).then_inc(rope_step.sem, 1)
            dve.wait_ge(rope_step.sem, start + 1)
            nc.vector.tensor_tensor(dst, dst, turned, ALU.add).then_inc(rope_step.sem, 1)

        def project_back(act_in, w, gate, n_chunks, bias_row):
            gated = gate is not None
            wide = gate == "mlp"
            spreads = (2 if wide else 1) if gated else 0
            ac0, dv0, rows0 = act_done.reserve(C * spreads), dve_done.reserve(spreads), pe_done.reserve(spreads)
            mo0, pr0 = moved.reserve(T + (bias_row is not None)), product.reserve(T)
            with nc.Block() as block:
                @block.vector
                def _(dve):
                    if gated:
                        dve.wait_ge(pe_done.sem, rows0 + 1)
                        for c in range(n_chunks):
                            last = nc.vector.tensor_tensor(w_gated[:, c, :], w[:, c, :], ps[:, 0, 0:D], ALU.mult)
                        last.then_inc(dve_done.sem, 1)
                        if wide:
                            dve.wait_ge(pe_done.sem, rows0 + 2)
                            nc.vector.tensor_copy(gb2_row[:], ps[:, 1, 0:D]).then_inc(dve_done.sem, 1)
                            dve.wait_ge(dve_done.sem, dv0 + 2)
                    if bias_row is not None:
                        for t in range(T):
                            last = nc.vector.tensor_tensor(x[:, t, :], x[:, t, :], bias_row[:], ALU.add)
                        last.then_inc(moved.sem, 1)
                        dve.wait_ge(moved.sem, mo0 + 1)
                    m0 = mo0 + (1 if bias_row is not None else 0)
                    for t in range(T):
                        dve.wait_ge(product.sem, pr0 + t + 1)
                        nc.vector.tensor_tensor(x[:, t, :], x[:, t, :], ps[:, 2 + t % 4, 0:D], ALU.add)\
                            .then_inc(moved.sem, 1)

                @block.scalar
                def _(act):
                    if gated:
                        gi = dict(msa=0, x=1, mlp=2)[gate]
                        k = 0
                        for which in ([gi, 3] if wide else [gi]):
                            for c in range(C):
                                if k >= 2:
                                    act.wait_ge(pe_done.sem, rows0 + 1)
                                nc.scalar.activation(spread[:, c, :], gates_b[:, which, c:c + 1].to_broadcast([P, P]),
                                                     ACT.Copy).then_inc(act_done.sem, 1)
                                k += 1

                @block.tensor
                def _(pe):
                    if gated:
                        for k in range(2 if wide else 1):
                            for c in range(C):
                                pe.wait_ge(act_done.sem, ac0 + 2 * k + c + 1)
                                last = nc.tensor.matmul(ps[:, k, c * P:(c + 1) * P], spread[:, c, :], ident,
                                                        start=True, stop=True)
                            last.then_inc(pe_done.sem, 1)
                        pe.wait_ge(dve_done.sem, dv0 + 1)
                    weights = w_gated if gated else w
                    m0 = mo0 + (1 if bias_row is not None else 0)
                    for t in range(T):
                        if t >= 4:
                            pe.wait_ge(moved.sem, m0 + t - 3)
                        for c in range(n_chunks):
                            last = nc.tensor.matmul(ps[:, 2 + t % 4, 0:D], act_in[:, c, t * P:(t + 1) * P],
                                                    weights[:, c, :], start=(c == 0), stop=(c == n_chunks - 1))
                        last.then_inc(product.sem, 1)

        ada_w = arena_a[:, 0:C * 18 * P].rearrange("p (c n) -> p c n", c=C)
        ss_q = arena_a[:, 4608:5632].rearrange("p (c n) -> p c n", c=C)
        ss_kv = arena_a[:, 5632:6656].rearrange("p (c n) -> p c n", c=C)
        w_kv = arena_r[:, 0:1024].rearrange("p (c n) -> p c n", c=C)
        w_ck = arena_r[:, 1024:1536].rearrange("p (c n) -> p c n", c=C)
        w_cv = arena_r[:, 1536:2048].rearrange("p (c n) -> p c n", c=C)
        cT_norm = arena_r[:, 2048:3072].rearrange("p (c n) -> p c n", c=C)
        cT_raw = arena_r[:, 3072:4096].rearrange("p (c n) -> p c n", c=C)
        kc = arena_r[:, 4096:6144].rearrange("p (c b l k) -> p c b l k", c=C, b=B, l=2)
        kc_flat = arena_r[:, 4096:6144].rearrange("p (c n) -> p c n", c=C)
        kc_parts = k_parts
        mask_raw = arena_r[:, 6144:8192].bitcast(U8).rearrange("p (t k) -> p t k", t=T)
        ctx_tok = x[:, 0:B, :]
        vec_rows = sums[0:N_VEC, 0, 0:P]
        cond = sums[0:B, 0, 128:128 + D]
        ctx_mask = sums[:, 1, 0:B * LC // 4].bitcast(U8).rearrange("p (b k) -> p b k", b=B)
        condT = sums[:, 0, 512:512 + C * B].rearrange("p (c b) -> p c b", c=C)
        siluT = sums[:, 0, 544:544 + C * B].rearrange("p (c b) -> p c b", c=C)
        expT = sums[:, 0, 576:576 + C * B].rearrange("p (c b) -> p c b", c=C)
        mod = sums[:, 0, 640:640 + N_MOD * B].rearrange("p (j b) -> p j b", j=N_MOD)
        bv_row = sums[:, 0, 768:768 + D]
        any_ctx = sums[:, 1, 128:128 + B]
        key_bias = sums[:, 1, 256:768].bitcast(BF16).rearrange("p (b l k) -> p b l k", b=B, l=2)
        any_q = sums[:, 1, 800:800 + T]
        none_q = sums[:, 1, 816:816 + T]
        keep = sums[:, 1, 832:832 + T]
        seen = sums[:, 1, 848:848 + T * T].rearrange("p (t k) -> p t k", t=T)
        list_tmp = sums[:, 1, 920:920 + 24]
        bias_nat = xT[:].rearrange("p c s -> p (c s)").bitcast(BF16).rearrange("p (t k) -> p t k", t=4)

        with nc.Block() as block:
            @block.sync
            def _(sp):
                def load(dst, src):
                    sp.dma_start(dst[:], src).then_inc(loads.sem, 16)
                    loads.at += 16
                load(const[:], a["shape_consts"])
                for name, (at, n) in VEC_ROWS.items():
                    load(vec_rows[at:at + n, :], a[name].rearrange("(j p) -> j p", p=P))
                load(cond, a["cond"])
                load(ctx_mask, a["ctx_mask"].rearrange("(o b) k -> o b k", o=1).to_broadcast([P, B, LC]))
                for dst, name in ((ss_q, "Wss_q"), (ss_kv, "Wss_kv"), (ada_w, "adaLN_W"), (w_kv, "Wkv"),
                                  (w_ck, "ck_W"), (w_cv, "cv_W")):
                    load(dst, a[name].rearrange("(c p) n -> p c n", p=P))
                sp.wait_ge(pool_done.sem, 1)
                load(ctx_tok[0:LC], a["ctx"].rearrange("b k d -> k b d"))
                load(mask_raw, a["mask"].rearrange("(t p) k -> p t k", p=P))
                for dst, name in ((w_q, "Wq"), (w_p, "Wp"), (w_qkv, "qkv_W"), (w_out, "attn_out_W"), (w_cq, "cq_W"),
                                  (w_co, "co_W"), (w_1, "mlp_W1"), (w_2, "mlp_W2")):
                    load(dst, a[name].rearrange("(c p) n -> p c n", p=P))
                sp.wait_ge(loads.sem, loads.at)

            @block.gpsimd
            def _(pool):
                nc.gpsimd.memset(ctx_tok[:], 0.0).then_inc(pool_done.sem, 1)
                nc.gpsimd.memset(minus_half[:], -0.5)
                nc.gpsimd.memset(ones_row[:], 1.0)
                nc.gpsimd.memset(v_pad[:], 0.0)
                nc.gpsimd.memset(ones_pad[:], 0.0).then_inc(pool_done.sem, 1)
                pool.wait_ge(pool_done.sem, 2)
                nc.gpsimd.memset(ones_pad[:, 0, 0:HD], 1.0)
                nc.gpsimd.memset(ones_pad[:, 1, HD:2 * HD], 1.0)
                pool_done.at = 2

            @block.vector
            def _(dve):
                nc.vector.memset(k_ctx[BIAS_ROW:P], 1.0)
                nc.vector.memset(key_bias[0:1], MASKED)
                nc.vector.memset(k_self[BIAS_ROW:P], 1.0).then_inc(dve_done.sem, 1)
                dve.wait_ge(dve_done.sem, 1)
                nc.vector.memset(key_bias[0:1, :, 0, 0:LC], 0.0)
                nc.vector.memset(k_self[BIAS_ROW:BIAS_ROW + 1], 0.0)

        with nc.Block() as block:
            @block.tensor
            def _(pe):
                nc.tensor.transpose(ps[:, 0, 0:N_VEC], vec_rows, ident[0:N_VEC, 0:N_VEC])
                for c in range(C):
                    last = nc.tensor.transpose(ps[:, 1, c * B:(c + 1) * B], cond[:, c * P:(c + 1) * P],
                                               ident[0:B, 0:B])
                last.then_inc(pe_done.sem, 1)

            @block.scalar
            def _(act):
                act.wait_ge(dve_done.sem, 2)
                nc.scalar.activation(expT, condT, ACT.Exp, scale=-1.0).then_inc(act_done.sem, 1)

            @block.vector
            def _(dve):
                nc.vector.tensor_copy(ident_bf[:], ident)
                dve.wait_ge(pe_done.sem, 1)
                nc.vector.tensor_copy(vec[:], ps[:, 0, 0:N_VEC])
                nc.vector.tensor_copy(condT, ps[:, 1, 0:C * B].rearrange("p (c b) -> p c b", c=C))\
                    .then_inc(dve_done.sem, 1)
                dve.wait_ge(act_done.sem, 1)
                nc.vector.tensor_scalar(expT, expT, 1.0, None, ALU.add).then_inc(dve_done.sem, 1)
                dve.wait_ge(dve_done.sem, 3)
                nc.vector.reciprocal(siluT, expT).then_inc(dve_done.sem, 1)
                dve.wait_ge(dve_done.sem, 4)
                nc.vector.tensor_tensor(siluT, siluT, condT, ALU.mult)
                nc.vector.tensor_reduce(any_ctx, ctx_mask, AX_X, ALU.max).then_inc(dve_done.sem, 1)
                dve.wait_ge(dve_done.sem, 5)
                nc.vector.tensor_scalar(list_tmp[0:1, 0:B], any_ctx[0:1, :], -MASKED, None, ALU.mult)\
                    .then_inc(dve_done.sem, 1)
                dve.wait_ge(dve_done.sem, 6)
                for b in range(B):
                    last = nc.vector.tensor_scalar(key_bias[0:1, b, 1, 0:LC], ctx_mask[0:1, b, :], 1.0,
                                                   list_tmp[0:1, b:b + 1], ALU.subtract, ALU.mult)
                last.then_inc(dve_done.sem, 1)
                dve_done.at = 7
            act_done.at = pe_done.at = 1

        with nc.Block() as block:
            @block.tensor
            def _(pe):
                for j in range(N_MOD):
                    w, at, c_in = (ss_q, j, siluT) if j < 4 else (ss_kv, j - 4, siluT) if j < 8 else (ada_w, j - 8, condT)
                    for c in range(C):
                        last = nc.tensor.matmul(ps[:, 0, j * B:(j + 1) * B], w[:, c, at * P:(at + 1) * P],
                                                c_in[:, c, :], start=(c == 0), stop=(c == C - 1))
                last.then_inc(pe_done.sem, 1)
                for c in range(C):
                    for k, name in enumerate(("bp", "bkv")):
                        pe.wait_ge(act_done.sem, 1 + 2 * c + k + 1)
                        last = nc.tensor.matmul(ps[:, 1 + k, c * P:(c + 1) * P], spread[:, k, :], ident,
                                                start=True, stop=True)
                    last.then_inc(pe_done.sem, 1)

            @block.scalar
            def _(act):
                for c in range(C):
                    if c:
                        act.wait_ge(pe_done.sem, 3)
                    for k, col in enumerate((vcol("bp", c), vcol("bkv", 2 + c))):
                        nc.scalar.activation(spread[:, k, :], col.to_broadcast([P, P]), ACT.Copy)\
                            .then_inc(act_done.sem, 1)

            @block.vector
            def _(dve):
                dve.wait_ge(pe_done.sem, 2)
                for b in range(B):
                    last = nc.vector.tensor_tensor(mod[:, :, b],
                                                   ps[:, 0, 0:N_MOD * B].rearrange("p (j b) -> p j b", j=N_MOD)[:, :, b],
                                                   vec[:, 0:N_MOD], ALU.add)
                last.then_inc(dve_done.sem, 1)
                dve.wait_ge(dve_done.sem, 8)
                for i, (norm, (sc, sh)) in enumerate(NORMS.items()):
                    for c in range(C):
                        nc.vector.tensor_scalar(affine[:, :, i, 0, c], mod[:, sc + c, :], 1.0, None, ALU.add)
                        last = nc.vector.tensor_copy(affine[:, :, i, 1, c], mod[:, sh + c, :])
                for c in range(C):
                    for i, j in enumerate((GATES["msa"], GATES["x"], GATES["mlp"])):
                        nc.vector.tensor_copy(gates[:, :, i, c], mod[:, j + c, :])
                    last = nc.vector.tensor_scalar(gates[:, :, 3, c], mod[:, GATES["mlp"] + c, :], vcol("mlp_b2", c),
                                                   None, ALU.mult)
                last.then_inc(dve_done.sem, 1)
                dve.wait_ge(dve_done.sem, 9)
                for i, name in ((2, "norm1_w"), (3, "normc_w"), (4, "norm2_w")):
                    for c in range(C):
                        last = nc.vector.tensor_scalar(affine[:, :, i, 0, c], affine[:, :, i, 0, c], vcol(name, c),
                                                       None, ALU.mult)
                dve.wait_ge(pe_done.sem, 4)
                nc.vector.tensor_copy(bp_row[:], ps[:, 1, 0:D])
                nc.vector.tensor_copy(bv_row, ps[:, 2, 0:D]).then_inc(dve_done.sem, 1)
                dve_done.at = 10
            act_done.at, pe_done.at = 5, 4

        with nc.Block() as block:
            @block.tensor
            def _(pe):
                for c in range(C):
                    for b in range(B):
                        last = nc.tensor.transpose(ps[:, c, b * P:(b + 1) * P], ctx_tok[:, b, c * P:(c + 1) * P], ident)
                last.then_inc(pe_done.sem, 1)

            @block.vector
            def _(dve):
                dve.wait_ge(pe_done.sem, 5)
                for c in range(C):
                    last = nc.vector.tensor_copy(cT_raw[:, c, :], ps[:, c, :])
                last.then_inc(dve_done.sem, 1)
            dve_done.at, pe_done.at = 11, 5
        norm_stage(lambda t: ctx_tok[:, t, :], B, lambda c, g: affine[:, g, 1, 0, c:c + 1],
                   lambda c, g: affine[:, g, 1, 1, c:c + 1], cT_norm, B, P)

        with nc.Block() as block:
            @block.tensor
            def _(pe):
                for layer, (w, src) in enumerate(((w_kv, cT_norm), (w_ck, cT_raw))):
                    for m in range(C):
                        for c in range(C):
                            last = nc.tensor.matmul(ps[:, 2 * layer + m, :], w[:, c, m * P:(m + 1) * P],
                                                    src[:, c, :],
                                                    start=(c == 0), stop=(c == C - 1))
                last.then_inc(pe_done.sem, 1)
                for layer in range(2):
                    for b in range(B):
                        src, w = (cT_norm, w_kv[:, :, D:2 * D]) if layer == 0 else (cT_raw, w_cv)
                        for c in range(C):
                            last = nc.tensor.matmul(ps[:, 4 + b, layer * D:(layer + 1) * D],
                                                    src[:, c, b * P:(b + 1) * P], w[:, c, :],
                                                    start=(c == 0), stop=(c == C - 1))
                last.then_inc(pe_done.sem, 1)

            @block.vector
            def _(dve):
                dve.wait_ge(pe_done.sem, 6)
                for c in range(C):
                    for b in range(B):
                        nc.vector.tensor_scalar(kc[:, c, b, 0, :], ps[:, c, b * P:(b + 1) * P], vcol("bkv", c), None,
                                                ALU.add)
                        last = nc.vector.tensor_scalar(kc[:, c, b, 1, :], ps[:, 2 + c, b * P:(b + 1) * P],
                                                       any_ctx[:, b:b + 1], None, ALU.mult)
                last.then_inc(dve_done.sem, 1)
                dve.wait_ge(pe_done.sem, 7)
                for b in range(B):
                    nc.vector.tensor_tensor(v_ctx[:, b, 0, :], ps[:, 4 + b, 0:D], bv_row, ALU.add)
                    last = nc.vector.tensor_copy(v_ctx[:, b, 1, :], ps[:, 4 + b, D:2 * D])
                dve.wait_ge(dve_done.sem, 12)
                nc.vector.tensor_copy(kc_parts[:, 0], kc_flat).then_inc(dve_done.sem, 1)
                dve.wait_ge(dve_done.sem, 13)
                nc.vector.tensor_tensor(kc_flat, kc_flat, kc_parts[:, 0], ALU.subtract).then_inc(dve_done.sem, 1)
                dve.wait_ge(dve_done.sem, 14)
                nc.vector.tensor_copy(kc_parts[:, 1], kc_flat).then_inc(dve_done.sem, 1)
                dve.wait_ge(dve_done.sem, 15)
                nc.vector.tensor_tensor(kc_parts[:, 2], kc_flat, kc_parts[:, 1], ALU.subtract)\
                    .then_inc(dve_done.sem, 1)
                dve_done.at = 16

            @block.sync
            def _(sp):
                for h in range(NH):
                    sp.dma_start(k_ctx[BIAS_ROW:BIAS_ROW + 1, h, :], key_bias[0:1].rearrange("o b l k -> o (b l k)"))\
                        .then_inc(stacked.sem, 16)
                sp.wait_ge(dve_done.sem, 16)
                for s, part in enumerate(K_SLOTS):
                    stack_dmas(sp, k_ctx, lambda i, g: kc_parts[:, i, g, :], s, part)
                stacked.at = 16 * (N_SLOT * C + NH)
                sp.wait_ge(stacked.sem, stacked.at)
            pe_done.at = 7

        with nc.Block() as block:
            @block.vector
            def _(dve):
                nc.vector.tensor_reduce(any_q, mask_raw, AX_X, ALU.max).then_inc(dve_done.sem, 1)
                nc.vector.tensor_reduce(seen, mask_raw.rearrange("p t (j k) -> p t j k", k=P), AX_X, ALU.max)\
                    .then_inc(dve_done.sem, 1)
                dve.wait_ge(dve_done.sem, 18)
                nc.vector.tensor_reduce(keep, seen.rearrange("p t k -> p k t"), AX_X, ALU.max)
                nc.vector.tensor_scalar(none_q, any_q, -MASKED, None, ALU.mult)
                nc.vector.tensor_reduce(list_tmp[:, 0:1], any_q, AX_X, ALU.min).then_inc(dve_done.sem, 1)
                dve.wait_ge(dve_done.sem, 19)
                nc.vector.tensor_scalar(list_tmp[:, 0:1], list_tmp[:, 0:1], -1.0, 1.0, ALU.mult, ALU.add)\
                    .then_inc(dve_done.sem, 1)
                dve.wait_ge(dve_done.sem, 20)
                nc.vector.tensor_scalar(keep, keep, list_tmp[:, 0:1], None, ALU.max).then_inc(dve_done.sem, 1)
                dve.wait_ge(pe_done.sem, 8)
                nc.vector.tensor_reduce(list_tmp[0:T, 1:2], ps[0:T, 0, 0:P], AX_X, ALU.max)\
                    .then_inc(dve_done.sem, 1)
                dve.wait_ge(pe_done.sem, 9)
                nc.vector.tensor_copy(list_tmp[0:T, 2:3], ps[0:T, 1, 0:1]).then_inc(dve_done.sem, 1)
                dve.wait_ge(dve_done.sem, 23)
                nc.vector.tensor_scalar(list_tmp[0:T, 8:8 + T], constant("iota")[0:T, :], list_tmp[0:T, 2:3],
                                        list_tmp[0:T, 1:2], ALU.is_equal, ALU.mult).then_inc(dve_done.sem, 1)
                dve.wait_ge(pe_done.sem, 10)
                nc.vector.tensor_copy(tile_list[0:1, :], ps[0:1, 2, 0:1 + T]).then_inc(dve_done.sem, 1)

            @block.tensor
            def _(pe):
                pe.wait_ge(dve_done.sem, 21)
                nc.tensor.transpose(ps[0:T, 0, 0:P], keep, ident).then_inc(pe_done.sem, 1)
                pe.wait_ge(dve_done.sem, 22)
                nc.tensor.matmul(ps[0:T, 1, 0:1], constant("before")[0:T, :], list_tmp[0:T, 1:2], start=True, stop=True)\
                    .then_inc(pe_done.sem, 1)
                pe.wait_ge(dve_done.sem, 24)
                nc.tensor.matmul(ps[0:1, 2, 0:1], constant("iota")[0:T, 1:2], list_tmp[0:T, 1:2], start=True, stop=True)
                nc.tensor.matmul(ps[0:1, 2, 1:1 + T], constant("tile")[0:T, :], list_tmp[0:T, 8:8 + T], start=True,
                                 stop=True).then_inc(pe_done.sem, 1)
            dve_done.at, pe_done.at = 25, 10
        for q4 in range(2):
            with nc.Block() as block:
                d0, p0 = dve_done.reserve(3), pe_done.reserve(8)

                @block.vector
                def _(dve):
                    for t in range(4):
                        tt = 4 * q4 + t
                        last = nc.vector.tensor_scalar(bias_nat[:, t, :], mask_raw[:, tt, :], 1.0, none_q[:, tt:tt + 1],
                                                       ALU.subtract, ALU.mult)
                    last.then_inc(dve_done.sem, 1)
                    for j in range(T):
                        dve.wait_ge(pe_done.sem, p0 + j + 1)
                        last = nc.vector.tensor_copy(mask_bias[:, j, q4 * HALF:(q4 + 1) * HALF],
                                                     ps[:, j % 8, :].bitcast(BF16)[:, 0:HALF])

                @block.tensor
                def _(pe):
                    pe.wait_ge(dve_done.sem, d0 + 1)
                    for j in range(T):
                        for t in range(4):
                            last = nc.tensor.transpose(ps[:, j % 8, :].bitcast(BF16)[:, t * P:(t + 1) * P],
                                                       bias_nat[:, t, j * P:(j + 1) * P], ident_bf[:])
                        last.then_inc(pe_done.sem, 1)
                dve_done.at = d0 + 1
        with nc.Block() as block:
            d0, p0, a0 = dve_done.at, pe_done.at, act_done.at

            @block.scalar
            def _(act):
                for t in range(T):
                    if t >= 2:
                        act.wait_ge(pe_done.sem, p0 + t - 1)
                    nc.scalar.activation(spread[:, t % 2, :], any_q[:, t:t + 1].to_broadcast([P, P]), ACT.Copy)\
                        .then_inc(act_done.sem, 1)

            @block.tensor
            def _(pe):
                for t in range(T):
                    pe.wait_ge(act_done.sem, a0 + t + 1)
                    nc.tensor.matmul(ps[:, t // 4, (t % 4) * P:(t % 4 + 1) * P], spread[:, t % 2, :], ident, start=True,
                                     stop=True).then_inc(pe_done.sem, 1)

            @block.vector
            def _(dve):
                dve.wait_ge(pe_done.sem, p0 + T)
                for half in range(2):
                    for k, table in enumerate((cos_k, sin_k)):
                        nc.vector.tensor_tensor(rope_q[:, k, half * HALF:(half + 1) * HALF], ps[:, half, :], table,
                                                ALU.mult)
        clear_signals()
        n_tiles = nc.values_load(tile_list[0:1, 0:1], min_val=1, max_val=T)

        with nc.Fori(0, B) as b:
            with nc.Block() as block:
                @block.sync
                def _(sp):
                    sp.dma_start(x[:], a["x"][b].rearrange("(t p) d -> p t d", p=P)).then_inc(loads.sem, 16)
                    sp.wait_ge(loads.sem, 16)

                @block.vector
                def _(dve):
                    nc.vector.tensor_copy(affine_b[:].rearrange("p n k c -> p (n k c)"),
                                          affine[:, bass.ds(b, 1)].rearrange("p o n k c -> p (o n k c)"))
                    nc.vector.tensor_copy(gates_b[:].rearrange("p n c -> p (n c)"),
                                          gates[:, bass.ds(b, 1)].rearrange("p o n c -> p (o n c)"))
                    pad_v(dve, v_ctx[:, bass.ds(b, 1), 0, :].rearrange("p o d -> p (o d)"))

            def norm(i):
                norm_stage(lambda t: x[:, t, :], T, lambda c, g: affine_b[:, i, 0, c:c + 1],
                           lambda c, g: affine_b[:, i, 1, c:c + 1], xT, 2, HALF)

            def cross(layer):
                def k_of(h, rows, n):
                    return k_ctx[0:rows, h, bass.ds(b * (2 * P) + layer * P, n)]
                attention_max((LC, lambda h, rows: k_of(h, rows, LC)), False, None)
                max_to_stack()
                attention_sum(lambda h, rows: k_of(h, rows, P), None, False)

            norm(0)
            query_stage(w_q, lambda m: vcol("bq", m), False)
            cross(0)
            project_back(xT, w_p, None, C, bp_row)

            norm(2)
            with nc.Block() as block:
                pr0, ro0, hi0 = product.reserve(8), rope_step.reserve(8), high_ready.reserve(4)
                re0, mi0, mo0 = rest_ready.reserve(4), middle_ready.reserve(4), moved.reserve(4)
                lo0 = low_ready.reserve(4)

                @block.tensor
                def _(pe):
                    for u in range(4):
                        m, cols = u // 2, slice(u % 2 * HALF, (u % 2 + 1) * HALF)
                        for c in range(C):
                            last = nc.tensor.matmul(ps[:, u, :], w_qkv[:, c, D + m * P:D + (m + 1) * P],
                                                    xT[:, c, cols],
                                                    start=(c == 0), stop=(c == C - 1))
                        last.then_inc(product.sem, 1)
                    for u in range(4):
                        for t in (2 * u, 2 * u + 1):
                            for c in range(C):
                                last = nc.tensor.matmul(ps[:, 4 + u, (t % 2) * D:(t % 2 + 1) * D],
                                                        xT[:, c, t * P:(t + 1) * P], w_qkv[:, c, 2 * D:3 * D],
                                                        start=(c == 0), stop=(c == C - 1))
                        last.then_inc(product.sem, 1)

                @block.vector
                def _(dve):
                    for u in range(4):
                        m, cols = u // 2, slice(u % 2 * HALF, (u % 2 + 1) * HALF)
                        dve.wait_ge(product.sem, pr0 + u + 1)
                        rope_unit(dve, ps[:, u, :], part_rest[:, m, cols], shuffled[:, m, cols], cos_k, sin_k,
                                  ro0 + 2 * u)
                    for u in range(4):
                        m, cols = u // 2, slice(u % 2 * HALF, (u % 2 + 1) * HALF)
                        dve.wait_ge(high_ready.sem, hi0 + u + 1)
                        nc.vector.tensor_tensor(part_rest[:, m, cols], part_rest[:, m, cols], k_parts[:, 0, m, cols],
                                                ALU.subtract).then_inc(rest_ready.sem, 1)
                    for u in range(4):
                        m, cols = u // 2, slice(u % 2 * HALF, (u % 2 + 1) * HALF)
                        dve.wait_ge(middle_ready.sem, mi0 + u + 1)
                        nc.vector.tensor_tensor(k_parts[:, 2, m, cols], part_rest[:, m, cols], k_parts[:, 1, m, cols],
                                                ALU.subtract).then_inc(low_ready.sem, 1)

                @block.scalar
                def _(act):
                    for u in range(4):
                        m, cols = u // 2, slice(u % 2 * HALF, (u % 2 + 1) * HALF)
                        act.wait_ge(rope_step.sem, ro0 + 2 * u + 2)
                        nc.scalar.activation(k_parts[:, 0, m, cols], part_rest[:, m, cols], ACT.Copy)\
                            .then_inc(high_ready.sem, 1)
                    for u in range(4):
                        m, cols = u // 2, slice(u % 2 * HALF, (u % 2 + 1) * HALF)
                        act.wait_ge(rest_ready.sem, re0 + u + 1)
                        nc.scalar.activation(k_parts[:, 1, m, cols], part_rest[:, m, cols], ACT.Copy)\
                            .then_inc(middle_ready.sem, 1)
                    for u in range(4):
                        act.wait_ge(product.sem, pr0 + 5 + u)
                        nc.scalar.activation(v_self[:, 2 * u:2 * u + 2, :].rearrange("p t d -> p (t d)"), ps[:, 4 + u, :],
                                             ACT.Copy).then_inc(moved.sem, 1)
            query_stage(w_qkv, None, True)
            with nc.Block() as block:
                @block.vector
                def _(dve):
                    nc.vector.memset(neg_max[:], 3e38)
                    nc.vector.memset(sums[:], 0.0)
                    nc.vector.memset(xT[:], 0.0)
            clear_signals()

            def biases(j):
                return lambda cols: mask_bias[:, bass.ds(j, 1), cols].rearrange("p o q -> p (o q)")

            def stack_key_tile(j):
                with nc.Block() as block:
                    @block.sync
                    def _(sp):
                        for s, part in enumerate(K_SLOTS):
                            stack_dmas(sp, k_self, lambda i, g: k_parts[:, i, g, bass.ds(j * P, P)], s, part)
                        n = 16 * N_SLOT * C
                        sp.wait_ge(stacked.sem, stacked.reserve(n) + n)

                    @block.vector
                    def _(dve):
                        pad_v(dve, v_self[:, bass.ds(j, 1), :].rearrange("p o d -> p (o d)"))

            with nc.Fori(0, n_tiles) as i:
                j = nc.values_load(tile_list[0:1, bass.ds(i + 1, 1)], min_val=0, max_val=T - 1)
                stack_key_tile(j)
                attention_max((P, lambda h, rows: k_self[0:rows, h, :]), True, biases(j))
                clear_signals()
            max_to_stack()
            clear_signals()
            with nc.Fori(0, n_tiles) as i:
                j = nc.values_load(tile_list[0:1, bass.ds(i + 1, 1)], min_val=0, max_val=T - 1)
                stack_key_tile(j)
                attention_sum(lambda h, rows: k_self[0:rows, h, :], biases(j), True)
                clear_signals()
            with nc.Block() as block:
                @block.vector
                def _(dve):
                    nc.vector.reciprocal(sums[:], sums[:]).then_inc(recip_done.sem, 1)
                    dve.wait_ge(recip_done.sem, recip_done.reserve(1) + 1)
                    nc.vector.tensor_tensor(xT[:], xT[:], sums[:], ALU.mult)
                    pad_v(dve, v_ctx[:, bass.ds(b, 1), 1, :].rearrange("p o d -> p (o d)"))
            project_back(xT, w_out, "msa", C, None)

            norm(3)
            query_stage(w_cq, lambda m: 0.0, False)
            cross(1)
            project_back(xT, w_co, "x", C, None)

            norm(4)
            with nc.Block() as block:
                n = 2 * (FF // P)
                pr0, mo0 = product.reserve(n), moved.reserve(n)

                @block.tensor
                def _(pe):
                    for u in range(n):
                        f, cols = u // 2, slice(u % 2 * HALF, (u % 2 + 1) * HALF)
                        if u >= 4:
                            pe.wait_ge(moved.sem, mo0 + u - 3)
                        for c in range(C):
                            last = nc.tensor.matmul(ps[:, u % 4, :], w_1[:, c, f * P:(f + 1) * P], xT[:, c, cols],
                                                    start=(c == 0), stop=(c == C - 1))
                        last.then_inc(product.sem, 1)

                @block.scalar
                def _(act):
                    for u in range(n):
                        f, cols = u // 2, slice(u % 2 * HALF, (u % 2 + 1) * HALF)
                        act.wait_ge(product.sem, pr0 + u + 1)
                        nc.scalar.activation(hidden[:, f, cols], ps[:, u % 4, :], ACT.Gelu_apprx_tanh,
                                             bias=vcol("mlp_b1", f)).then_inc(moved.sem, 1)
            project_back(hidden, w_2, "mlp", FF // P, gb2_row)
            with nc.Block() as block:
                @block.sync
                def _(sp):
                    sp.dma_start(out[b].rearrange("(t p) d -> p t d", p=P), x[:]).then_inc(stored.sem, 16)
                    sp.wait_ge(stored.sem, 16)
            clear_signals()


_NAMES = {
    "x": "x", "ctx": "ctx_1024", "cond": "cond_1024", "ctx_mask": "mask_BxS2_bf1", "mask": "mask_SxS_bk0",
    "Wq": "L0_xcond_Wq", "bq": "L0_xcond_bq", "Wkv": "L0_xcond_Wkv", "bkv": "L0_xcond_bkv", "Wp": "L0_xcond_Wp",
    "bp": "L0_xcond_bp", "Wss_q": "L0_xcond_Wss_q", "bss_q": "L0_xcond_bss_q", "Wss_kv": "L0_xcond_Wss_kv",
    "bss_kv": "L0_xcond_bss_kv", "adaLN_W": "L1_xcond_adaLN_W", "adaLN_b": "L1_xcond_adaLN_b",
    "norm1_w": "L1_xcond_norm1_w", "qkv_W": "L1_xcond_qkv_W", "attn_out_W": "L1_xcond_attn_out_W",
    "normc_w": "L1_xcond_normc_w", "cq_W": "L1_xcond_cq_W", "ck_W": "L1_xcond_ck_W", "cv_W": "L1_xcond_cv_W",
    "co_W": "L1_xcond_co_W", "norm2_w": "L1_xcond_norm2_w", "mlp_W1": "L1_xcond_mlp_W1",
    "mlp_b1": "L1_xcond_mlp_b1", "mlp_W2": "L1_xcond_mlp_W2", "mlp_b2": "L1_xcond_mlp_b2",
}


def by_component(v):
    import numpy as np
    shape = v.shape
    return np.ascontiguousarray(v.reshape(-1, shape[-1] // P, HPC, HD).swapaxes(2, 3)).reshape(shape)


def shape_consts():
    import numpy as np
    t = np.zeros((P, CONST_N), np.float32)

    def put(name, v):
        at, n = CONST_COLS[name]
        t[:v.shape[0], at:at + n] = v
    put("ident", np.eye(P, dtype=np.float32))
    inv_freq = 1.0 / 10000.0 ** (np.arange(0, HD, 2, dtype=np.float32) / HD)
    angle = np.outer(np.arange(S // 2, dtype=np.float32), inv_freq).T
    feature = np.arange(P) // HPC
    put("cos", np.cos(angle)[feature % (HD // 2)].astype(np.float32))
    sign = np.where(feature < HD // 2, 1.0, -1.0)[:, None]
    put("sin", (sign * np.sin(angle)[feature % (HD // 2)]).astype(np.float32))
    i = np.arange(T)
    put("before", (i[:, None] < i[None, :]).astype(np.float32))
    put("iota", np.tile(i.astype(np.float32), (T, 1)))
    put("tile", i[:, None].astype(np.float32))
    return t


def kernel(**inputs):
    import numpy as np
    import concourse.bacc as bacc
    from concourse.bass_utils import run_bass_kernel_spmd

    nc = bacc.Bacc("TRN2", target_bir_lowering=False, num_devices=1, dynamic_dma_scratch_size=1024)
    arrays, aps = {}, {}
    given = {short: np.ascontiguousarray(inputs[name]) for short, name in _NAMES.items()}
    for short in ("Wq", "bq", "cq_W", "ck_W"):
        given[short] = by_component(given[short])
    for short, n in (("Wkv", D), ("bkv", D), ("qkv_W", 2 * D)):
        given[short] = np.concatenate([by_component(given[short][..., :n]), given[short][..., n:]], axis=-1)
    given["shape_consts"] = shape_consts()
    for short, v in given.items():
        arrays[f"in_{short}"] = v
        aps[short] = nc.dram_tensor(f"in_{short}", v.shape, mybir.dt.from_np(v.dtype), kind="ExternalInput").ap()
    out = nc.dram_tensor("out_0", (B, S, D), F32, kind="ExternalOutput").ap()
    build(nc, aps, out)
    r = run_bass_kernel_spmd(nc, [arrays], core_ids=[0])
    return r.results[0]["out_0"]
```

```python
from contextlib import ExitStack

import concourse.bass as bass
from concourse import mybir

F32 = mybir.dt.float32
BF16 = mybir.dt.bfloat16
U8 = mybir.dt.uint8
I32 = mybir.dt.int32
ALU = mybir.AluOpType
ACT = mybir.ActivationFunctionType
AX_X = mybir.AxisListType.X

P = 128
B, S, D = 4, 1024, 256
C = D // P
T = S // P
HALF = 512
NH, HD = 16, 16
LC = 77
HPC = P // HD
FF = 4 * D
EPS = 1e-5
SCALE = HD ** -0.5
MASKED = -1e30
N_SLOT = 6
Q_SLOTS = (0, 0, 1, 0, 2, 1)
K_SLOTS = (0, 1, 0, 2, 0, 1)
BIAS_ROW = N_SLOT * HD
MAX_ROWS = BIAS_ROW + 1
STACK = MAX_ROWS + 3

CONST_COLS = dict(ident=(0, P), cos=(P, S // 2), sin=(P + S // 2, S // 2),
                  before=(P + S, T), iota=(P + S + T, T), tile=(P + S + 2 * T, 1))
CONST_N = P + S + 2 * T + 1

VEC_ROWS = {}
_at = 0
for _name, _n in (("bss_q", 4), ("bss_kv", 4), ("adaLN_b", 18), ("bq", 2), ("bkv", 4), ("norm1_w", 2),
                  ("normc_w", 2), ("norm2_w", 2), ("mlp_b1", 8), ("bp", 2), ("mlp_b2", 2)):
    VEC_ROWS[_name] = (_at, _n)
    _at += _n
N_VEC = _at
N_MOD = 26
NORMS = dict(q0=(0, 2), kv0=(4, 6), n1=(10, 8), nc=(16, 14), n2=(22, 20))
GATES = dict(msa=12, x=18, mlp=24)


class Stage:

    def __init__(self, pe=None, act=None, dve=None, pool=None, sp=None, act_high=None, act_middle=None,
                 done=None, xhat_done=None, read=None, x_done=None, ready=None):
        self.pe, self.act, self.dve, self.pool, self.sp = pe, act, dve, pool, sp
        self.act_high, self.act_middle = act_high, act_middle
        self.done, self.xhat_done, self.read, self.x_done, self.ready = done, xhat_done, read, x_done, ready


class Signal:

    def __init__(self, sem):
        self.sem, self.at = sem, 0

    def reserve(self, n):
        start = self.at
        self.at += n
        return start


def build(nc, a, out):
    ctx = ExitStack()
    with ctx:
        def sb(name, shape, dt=F32):
            return ctx.enter_context(nc.sbuf_tensor(name, shape, dt))

        const = sb("const", [P, CONST_N])

        def constant(name):
            at, n = CONST_COLS[name]
            return const[:, at:at + n]

        ident, cos_k, sin_k = constant("ident"), constant("cos"), constant("sin")
        ident_bf = sb("ident_bf", [P, P], BF16)
        rope_q = sb("rope_q", [P, 2, S])
        w_q = sb("w_q", [P, C, D])
        w_p = sb("w_p", [P, C, D])
        w_qkv = sb("w_qkv", [P, C, 3 * D])
        w_out = sb("w_out", [P, C, D])
        w_cq = sb("w_cq", [P, C, D])
        w_co = sb("w_co", [P, C, D])
        w_1 = sb("w_1", [P, C, FF])
        w_2 = sb("w_2", [P, FF // P, D])
        w_gated = sb("w_gated", [P, 2 * C + FF // P, D])
        vec = sb("vec", [P, N_VEC])
        affine = sb("affine", [P, B, 5, 2, C])
        gates = sb("gates", [P, B, 4, C])
        affine_b = sb("affine_b", [P, 5, 2, C])
        gates_b = sb("gates_b", [P, 4, C])
        bp_row = sb("bp_row", [P, D])
        gb2_row = sb("gb2_row", [P, D])
        spread = sb("spread", [P, 2, P])
        x = sb("x", [P, T, D])
        xT = sb("xT", [P, C, S])
        xhat = sb("xhat", [P, T, D])
        arena_a = sb("arena_a", [P, 8192])
        arena_r = sb("arena_r", [P, 10240])
        k_parts = sb("k_parts", [P, 3, C, S], BF16)
        v_self = sb("v_self", [P, T, D])
        v_ctx = sb("v_ctx", [P, B, 2, D])
        v_pad = sb("v_pad", [P, 2, NH, 2 * HD])
        ones_pad = sb("ones_pad", [P, 2, 2 * HD])
        k_ctx = sb("k_ctx", [P, NH, 2 * P], BF16)
        k_self = sb("k_self", [P, NH, P], BF16)
        mask_bias = sb("mask_bias", [P, T, S], BF16)
        ones_row = sb("ones_row", [NH, S], BF16)
        tile_list = sb("tile_list", [1, 1 + T], I32)
        stats = sb("stats", [P, T, 6])
        mean_var = sb("mean_var", [P, T, 2])
        var_eps = sb("var_eps", [P, T])
        rstd = sb("rstd", [P, T])
        minus_half = sb("minus_half", [P, T])
        neg_max = sb("neg_max", [P, 2, NH, T // 2])
        tile_max = sb("tile_max", [P, 2, NH, T // 2])
        max_rest = spread
        max_parts = sb("max_parts", [P, 2, 3, P], BF16)

        q_stack = arena_a[:, :].bitcast(BF16).rearrange("p (h s) -> p h s", h=NH)
        q_stack = arena_a[:, :].bitcast(BF16).rearrange("p (u h s) -> p u h s", u=2, h=NH)
        hidden = arena_a[:, :].rearrange("p (u f s) -> p u f s", u=2, f=FF // P)
        probs = arena_r[:, 0:4096].rearrange("p (n k s) -> p n k s", n=4, k=2)
        k_rest = arena_r[:, 0:C * S].rearrange("p (c s) -> p c s", c=C)
        q_rest = arena_r[:, 4096:6144].rearrange("p (c s) -> p c s", c=C)
        q_parts = arena_r[:, 6144:9216].bitcast(BF16).rearrange("p (i c s) -> p i c s", i=3, c=C)
        inverse = arena_r[:, 9216:10240].rearrange("p (g s) -> p g s", g=C)
        turned = inverse
        sums = xhat[:].rearrange("p t d -> p (t d)").rearrange("p (c s) -> p c s", c=C)
        k_ctx_dram = nc.dram_tensor("k_ctx_stacks", (STACK, NH, B * 2 * P), BF16, kind="Internal").ap()

        ps = ctx.enter_context(nc.psum_tensor("ps", [P, 8, HALF], F32))

        signals = []

        def signal(name):
            s = Signal(ctx.enter_context(nc.semaphore(name)))
            signals.append(s)
            return s

        loads = signal("loads")
        stored = signal("stored")
        k_stacked = signal("k_stacked")
        q_stacked = [signal("q_stacked_0"), signal("q_stacked_1")]
        pe_done = signal("pe_done")
        act_done = signal("act_done")
        dve_done = signal("dve_done")
        pool_done = signal("pool_done")
        stats_ready = signal("stats_ready")
        var_ready = signal("var_ready")
        rstd_ready = signal("rstd_ready")
        xhat_ready = signal("xhat_ready")
        xT_transposed = signal("xT_transposed")
        xT_ready = signal("xT_ready")
        xT_dve = signal("xT_dve")
        biased = signal("biased")
        x_ready = signal("x_ready")
        gate_spread = signal("gate_spread")
        gate_rows = signal("gate_rows")
        gated = signal("gated")
        product = signal("product")
        moved = signal("moved")
        high_ready = signal("high_ready")
        rest_ready = signal("rest_ready")
        middle_ready = signal("middle_ready")
        low_ready = signal("low_ready")
        rope_step = signal("rope_step")
        rope_added = signal("rope_added")
        scores_ready = signal("scores_ready")
        max_taken = signal("max_taken")
        max_turned = signal("max_turned")
        max_high = signal("max_high")
        max_rest1 = signal("max_rest1")
        max_middle = signal("max_middle")
        max_low = signal("max_low")
        keyed_ready = signal("keyed_ready")
        exp_done = signal("exp_done")
        pv_done = signal("pv_done")
        recip_done = signal("recip_done")
        normed = signal("normed")

        def clear_signals():
            for s in signals:
                nc.sync.sem_clear(s.sem)
                s.at = 0
            nc.all_engine_barrier()


        def vcol(name, i=0):
            at = VEC_ROWS[name][0] + i
            return vec[:, at:at + 1]

        def pad_v(engine, slot, of):
            src = of.rearrange("p (g two d) -> p g two d", two=2, d=HD)
            dst = v_pad[:, slot].rearrange("p (g two) (z d) -> p g two z d", two=2, z=2)
            engine.tensor_copy(dst[:, :, 0, 0, :], src[:, :, 0, :])
            return engine.tensor_copy(dst[:, :, 1, 1, :], src[:, :, 1, :])

        def context_norm(x_tiles, n_tiles, norm_scale, norm_shift, dst, n_groups, group_cols):
            per_group = n_tiles // n_groups
            st0, va0, rs0 = stats_ready.reserve(2), var_ready.reserve(1), rstd_ready.reserve(1)
            xh0, xt0 = xhat_ready.reserve(n_tiles), xT_transposed.reserve(2 * n_groups)
            xa0, xd0 = xT_ready.reserve(n_groups), xT_dve.reserve(n_groups)
            with nc.Block() as block:
                @block.vector
                def _(dve):
                    for t in range(n_tiles):
                        last = nc.vector.bn_stats(stats[:, t, :], x_tiles(t))
                    last.then_inc(stats_ready.sem, 1)
                    dve.wait_ge(stats_ready.sem, st0 + 1)
                    for t in range(n_tiles):
                        last = nc.vector.bn_aggr(mean_var[:, t, :], stats[:, t, :])
                    last.then_inc(stats_ready.sem, 1)
                    dve.wait_ge(stats_ready.sem, st0 + 2)
                    nc.vector.tensor_scalar(var_eps[:, 0:n_tiles], mean_var[:, 0:n_tiles, 1], EPS, None,
                                            ALU.add).then_inc(var_ready.sem, 1)
                    dve.wait_ge(rstd_ready.sem, rs0 + 1)
                    for t in range(n_tiles):
                        nc.vector.tensor_scalar(xhat[:, t, :], x_tiles(t), mean_var[:, t, 0:1],
                                                rstd[:, t:t + 1], ALU.subtract, ALU.mult)\
                            .then_inc(xhat_ready.sem, 1)
                    for g in range(n_groups):
                        dve.wait_ge(xT_transposed.sem, xt0 + 2 * g + 2)
                        nc.vector.tensor_scalar(dst[:, 1, g * group_cols:(g + 1) * group_cols],
                                                ps[:, 2 * g + 1, 0:group_cols], norm_scale(1, g),
                                                norm_shift(1, g), ALU.mult, ALU.add)\
                            .then_inc(xT_dve.sem, 1)

                @block.gpsimd
                def _(pool):
                    pool.wait_ge(var_ready.sem, va0 + 1)
                    nc.gpsimd.tensor_tensor(rstd[:, 0:n_tiles], var_eps[:, 0:n_tiles],
                                            minus_half[:, 0:n_tiles], ALU.pow).then_inc(rstd_ready.sem, 1)

                @block.tensor
                def _(pe):
                    for g in range(n_groups):
                        for c in range(C):
                            for t in range(per_group):
                                if c == 0:
                                    pe.wait_ge(xhat_ready.sem, xh0 + g * per_group + t + 1)
                                last = nc.tensor.transpose(ps[:, 2 * g + c, t * P:(t + 1) * P],
                                                           xhat[:, g * per_group + t, c * P:(c + 1) * P],
                                                           ident)
                            last.then_inc(xT_transposed.sem, 1)

                @block.scalar
                def _(act):
                    for g in range(n_groups):
                        act.wait_ge(xT_transposed.sem, xt0 + 2 * g + 1)
                        nc.scalar.activation(dst[:, 0, g * group_cols:(g + 1) * group_cols],
                                             ps[:, 2 * g, 0:group_cols], ACT.Identity,
                                             bias=norm_shift(0, g), scale=norm_scale(0, g))\
                            .then_inc(xT_ready.sem, 1)

        def stack_dmas(sp, stack, parts, slot, part, signal):
            for g in range(C):
                sp.dma_start(stack[slot * HD:(slot + 1) * HD, g * HPC:(g + 1) * HPC, :], parts(part, g))\
                    .then_inc(signal.sem, 16)


        def norm(half, i, x_wait):
            st0, va0, rs0 = stats_ready.reserve(2), var_ready.reserve(1), rstd_ready.reserve(1)
            xh0, xt0, xr0 = xhat_ready.reserve(4), xT_transposed.reserve(1), xT_ready.reserve(2)
            tiles = range(4 * half, 4 * half + 4)
            four = slice(4 * half, 4 * half + 4)

            def dve(dve):
                if x_wait is not None:
                    dve.wait_ge(x_ready.sem, x_wait)
                for t in tiles:
                    last = nc.vector.bn_stats(stats[:, t, :], x[:, t, :])
                last.then_inc(stats_ready.sem, 1)
                dve.wait_ge(stats_ready.sem, st0 + 1)
                for t in tiles:
                    last = nc.vector.bn_aggr(mean_var[:, t, :], stats[:, t, :])
                last.then_inc(stats_ready.sem, 1)
                dve.wait_ge(stats_ready.sem, st0 + 2)
                nc.vector.tensor_scalar(var_eps[:, four], mean_var[:, four, 1], EPS, None, ALU.add)\
                    .then_inc(var_ready.sem, 1)
                dve.wait_ge(rstd_ready.sem, rs0 + 1)
                for t in tiles:
                    nc.vector.tensor_scalar(xhat[:, t, :], x[:, t, :], mean_var[:, t, 0:1], rstd[:, t:t + 1],
                                            ALU.subtract, ALU.mult).then_inc(xhat_ready.sem, 1)

            def pool(pool):
                pool.wait_ge(var_ready.sem, va0 + 1)
                nc.gpsimd.tensor_tensor(rstd[:, four], var_eps[:, four], minus_half[:, four], ALU.pow)\
                    .then_inc(rstd_ready.sem, 1)

            def pe(pe):
                for k, t in enumerate(tiles):
                    pe.wait_ge(xhat_ready.sem, xh0 + k + 1)
                    for c in range(C):
                        last = nc.tensor.transpose(ps[:, 2 * half + c, k * P:(k + 1) * P],
                                                   xhat[:, t, c * P:(c + 1) * P], ident)
                last.then_inc(xT_transposed.sem, 1)

            def act(act):
                act.wait_ge(xT_transposed.sem, xt0 + 1)
                for c in range(C):
                    nc.scalar.activation(xT[:, c, half * HALF:(half + 1) * HALF], ps[:, 2 * half + c, :],
                                         ACT.Identity, bias=affine_b[:, i, 1, c:c + 1],
                                         scale=affine_b[:, i, 0, c:c + 1]).then_inc(xT_ready.sem, 1)
            return Stage(dve=dve, pool=pool, pe=pe, act=act, done=xr0 + 2, xhat_done=xh0 + 4)

        def add_bias(half, after, row):
            bi0 = biased.reserve(1)

            def pool(pool):
                pool.wait_ge(xhat_ready.sem, after.xhat_done)
                nc.gpsimd.tensor_tensor(x[:, 4 * half:4 * half + 4, :], x[:, 4 * half:4 * half + 4, :],
                                        row[:].rearrange("p (o d) -> p o d", o=1).to_broadcast([P, 4, D]), ALU.add)\
                    .then_inc(biased.sem, 1)
            return Stage(pool=pool, done=bi0 + 1)

        def parts_of(half, rest, parts, source):
            hi0, re0, mi0, lo0 = (s.reserve(C) for s in (high_ready, rest_ready, middle_ready, low_ready))
            cols = slice(half * HALF, (half + 1) * HALF)

            def act_high(act, wait):
                for m in range(C):
                    wait(act, m)
                    bank, bias = source(m) if source else (rest[:, m, cols], 0.0)
                    nc.scalar.activation(parts[:, 0, m, cols], bank, ACT.Identity, bias=bias)\
                        .then_inc(high_ready.sem, 1)

            def act_middle(act):
                for m in range(C):
                    act.wait_ge(rest_ready.sem, re0 + m + 1)
                    nc.scalar.activation(parts[:, 1, m, cols], rest[:, m, cols], ACT.Copy)\
                        .then_inc(middle_ready.sem, 1)

            def dve(dve):
                for m in range(C):
                    dve.wait_ge(high_ready.sem, hi0 + m + 1)
                    if source:
                        bank, bias = source(m)
                        nc.vector.scalar_tensor_tensor(rest[:, m, cols], bank, bias, parts[:, 0, m, cols],
                                                       ALU.add, ALU.subtract).then_inc(rest_ready.sem, 1)
                    else:
                        nc.vector.tensor_tensor(rest[:, m, cols], rest[:, m, cols], parts[:, 0, m, cols],
                                                ALU.subtract).then_inc(rest_ready.sem, 1)

            def pool(pool):
                for m in range(C):
                    pool.wait_ge(middle_ready.sem, mi0 + m + 1)
                    nc.gpsimd.tensor_tensor(parts[:, 2, m, cols], rest[:, m, cols], parts[:, 1, m, cols],
                                            ALU.subtract).then_inc(low_ready.sem, 1)
            ready = ((high_ready.sem, hi0 + C), (middle_ready.sem, mi0 + C), (low_ready.sem, lo0 + C))
            return Stage(act_high=act_high, act_middle=act_middle, dve=dve, pool=pool, ready=ready)

        def stack_q(sp, half, parts):
            cols = slice(half * HALF, (half + 1) * HALF)
            for part, ready in enumerate(parts.ready):
                sp.wait_ge(*ready)
                for s in range(N_SLOT):
                    if Q_SLOTS[s] == part:
                        stack_dmas(sp, q_stack[:, half], lambda i, g: q_parts[:, i, g, cols], s, part,
                                   q_stacked[half])
            q_stacked[half].reserve(16 * N_SLOT * C)

        def query(half, w, bias, after):
            pr0 = product.reserve(C)
            parts = parts_of(half, q_rest, q_parts, lambda m: (ps[:, 4 + 2 * half + m, :], bias(m)))

            def pe(pe):
                pe.wait_ge(xT_ready.sem, after.done)
                for m in range(C):
                    for c in range(C):
                        last = nc.tensor.matmul(ps[:, 4 + 2 * half + m, :], w[:, c, m * P:(m + 1) * P],
                                                xT[:, c, half * HALF:(half + 1) * HALF],
                                                start=(c == 0), stop=(c == C - 1))
                    last.then_inc(product.sem, 1)

            def act(act):
                parts.act_high(act, lambda act, m: act.wait_ge(product.sem, pr0 + m + 1))
                parts.act_middle(act)
            return Stage(pe=pe, act=act, dve=parts.dve, pool=parts.pool,
                                   sp=lambda sp: stack_q(sp, half, parts))

        def scores_max(half, k_of, keys, mask_tile, running, free):
            n = 8
            sc0, mt0 = scores_ready.reserve(n), max_taken.reserve(n)
            view = ps[:].rearrange("p (u b) (h k) -> p u (b h) k", u=4, h=4)
            dst = tile_max if running else neg_max

            def pe(pe, first, end):
                if first == 0:
                    free(pe)
                for k in range(first, end):
                    t = 4 * half + k // 2
                    if mt0 + k >= 2:
                        pe.wait_ge(max_taken.sem, mt0 + k - 1)
                    for i in range(8):
                        h = k % 2 * 8 + i
                        o = view[:, k % 2, i, 0:keys]
                        if mask_tile is not None:
                            nc.tensor.matmul(o, mask_tile(slice(t * P, (t + 1) * P)), ident_bf[:],
                                             start=True, stop=False)
                        last = nc.tensor.matmul(o, q_stack[0:BIAS_ROW + 1, half, h, k // 2 * P:(k // 2 + 1) * P],
                                                k_of(h, BIAS_ROW + 1), start=mask_tile is None, stop=True)
                    last.then_inc(scores_ready.sem, 1)

            def dve(dve, first, end):
                for k in range(first, end):
                    dve.wait_ge(scores_ready.sem, sc0 + k + 1)
                    nc.vector.tensor_reduce(dst[:, half, k % 2 * 8:k % 2 * 8 + 8, k // 2],
                                            view[:, k % 2, :, 0:keys], AX_X, ALU.max, negate=True)\
                        .then_inc(max_taken.sem, 1)
            return Stage(pe=pe, dve=dve, done=mt0 + n)

        def turn_max(half, taken):
            tu0, hi0 = max_turned.reserve(1), max_high.reserve(1)
            re0, mi0, lo0 = max_rest1.reserve(1), max_middle.reserve(1), max_low.reserve(1)
            rows = NH * T // 2
            bank = ps[0:rows, 4 + 2 * half, 0:P]

            def pe(pe):
                if taken is not None:
                    pe.wait_ge(max_taken.sem, taken)
                nc.tensor.transpose(bank, neg_max[:, half].rearrange("p h t -> p (h t)"), ident)\
                    .then_inc(max_turned.sem, 1)

            def act(act):
                act.wait_ge(max_turned.sem, tu0 + 1)
                nc.scalar.activation(max_parts[0:rows, half, 0, :], bank, ACT.Copy).then_inc(max_high.sem, 1)
                act.wait_ge(max_rest1.sem, re0 + 1)
                nc.scalar.activation(max_parts[0:rows, half, 1, :], max_rest[0:rows, half, :], ACT.Copy)\
                    .then_inc(max_middle.sem, 1)

            def dve(dve):
                dve.wait_ge(max_high.sem, hi0 + 1)
                nc.vector.tensor_tensor(max_rest[0:rows, half, :], bank, max_parts[0:rows, half, 0, :],
                                        ALU.subtract).then_inc(max_rest1.sem, 1)

            def pool(pool):
                pool.wait_ge(max_middle.sem, mi0 + 1)
                nc.gpsimd.tensor_tensor(max_parts[0:rows, half, 2, :], max_rest[0:rows, half, :],
                                        max_parts[0:rows, half, 1, :], ALU.subtract).then_inc(max_low.sem, 1)

            def sp(sp):
                for i, ready in enumerate(((max_high.sem, hi0 + 1), (max_middle.sem, mi0 + 1),
                                           (max_low.sem, lo0 + 1))):
                    sp.wait_ge(*ready)
                    row = q_stack[MAX_ROWS + i:MAX_ROWS + i + 1, half]
                    sp.dma_start(row.rearrange("o h (t q) -> o (h t) q", q=P), max_parts[0:rows, half, i, :])\
                        .then_inc(q_stacked[half].sem, 16)
                q_stacked[half].reserve(48)
            return Stage(pe=pe, act=act, dve=dve, pool=pool, sp=sp, read=re0 + 1)

        def weigh(half, k_of, v, mask_tile, add_to, q_ready, free):
            ke0, ex0, pv0 = keyed_ready.reserve(NH // 2), exp_done.reserve(NH // 2), pv_done.reserve(4)
            rd0, no0 = recip_done.reserve(C), normed.reserve(C)
            cols = slice(half * HALF, (half + 1) * HALF)

            def pe(pe, between=None):
                def products(quad):
                    g, sub = quad // 2, quad % 2
                    pe.wait_ge(exp_done.sem, ex0 + 2 * quad + 2)
                    if sub == 0:
                        free(pe, g)
                        if half == 1:
                            pe.wait_ge(normed.sem, no0 - C + g + 1)
                    for what in range(2):
                        for j in range(4):
                            n = 4 * quad + j
                            w = v[:, 8 * g + 2 * j + sub, :] if what == 0 else ones_pad[:, sub, :]
                            last = nc.tensor.matmul(ps[32 * j:32 * j + 32, 4 + 2 * g + what, :], w,
                                                    probs[:, n // 2 % 4, n % 2, :],
                                                    start=(sub == 0), stop=(sub == 1), skip_group_check=True)
                    last.then_inc(pv_done.sem, 1)

                if q_ready is not None:
                    pe.wait_ge(q_stacked[half].sem, q_ready)
                for n in range(NH):
                    quad, j = n // 4, n % 4
                    h = 8 * (quad // 2) + 2 * j + quad % 2
                    if n % 2 == 0 and n >= 4:
                        pe.wait_ge(exp_done.sem, ex0 + n // 2 - 1)
                    o = ps[:, n % 4, :]
                    if mask_tile is not None:
                        nc.tensor.matmul(o, ident_bf[:], mask_tile(cols), start=True, stop=False)
                    last = nc.tensor.matmul(o, k_of(h, STACK), q_stack[0:STACK, half, h, :],
                                            start=mask_tile is None, stop=True)
                    if n % 2 == 1:
                        last.then_inc(keyed_ready.sem, 1)
                    if n == 3 and between:
                        between(pe)
                    if j == 3 and quad >= 1:
                        products(quad - 1)
                products(3)

            def act(act, between=None):
                for p in range(NH // 2):
                    act.wait_ge(keyed_ready.sem, ke0 + p + 1)
                    if 8 * half + p >= 4:
                        act.wait_ge(pv_done.sem, pv0 + p // 2 - 1)
                    nc.scalar.activation(probs[:, p % 4].rearrange("p k s -> p (k s)"),
                                         ps[:, 2 * (p % 2):2 * (p % 2) + 2, :].rearrange("p a b -> p (a b)"),
                                         ACT.Exp, scale=SCALE).then_inc(exp_done.sem, 1)
                    if p == 1 and between:
                        between(act)

            def dve(dve):
                for g in range(C):
                    dve.wait_ge(pv_done.sem, pv0 + 2 * g + 2)
                    o, total = ps[:, 4 + 2 * g, :], ps[:, 5 + 2 * g, :]
                    if add_to:
                        nc.vector.tensor_tensor(sums[:, g, cols], sums[:, g, cols], total, ALU.add)\
                            .then_inc(recip_done.sem, 1)
                        nc.vector.tensor_tensor(xT[:, g, cols], xT[:, g, cols], o, ALU.add)\
                            .then_inc(normed.sem, 1)
                    else:
                        nc.vector.reciprocal(inverse[:, g, :], total).then_inc(recip_done.sem, 1)
                        dve.wait_ge(recip_done.sem, rd0 + g + 1)
                        nc.vector.tensor_tensor(xT[:, g, cols], o, inverse[:, g, :], ALU.mult)\
                            .then_inc(normed.sem, 1)
            return Stage(pe=pe, act=act, dve=dve, done=no0 + C)

        def project_back(half, act_in, weights, n_chunks, wait_input, wait_bias):
            pr0, xr0 = product.reserve(2), x_ready.reserve(2)

            def pe(pe):
                wait_input(pe)
                for k in range(2):
                    for r in range(2):
                        for c in range(n_chunks):
                            last = nc.tensor.matmul(ps[:, 2 * half + k, r * D:(r + 1) * D], act_in(c, 2 * k + r),
                                                    weights[:, c, :], start=(c == 0), stop=(c == n_chunks - 1))
                    last.then_inc(product.sem, 1)

            def dve(dve):
                if wait_bias is not None:
                    dve.wait_ge(biased.sem, wait_bias)
                for k in range(2):
                    dve.wait_ge(product.sem, pr0 + k + 1)
                    two = x[:, 4 * half + 2 * k:4 * half + 2 * k + 2, :].rearrange("p t d -> p (t d)")
                    nc.vector.tensor_tensor(two, two, ps[:, 2 * half + k, :], ALU.add).then_inc(x_ready.sem, 1)
            return Stage(pe=pe, dve=dve, done=xr0 + 2)

        def xT_tile(half):
            return lambda c, k: xT[:, c, half * HALF + k * P:half * HALF + (k + 1) * P]

        ada_w = arena_a[:, 0:C * 18 * P].rearrange("p (c n) -> p c n", c=C)
        ss_q = arena_a[:, 4608:5632].rearrange("p (c n) -> p c n", c=C)
        ss_kv = arena_a[:, 5632:6656].rearrange("p (c n) -> p c n", c=C)
        w_kv = arena_r[:, 0:1024].rearrange("p (c n) -> p c n", c=C)
        w_ck = arena_r[:, 1024:1536].rearrange("p (c n) -> p c n", c=C)
        w_cv = arena_r[:, 1536:2048].rearrange("p (c n) -> p c n", c=C)
        cT_norm = arena_r[:, 2048:3072].rearrange("p (c n) -> p c n", c=C)
        cT_raw = arena_r[:, 3072:4096].rearrange("p (c n) -> p c n", c=C)
        kc = arena_r[:, 4096:6144].rearrange("p (c b l k) -> p c b l k", c=C, b=B, l=2)
        kc_flat = arena_r[:, 4096:6144].rearrange("p (c n) -> p c n", c=C)
        kc_parts = k_parts
        mask_raw = arena_r[:, 6144:8192].bitcast(U8).rearrange("p (t k) -> p t k", t=T)
        k_ctx_all = arena_a[:, :].bitcast(BF16).rearrange("p (h k) -> p h k", h=NH)
        ctx_tok = x[:, 0:B, :]
        temps = arena_r[:, 8192:10240].rearrange("p (c s) -> p c s", c=C)
        vec_rows = temps[0:N_VEC, 0, 0:P]
        cond = temps[0:B, 0, 128:128 + D]
        ctx_mask = temps[:, 1, 0:B * LC // 4].bitcast(U8).rearrange("p (b k) -> p b k", b=B)
        condT = temps[:, 0, 512:512 + C * B].rearrange("p (c b) -> p c b", c=C)
        siluT = temps[:, 0, 544:544 + C * B].rearrange("p (c b) -> p c b", c=C)
        expT = temps[:, 0, 576:576 + C * B].rearrange("p (c b) -> p c b", c=C)
        mod = temps[:, 0, 640:640 + N_MOD * B].rearrange("p (j b) -> p j b", j=N_MOD)
        bv_row = temps[:, 0, 768:768 + D]
        any_ctx = temps[:, 1, 128:128 + B]
        key_bias = temps[:, 1, 256:768].bitcast(BF16).rearrange("p (b l k) -> p b l k", b=B, l=2)
        any_q = temps[:, 1, 800:800 + T]
        none_q = temps[:, 1, 816:816 + T]
        keep = temps[:, 1, 832:832 + T]
        seen = temps[:, 1, 848:848 + T * T].rearrange("p (t k) -> p t k", t=T)
        list_tmp = temps[:, 1, 920:920 + 24]
        bias_nat = xT[:].rearrange("p c s -> p (c s)").bitcast(BF16).rearrange("p (t k) -> p t k", t=4)

        with nc.Block() as block:
            @block.sync
            def _(sp):
                def load(dst, src):
                    sp.dma_start(dst[:], src).then_inc(loads.sem, 16)
                    loads.at += 16
                load(const[:], a["shape_consts"])
                for name, (at, n) in VEC_ROWS.items():
                    load(vec_rows[at:at + n, :], a[name].rearrange("(j p) -> j p", p=P))
                load(cond, a["cond"])
                load(ctx_mask, a["ctx_mask"].rearrange("(o b) k -> o b k", o=1).to_broadcast([P, B, LC]))
                for dst, name in ((ss_q, "Wss_q"), (ss_kv, "Wss_kv"), (ada_w, "adaLN_W"), (w_kv, "Wkv"),
                                  (w_ck, "ck_W"), (w_cv, "cv_W")):
                    load(dst, a[name].rearrange("(c p) n -> p c n", p=P))
                sp.wait_ge(pool_done.sem, 1)
                load(ctx_tok[0:LC], a["ctx"].rearrange("b k d -> k b d"))
                load(mask_raw, a["mask"].rearrange("(t p) k -> p t k", p=P))
                for dst, name in ((w_q, "Wq"), (w_p, "Wp"), (w_qkv, "qkv_W"), (w_out, "attn_out_W"), (w_cq, "cq_W"),
                                  (w_co, "co_W"), (w_1, "mlp_W1"), (w_2, "mlp_W2")):
                    load(dst, a[name].rearrange("(c p) n -> p c n", p=P))
                sp.wait_ge(loads.sem, loads.at)

            @block.gpsimd
            def _(pool):
                nc.gpsimd.memset(ctx_tok[:], 0.0).then_inc(pool_done.sem, 1)
                nc.gpsimd.memset(minus_half[:], -0.5)
                nc.gpsimd.memset(ones_row[:], 1.0)
                nc.gpsimd.memset(v_pad[:], 0.0)
                nc.gpsimd.memset(ones_pad[:], 0.0).then_inc(pool_done.sem, 1)
                pool.wait_ge(pool_done.sem, 2)
                nc.gpsimd.memset(ones_pad[:, 0, 0:HD], 1.0)
                nc.gpsimd.memset(ones_pad[:, 1, HD:2 * HD], 1.0)
                pool_done.at = 2

            @block.vector
            def _(dve):
                nc.vector.memset(key_bias[0:1], MASKED)
                nc.vector.memset(k_self[BIAS_ROW:P], 1.0).then_inc(dve_done.sem, 1)
                dve.wait_ge(dve_done.sem, 1)
                nc.vector.memset(key_bias[0:1, :, 0, 0:LC], 0.0)
                nc.vector.memset(k_self[BIAS_ROW:BIAS_ROW + 1], 0.0)

        with nc.Block() as block:
            @block.tensor
            def _(pe):
                nc.tensor.transpose(ps[:, 0, 0:N_VEC], vec_rows, ident[0:N_VEC, 0:N_VEC])
                for c in range(C):
                    last = nc.tensor.transpose(ps[:, 1, c * B:(c + 1) * B], cond[:, c * P:(c + 1) * P],
                                               ident[0:B, 0:B])
                last.then_inc(pe_done.sem, 1)

            @block.scalar
            def _(act):
                act.wait_ge(dve_done.sem, 2)
                nc.scalar.activation(expT, condT, ACT.Exp, scale=-1.0).then_inc(act_done.sem, 1)

            @block.vector
            def _(dve):
                nc.vector.tensor_copy(ident_bf[:], ident)
                dve.wait_ge(pe_done.sem, 1)
                nc.vector.tensor_copy(vec[:], ps[:, 0, 0:N_VEC])
                nc.vector.tensor_copy(condT, ps[:, 1, 0:C * B].rearrange("p (c b) -> p c b", c=C))\
                    .then_inc(dve_done.sem, 1)
                dve.wait_ge(act_done.sem, 1)
                nc.vector.tensor_scalar(expT, expT, 1.0, None, ALU.add).then_inc(dve_done.sem, 1)
                dve.wait_ge(dve_done.sem, 3)
                nc.vector.reciprocal(siluT, expT).then_inc(dve_done.sem, 1)
                dve.wait_ge(dve_done.sem, 4)
                nc.vector.tensor_tensor(siluT, siluT, condT, ALU.mult)
                nc.vector.tensor_reduce(any_ctx, ctx_mask, AX_X, ALU.max).then_inc(dve_done.sem, 1)
                dve.wait_ge(dve_done.sem, 5)
                nc.vector.tensor_scalar(list_tmp[0:1, 0:B], any_ctx[0:1, :], -MASKED, None, ALU.mult)\
                    .then_inc(dve_done.sem, 1)
                dve.wait_ge(dve_done.sem, 6)
                for b in range(B):
                    last = nc.vector.tensor_scalar(key_bias[0:1, b, 1, 0:LC], ctx_mask[0:1, b, :], 1.0,
                                                   list_tmp[0:1, b:b + 1], ALU.subtract, ALU.mult)
                last.then_inc(dve_done.sem, 1)
                dve_done.at = 7
            act_done.at = pe_done.at = 1

        with nc.Block() as block:
            @block.tensor
            def _(pe):
                for j in range(N_MOD):
                    w, at, c_in = (ss_q, j, siluT) if j < 4 else (ss_kv, j - 4, siluT) if j < 8 else (ada_w, j - 8, condT)
                    for c in range(C):
                        last = nc.tensor.matmul(ps[:, 0, j * B:(j + 1) * B], w[:, c, at * P:(at + 1) * P],
                                                c_in[:, c, :], start=(c == 0), stop=(c == C - 1))
                last.then_inc(pe_done.sem, 1)
                for c in range(C):
                    for k, name in enumerate(("bp", "bkv")):
                        pe.wait_ge(act_done.sem, 1 + 2 * c + k + 1)
                        last = nc.tensor.matmul(ps[:, 1 + k, c * P:(c + 1) * P], spread[:, k, :], ident,
                                                start=True, stop=True)
                    last.then_inc(pe_done.sem, 1)

            @block.scalar
            def _(act):
                for c in range(C):
                    if c:
                        act.wait_ge(pe_done.sem, 3)
                    for k, col in enumerate((vcol("bp", c), vcol("bkv", 2 + c))):
                        nc.scalar.activation(spread[:, k, :], col.to_broadcast([P, P]), ACT.Copy)\
                            .then_inc(act_done.sem, 1)

            @block.vector
            def _(dve):
                dve.wait_ge(pe_done.sem, 2)
                for b in range(B):
                    last = nc.vector.tensor_tensor(mod[:, :, b],
                                                   ps[:, 0, 0:N_MOD * B].rearrange("p (j b) -> p j b", j=N_MOD)[:, :, b],
                                                   vec[:, 0:N_MOD], ALU.add)
                last.then_inc(dve_done.sem, 1)
                dve.wait_ge(dve_done.sem, 8)
                for i, (norm, (sc, sh)) in enumerate(NORMS.items()):
                    for c in range(C):
                        nc.vector.tensor_scalar(affine[:, :, i, 0, c], mod[:, sc + c, :], 1.0, None, ALU.add)
                        last = nc.vector.tensor_copy(affine[:, :, i, 1, c], mod[:, sh + c, :])
                for c in range(C):
                    for i, j in enumerate((GATES["msa"], GATES["x"], GATES["mlp"])):
                        nc.vector.tensor_copy(gates[:, :, i, c], mod[:, j + c, :])
                    last = nc.vector.tensor_scalar(gates[:, :, 3, c], mod[:, GATES["mlp"] + c, :], vcol("mlp_b2", c),
                                                   None, ALU.mult)
                last.then_inc(dve_done.sem, 1)
                dve.wait_ge(dve_done.sem, 9)
                for i, name in ((2, "norm1_w"), (3, "normc_w"), (4, "norm2_w")):
                    for c in range(C):
                        last = nc.vector.tensor_scalar(affine[:, :, i, 0, c], affine[:, :, i, 0, c], vcol(name, c),
                                                       None, ALU.mult)
                dve.wait_ge(pe_done.sem, 4)
                nc.vector.tensor_copy(bp_row[:], ps[:, 1, 0:D])
                nc.vector.tensor_copy(bv_row, ps[:, 2, 0:D]).then_inc(dve_done.sem, 1)
                dve_done.at = 10
            act_done.at, pe_done.at = 5, 4

        with nc.Block() as block:
            @block.tensor
            def _(pe):
                for c in range(C):
                    for b in range(B):
                        last = nc.tensor.transpose(ps[:, c, b * P:(b + 1) * P], ctx_tok[:, b, c * P:(c + 1) * P], ident)
                last.then_inc(pe_done.sem, 1)

            @block.vector
            def _(dve):
                dve.wait_ge(pe_done.sem, 5)
                for c in range(C):
                    last = nc.vector.tensor_copy(cT_raw[:, c, :], ps[:, c, :])
                last.then_inc(dve_done.sem, 1)
            dve_done.at, pe_done.at = 11, 5
        context_norm(lambda t: ctx_tok[:, t, :], B, lambda c, g: affine[:, g, 1, 0, c:c + 1],
                   lambda c, g: affine[:, g, 1, 1, c:c + 1], cT_norm, B, P)

        with nc.Block() as block:
            @block.tensor
            def _(pe):
                for layer, (w, src) in enumerate(((w_kv, cT_norm), (w_ck, cT_raw))):
                    for m in range(C):
                        for c in range(C):
                            last = nc.tensor.matmul(ps[:, 2 * layer + m, :], w[:, c, m * P:(m + 1) * P],
                                                    src[:, c, :],
                                                    start=(c == 0), stop=(c == C - 1))
                last.then_inc(pe_done.sem, 1)
                for layer in range(2):
                    for b in range(B):
                        src, w = (cT_norm, w_kv[:, :, D:2 * D]) if layer == 0 else (cT_raw, w_cv)
                        for c in range(C):
                            last = nc.tensor.matmul(ps[:, 4 + b, layer * D:(layer + 1) * D],
                                                    src[:, c, b * P:(b + 1) * P], w[:, c, :],
                                                    start=(c == 0), stop=(c == C - 1))
                last.then_inc(pe_done.sem, 1)

            @block.vector
            def _(dve):
                nc.vector.memset(k_ctx_all[BIAS_ROW:P], 1.0).then_inc(xT_dve.sem, 1)
                dve.wait_ge(pe_done.sem, 6)
                for c in range(C):
                    for b in range(B):
                        nc.vector.tensor_scalar(kc[:, c, b, 0, :], ps[:, c, b * P:(b + 1) * P], vcol("bkv", c), None,
                                                ALU.add)
                        last = nc.vector.tensor_scalar(kc[:, c, b, 1, :], ps[:, 2 + c, b * P:(b + 1) * P],
                                                       any_ctx[:, b:b + 1], None, ALU.mult)
                last.then_inc(dve_done.sem, 1)
                dve.wait_ge(pe_done.sem, 7)
                for b in range(B):
                    nc.vector.tensor_tensor(v_ctx[:, b, 0, :], ps[:, 4 + b, 0:D], bv_row, ALU.add)
                    last = nc.vector.tensor_copy(v_ctx[:, b, 1, :], ps[:, 4 + b, D:2 * D])
                dve.wait_ge(dve_done.sem, 12)
                nc.vector.tensor_copy(kc_parts[:, 0], kc_flat).then_inc(dve_done.sem, 1)
                dve.wait_ge(dve_done.sem, 13)
                nc.vector.tensor_tensor(kc_flat, kc_flat, kc_parts[:, 0], ALU.subtract).then_inc(dve_done.sem, 1)
                dve.wait_ge(dve_done.sem, 14)
                nc.vector.tensor_copy(kc_parts[:, 1], kc_flat).then_inc(dve_done.sem, 1)
                dve.wait_ge(dve_done.sem, 15)
                nc.vector.tensor_tensor(kc_parts[:, 2], kc_flat, kc_parts[:, 1], ALU.subtract)\
                    .then_inc(dve_done.sem, 1)
                dve_done.at = 16

            @block.sync
            def _(sp):
                sp.wait_ge(xT_dve.sem, xT_dve.reserve(1) + 1)
                for h in range(NH):
                    sp.dma_start(k_ctx_all[BIAS_ROW:BIAS_ROW + 1, h, :],
                                 key_bias[0:1].rearrange("o b l k -> o (b l k)")).then_inc(k_stacked.sem, 16)
                sp.wait_ge(dve_done.sem, 16)
                for s, part in enumerate(K_SLOTS):
                    stack_dmas(sp, k_ctx_all, lambda i, g: kc_parts[:, i, g, :], s, part, k_stacked)
                k_stacked.at = 16 * (N_SLOT * C + NH)
                sp.wait_ge(k_stacked.sem, k_stacked.at)
                sp.dma_start(k_ctx_dram, k_ctx_all[0:STACK]).then_inc(stored.sem, 16)
                sp.wait_ge(stored.sem, 16)
            pe_done.at = 7

        with nc.Block() as block:
            @block.vector
            def _(dve):
                nc.vector.tensor_reduce(any_q, mask_raw, AX_X, ALU.max).then_inc(dve_done.sem, 1)
                nc.vector.tensor_reduce(seen, mask_raw.rearrange("p t (j k) -> p t j k", k=P), AX_X, ALU.max)\
                    .then_inc(dve_done.sem, 1)
                dve.wait_ge(dve_done.sem, 18)
                nc.vector.tensor_reduce(keep, seen.rearrange("p t k -> p k t"), AX_X, ALU.max)
                nc.vector.tensor_scalar(none_q, any_q, -MASKED, None, ALU.mult)
                nc.vector.tensor_reduce(list_tmp[:, 0:1], any_q, AX_X, ALU.min).then_inc(dve_done.sem, 1)
                dve.wait_ge(dve_done.sem, 19)
                nc.vector.tensor_scalar(list_tmp[:, 0:1], list_tmp[:, 0:1], -1.0, 1.0, ALU.mult, ALU.add)\
                    .then_inc(dve_done.sem, 1)
                dve.wait_ge(dve_done.sem, 20)
                nc.vector.tensor_scalar(keep, keep, list_tmp[:, 0:1], None, ALU.max).then_inc(dve_done.sem, 1)
                dve.wait_ge(pe_done.sem, 8)
                nc.vector.tensor_reduce(list_tmp[0:T, 1:2], ps[0:T, 0, 0:P], AX_X, ALU.max)\
                    .then_inc(dve_done.sem, 1)
                dve.wait_ge(pe_done.sem, 9)
                nc.vector.tensor_copy(list_tmp[0:T, 2:3], ps[0:T, 1, 0:1]).then_inc(dve_done.sem, 1)
                dve.wait_ge(dve_done.sem, 23)
                nc.vector.tensor_scalar(list_tmp[0:T, 8:8 + T], constant("iota")[0:T, :], list_tmp[0:T, 2:3],
                                        list_tmp[0:T, 1:2], ALU.is_equal, ALU.mult).then_inc(dve_done.sem, 1)
                dve.wait_ge(pe_done.sem, 10)
                nc.vector.tensor_copy(tile_list[0:1, :], ps[0:1, 2, 0:1 + T]).then_inc(dve_done.sem, 1)

            @block.tensor
            def _(pe):
                pe.wait_ge(dve_done.sem, 21)
                nc.tensor.transpose(ps[0:T, 0, 0:P], keep, ident).then_inc(pe_done.sem, 1)
                pe.wait_ge(dve_done.sem, 22)
                nc.tensor.matmul(ps[0:T, 1, 0:1], constant("before")[0:T, :], list_tmp[0:T, 1:2], start=True, stop=True)\
                    .then_inc(pe_done.sem, 1)
                pe.wait_ge(dve_done.sem, 24)
                nc.tensor.matmul(ps[0:1, 2, 0:1], constant("iota")[0:T, 1:2], list_tmp[0:T, 1:2], start=True, stop=True)
                nc.tensor.matmul(ps[0:1, 2, 1:1 + T], constant("tile")[0:T, :], list_tmp[0:T, 8:8 + T], start=True,
                                 stop=True).then_inc(pe_done.sem, 1)
            dve_done.at, pe_done.at = 25, 10
        for q4 in range(2):
            with nc.Block() as block:
                d0, p0 = dve_done.reserve(3), pe_done.reserve(8)

                @block.vector
                def _(dve):
                    for t in range(4):
                        tt = 4 * q4 + t
                        last = nc.vector.tensor_scalar(bias_nat[:, t, :], mask_raw[:, tt, :], 1.0, none_q[:, tt:tt + 1],
                                                       ALU.subtract, ALU.mult)
                    last.then_inc(dve_done.sem, 1)
                    for j in range(T):
                        dve.wait_ge(pe_done.sem, p0 + j + 1)
                        last = nc.vector.tensor_copy(mask_bias[:, j, q4 * HALF:(q4 + 1) * HALF],
                                                     ps[:, j % 8, :].bitcast(BF16)[:, 0:HALF])

                @block.tensor
                def _(pe):
                    pe.wait_ge(dve_done.sem, d0 + 1)
                    for j in range(T):
                        for t in range(4):
                            last = nc.tensor.transpose(ps[:, j % 8, :].bitcast(BF16)[:, t * P:(t + 1) * P],
                                                       bias_nat[:, t, j * P:(j + 1) * P], ident_bf[:])
                        last.then_inc(pe_done.sem, 1)
                dve_done.at = d0 + 1
        with nc.Block() as block:
            d0, p0, a0 = dve_done.at, pe_done.at, act_done.at

            @block.scalar
            def _(act):
                for t in range(T):
                    if t >= 2:
                        act.wait_ge(pe_done.sem, p0 + t - 1)
                    nc.scalar.activation(spread[:, t % 2, :], any_q[:, t:t + 1].to_broadcast([P, P]), ACT.Copy)\
                        .then_inc(act_done.sem, 1)

            @block.tensor
            def _(pe):
                for t in range(T):
                    pe.wait_ge(act_done.sem, a0 + t + 1)
                    nc.tensor.matmul(ps[:, t // 4, (t % 4) * P:(t % 4 + 1) * P], spread[:, t % 2, :], ident, start=True,
                                     stop=True).then_inc(pe_done.sem, 1)

            @block.vector
            def _(dve):
                dve.wait_ge(pe_done.sem, p0 + T)
                for half in range(2):
                    for k, table in enumerate((cos_k, sin_k)):
                        nc.vector.tensor_tensor(rope_q[:, k, half * HALF:(half + 1) * HALF], ps[:, half, :], table,
                                                ALU.mult)
        clear_signals()
        n_tiles = nc.values_load(tile_list[0:1, 0:1], min_val=1, max_val=T)

        with nc.Fori(0, B) as b:
            with nc.Block() as block:
                @block.sync
                def _(sp):
                    sp.dma_start(x[:], a["x"][b].rearrange("(t p) d -> p t d", p=P)).then_inc(loads.sem, 16)
                    sp.dma_start(k_ctx[0:STACK], k_ctx_dram[:, :, bass.ds(b * (2 * P), 2 * P)]).then_inc(loads.sem, 16)
                    sp.dma_start(q_stack[BIAS_ROW:BIAS_ROW + 1].rearrange("o u h s -> o (u h s)"), ones_row[:]).then_inc(loads.sem, 16)
                    sp.wait_ge(loads.sem, 48)

                @block.vector
                def _(dve):
                    nc.vector.tensor_copy(affine_b[:].rearrange("p n k c -> p (n k c)"),
                                          affine[:, bass.ds(b, 1)].rearrange("p o n k c -> p (o n k c)"))
                    nc.vector.tensor_copy(gates_b[:].rearrange("p n c -> p (n c)"),
                                          gates[:, bass.ds(b, 1)].rearrange("p o n c -> p (o n c)"))

                @block.gpsimd
                def _(pool):
                    pad_v(nc.gpsimd, 0, v_ctx[:, bass.ds(b, 1), 0, :].rearrange("p o d -> p (o d)"))

            def gate_weights():
                gs0, gr0, ga0 = gate_spread.reserve(8), gate_rows.reserve(4), gated.reserve(4)

                def act(act):
                    for i in range(4):
                        for c in range(C):
                            if i >= 1:
                                act.wait_ge(gate_rows.sem, gr0 + i)
                            nc.scalar.activation(spread[:, c, :], gates_b[:, i, c:c + 1].to_broadcast([P, P]),
                                                 ACT.Copy).then_inc(gate_spread.sem, 1)

                def pe(pe):
                    for i in range(4):
                        for c in range(C):
                            pe.wait_ge(gate_spread.sem, gs0 + C * i + c + 1)
                            at = c * P
                            last = nc.tensor.matmul(ps[:, i, at:at + P], spread[:, c, :], ident,
                                                    start=True, stop=True)
                        last.then_inc(gate_rows.sem, 1)

                def dve(dve):
                    for i, (w, at, n) in enumerate(((w_out, 0, C), (w_co, C, C), (w_2, 2 * C, FF // P), (None, 0, 0))):
                        dve.wait_ge(gate_rows.sem, gr0 + i + 1)
                        row = ps[:, i, 0:D]
                        if w is None:
                            nc.vector.tensor_copy(gb2_row[:], row).then_inc(gated.sem, 1)
                        else:
                            nc.vector.tensor_tensor(w_gated[:, at:at + n, :], w[:],
                                                    row.rearrange("p (o d) -> p o d", o=1).to_broadcast([P, n, D]),
                                                    ALU.mult).then_inc(gated.sem, 1)
                return Stage(act=act, pe=pe, dve=dve, done=ga0 + 4)

            def cross_attention(layer, norm_i, w_query, bias, weights, x_waits, row, extra):
                norms = [norm(u, norm_i, x_waits[u]) for u in range(2)]
                rows = [add_bias(u, norms[u], row) for u in range(2)] if row is not None else [None, None]
                queries = [query(u, w_query, bias, norms[u]) for u in range(2)]
                base = [q_stacked[u].reserve(0) for u in range(2)]
                stacks_at = [base[u] + 16 * N_SLOT * C for u in range(2)]

                def k_of(h, rows, n):
                    return k_ctx[0:rows, h, layer * P:layer * P + n]

                def free_max(u):
                    def wait(pe):
                        pe.wait_ge(q_stacked[u].sem, stacks_at[u])
                        if u == 0 and extra is not None:
                            pe.wait_ge(gated.sem, extra.done)
                    return wait
                maxes = [scores_max(u, lambda h, rows: k_of(h, rows, LC), LC, None, False, free_max(u))
                         for u in range(2)]
                turns = [turn_max(u, maxes[u].done) for u in range(2)]

                def free_out(u):
                    def wait(pe, g):
                        if u == 0:
                            pe.wait_ge(max_rest1.sem, turns[g].read)
                    return wait
                sums_ = [weigh(u, lambda h, rows: k_of(h, rows, P), v_pad[:, 0], None, False,
                               stacks_at[u] + 48, free_out(u)) for u in range(2)]
                outs = [project_back(u, xT_tile(u), weights, C,
                                     lambda pe, u=u: pe.wait_ge(normed.sem, sums_[u].done),
                                     rows[u].done if rows[u] else None) for u in range(2)]

                def pe(pe):
                    norms[0].pe(pe)
                    norms[1].pe(pe)
                    queries[0].pe(pe)
                    queries[1].pe(pe)
                    if extra is not None:
                        extra.pe(pe)
                    maxes[0].pe(pe, 0, 8)
                    maxes[1].pe(pe, 0, 4)
                    turns[0].pe(pe)
                    maxes[1].pe(pe, 4, 8)
                    pe.wait_ge(max_taken.sem, maxes[1].done)
                    turns[1].pe(pe)
                    sums_[0].pe(pe)
                    sums_[1].pe(pe)
                    outs[0].pe(pe)
                    outs[1].pe(pe)

                def act(act):
                    norms[0].act(act)
                    norms[1].act(act)
                    queries[0].act(act)
                    queries[1].act(act)
                    if extra is not None:
                        extra.act(act)
                    turns[0].act(act)
                    turns[1].act(act)
                    sums_[0].act(act)
                    sums_[1].act(act)

                def dve(dve):
                    norms[0].dve(dve)
                    norms[1].dve(dve)
                    queries[0].dve(dve)
                    queries[1].dve(dve)
                    if extra is not None:
                        extra.dve(dve)
                    maxes[0].dve(dve, 0, 8)
                    maxes[1].dve(dve, 0, 4)
                    turns[0].dve(dve)
                    maxes[1].dve(dve, 4, 8)
                    turns[1].dve(dve)
                    sums_[0].dve(dve)
                    sums_[1].dve(dve)
                    outs[0].dve(dve)
                    outs[1].dve(dve)

                def pool(pool):
                    norms[0].pool(pool)
                    norms[1].pool(pool)
                    queries[0].pool(pool)
                    queries[1].pool(pool)
                    for u in range(2):
                        if rows[u] is not None:
                            rows[u].pool(pool)
                    turns[0].pool(pool)
                    turns[1].pool(pool)

                def sp(sp):
                    for stage in (queries[0], queries[1], turns[0], turns[1]):
                        stage.sp(sp)
                return Stage(pe=pe, act=act, dve=dve, pool=pool, sp=sp, x_done=[o.done for o in outs])

            def self_inputs(x_waits):
                norms = [norm(u, 2, x_waits[u]) for u in range(2)]
                ro0, ra0, mo0 = rope_step.reserve(8), rope_added.reserve(8), moved.reserve(4)
                pr0 = product.reserve(12)
                k_sets = [parts_of(u, k_rest, k_parts, None) for u in range(2)]
                q_sets = [parts_of(u, q_rest, q_parts, None) for u in range(2)]

                def pe(pe):
                    norms[0].pe(pe)
                    norms[1].pe(pe)
                    for u in range(2):
                        pe.wait_ge(xT_ready.sem, norms[u].done)
                        for m in range(C):
                            for c in range(C):
                                last = nc.tensor.matmul(ps[:, 4 + 2 * u + m, :], w_qkv[:, c, D + m * P:D + (m + 1) * P],
                                                        xT[:, c, u * HALF:(u + 1) * HALF],
                                                        start=(c == 0), stop=(c == C - 1))
                            last.then_inc(product.sem, 1)
                    for k in range(4):
                        for t in (2 * k, 2 * k + 1):
                            for c in range(C):
                                last = nc.tensor.matmul(ps[:, k, (t % 2) * D:(t % 2 + 1) * D],
                                                        xT[:, c, t * P:(t + 1) * P], w_qkv[:, c, 2 * D:3 * D],
                                                        start=(c == 0), stop=(c == C - 1))
                        last.then_inc(product.sem, 1)
                    for u in range(2):
                        for m in range(C):
                            pe.wait_ge(rope_step.sem, ro0 + C * u + m + 1)
                            for c in range(C):
                                last = nc.tensor.matmul(ps[:, 4 + 2 * u + m, :], w_qkv[:, c, m * P:(m + 1) * P],
                                                        xT[:, c, u * HALF:(u + 1) * HALF],
                                                        start=(c == 0), stop=(c == C - 1))
                            last.then_inc(product.sem, 1)

                def rope(dve, n):
                    is_q, u, m = n // 4, n // 2 % 2, n % 2
                    cols = slice(u * HALF, (u + 1) * HALF)
                    dst = (q_rest if is_q else k_rest)[:, m, cols]
                    cos, sin = (rope_q[:, 0, cols], rope_q[:, 1, cols]) if is_q else (cos_k, sin_k)
                    of, turn = ps[:, 4 + 2 * u + m, :], turned[:, n % 2, :]
                    lower, upper = slice(0, P // 2), slice(P // 2, P)
                    dve.wait_ge(product.sem, pr0 + (8 if is_q else 0) + n % 4 + 1)
                    nc.vector.tensor_tensor(dst, of, cos, ALU.mult)
                    if n >= 2:
                        dve.wait_ge(rope_added.sem, ra0 + n - 1)
                    nc.vector.tensor_tensor(turn[lower], of[upper], sin[upper], ALU.mult)
                    nc.vector.tensor_tensor(turn[upper], of[lower], sin[lower], ALU.mult).then_inc(rope_step.sem, 1)

                def rope_add(pool, n):
                    is_q, u, m = n // 4, n // 2 % 2, n % 2
                    dst = (q_rest if is_q else k_rest)[:, m, u * HALF:(u + 1) * HALF]
                    pool.wait_ge(rope_step.sem, ro0 + n + 1)
                    nc.gpsimd.tensor_tensor(dst, dst, turned[:, n % 2, :], ALU.add).then_inc(rope_added.sem, 1)

                def turned_wait(first):
                    return lambda act, m: act.wait_ge(rope_added.sem, ra0 + first + m + 1)

                def dve(dve):
                    norms[0].dve(dve)
                    norms[1].dve(dve)
                    for n in range(4):
                        rope(dve, n)
                    k_sets[0].dve(dve)
                    rope(dve, 4)
                    rope(dve, 5)
                    k_sets[1].dve(dve)
                    rope(dve, 6)
                    rope(dve, 7)
                    q_sets[0].dve(dve)
                    q_sets[1].dve(dve)

                def pool(pool):
                    norms[0].pool(pool)
                    norms[1].pool(pool)
                    nc.gpsimd.memset(neg_max[:], 3e38)
                    for n in range(4):
                        rope_add(pool, n)
                    rope_add(pool, 4)
                    rope_add(pool, 5)
                    k_sets[0].pool(pool)
                    rope_add(pool, 6)
                    rope_add(pool, 7)
                    k_sets[1].pool(pool)
                    q_sets[0].pool(pool)
                    q_sets[1].pool(pool)
                    pool.wait_ge(product.sem, pr0 + 12)
                    nc.gpsimd.memset(sums[:], 0.0)
                    nc.gpsimd.memset(xT[:], 0.0)

                def act(act):
                    norms[0].act(act)
                    norms[1].act(act)
                    k_sets[0].act_high(act, turned_wait(0))
                    k_sets[1].act_high(act, turned_wait(2))
                    k_sets[0].act_middle(act)
                    for k in range(4):
                        act.wait_ge(product.sem, pr0 + 4 + k + 1)
                        nc.scalar.activation(v_self[:, 2 * k:2 * k + 2, :].rearrange("p t d -> p (t d)"), ps[:, k, :],
                                             ACT.Copy).then_inc(moved.sem, 1)
                    q_sets[0].act_high(act, turned_wait(4))
                    k_sets[1].act_middle(act)
                    q_sets[1].act_high(act, turned_wait(6))
                    q_sets[0].act_middle(act)
                    q_sets[1].act_middle(act)

                def sp(sp):
                    for u in range(2):
                        stack_q(sp, u, q_sets[u])
                        sp.wait_ge(q_stacked[u].sem, q_stacked[u].at)
                return Stage(pe=pe, act=act, dve=dve, pool=pool, sp=sp)

            with nc.Block() as block:
                gates_of = gate_weights()
                first = cross_attention(0, 0, w_q, lambda m: vcol("bq", m), w_p, (None, None), bp_row, gates_of)
                inputs = self_inputs(first.x_done)

                @block.tensor
                def _(pe):
                    first.pe(pe)
                    inputs.pe(pe)

                @block.scalar
                def _(act):
                    first.act(act)
                    inputs.act(act)

                @block.vector
                def _(dve):
                    first.dve(dve)
                    inputs.dve(dve)

                @block.gpsimd
                def _(pool):
                    first.pool(pool)
                    inputs.pool(pool)

                @block.sync
                def _(sp):
                    first.sp(sp)
                    inputs.sp(sp)
            clear_signals()

            def biases(j):
                return lambda cols: mask_bias[:, bass.ds(j, 1), cols].rearrange("p o q -> p (o q)")

            def stack_key_tile(sp, j):
                for s, part in enumerate(K_SLOTS):
                    stack_dmas(sp, k_self, lambda i, g: k_parts[:, i, g, bass.ds(j * P, P)], s, part, k_stacked)
                k_stacked.reserve(16 * N_SLOT * C)

            def key_stack(h, rows):
                return k_self[0:rows, h, :]

            with nc.Fori(0, n_tiles) as i:
                j = nc.values_load(tile_list[0:1, bass.ds(i + 1, 1)], min_val=0, max_val=T - 1)
                with nc.Block() as block:
                    maxes = [scores_max(u, key_stack, P, biases(j), True,
                                        lambda pe: pe.wait_ge(k_stacked.sem, 16 * N_SLOT * C)) for u in range(2)]

                    @block.sync
                    def _(sp):
                        stack_key_tile(sp, j)

                    @block.tensor
                    def _(pe):
                        maxes[0].pe(pe, 0, 8)
                        maxes[1].pe(pe, 0, 8)

                    @block.vector
                    def _(dve):
                        for u in range(2):
                            maxes[u].dve(dve, 0, 8)
                            dve.wait_ge(max_taken.sem, maxes[u].done)
                            nc.vector.tensor_tensor(neg_max[:, u], neg_max[:, u], tile_max[:, u], ALU.min)
                clear_signals()
            with nc.Block() as block:
                turns = [turn_max(u, None) for u in range(2)]

                @block.tensor
                def _(pe):
                    turns[0].pe(pe)
                    turns[1].pe(pe)

                @block.scalar
                def _(act):
                    turns[0].act(act)
                    turns[1].act(act)

                @block.vector
                def _(dve):
                    turns[0].dve(dve)
                    turns[1].dve(dve)

                @block.gpsimd
                def _(pool):
                    turns[0].pool(pool)
                    turns[1].pool(pool)

                @block.sync
                def _(sp):
                    turns[0].sp(sp)
                    turns[1].sp(sp)
                    for u in range(2):
                        sp.wait_ge(q_stacked[u].sem, q_stacked[u].at)
            clear_signals()
            with nc.Fori(0, n_tiles) as i:
                j = nc.values_load(tile_list[0:1, bass.ds(i + 1, 1)], min_val=0, max_val=T - 1)
                with nc.Block() as block:
                    pa0 = pool_done.reserve(1)
                    weighs = [weigh(u, key_stack, v_pad[:, 1], biases(j), True, None, lambda pe, g: None)
                              for u in range(2)]

                    @block.sync
                    def _(sp):
                        stack_key_tile(sp, j)

                    @block.gpsimd
                    def _(pool):
                        pad_v(nc.gpsimd, 1, v_self[:, bass.ds(j, 1), :].rearrange("p o d -> p (o d)"))\
                            .then_inc(pool_done.sem, 1)

                    @block.tensor
                    def _(pe):
                        pe.wait_ge(k_stacked.sem, 16 * N_SLOT * C)
                        pe.wait_ge(pool_done.sem, pa0 + 1)
                        weighs[0].pe(pe)
                        weighs[1].pe(pe)

                    @block.scalar
                    def _(act):
                        weighs[0].act(act)
                        weighs[1].act(act)

                    @block.vector
                    def _(dve):
                        weighs[0].dve(dve)
                        weighs[1].dve(dve)
                clear_signals()

            with nc.Block() as block:
                rd0, no0 = recip_done.reserve(2), normed.reserve(2)
                self_out = [project_back(u, xT_tile(u), w_gated[:, 0:C], C,
                                         lambda pe, u=u: pe.wait_ge(normed.sem, no0 + u + 1), None) for u in range(2)]
                second = cross_attention(1, 3, w_cq, lambda m: 0.0, w_gated[:, C:2 * C],
                                         [o.done for o in self_out], None, None)
                norms = [norm(u, 4, second.x_done[u]) for u in range(2)]
                rows = [add_bias(u, norms[u], gb2_row) for u in range(2)]
                F = FF // P
                pr0, mo0 = product.reserve(2 * F), moved.reserve(2 * F)
                mlp_out = [project_back(u, lambda c, k, u=u: hidden[:, u, c, k * P:(k + 1) * P],
                                        w_gated[:, 2 * C:2 * C + F], F,
                                        lambda pe, u=u: pe.wait_ge(moved.sem, mo0 + (u + 1) * F), rows[u].done)
                           for u in range(2)]

                @block.tensor
                def _(pe):
                    self_out[0].pe(pe)
                    self_out[1].pe(pe)
                    second.pe(pe)
                    norms[0].pe(pe)
                    norms[1].pe(pe)
                    for n in range(2 * F):
                        u, f = n // F, n % F
                        if f == 0:
                            pe.wait_ge(xT_ready.sem, norms[u].done)
                        if n >= 4:
                            pe.wait_ge(moved.sem, mo0 + n - 3)
                        for c in range(C):
                            last = nc.tensor.matmul(ps[:, 4 + n % 4, :], w_1[:, c, f * P:(f + 1) * P],
                                                    xT[:, c, u * HALF:(u + 1) * HALF],
                                                    start=(c == 0), stop=(c == C - 1))
                        last.then_inc(product.sem, 1)
                    mlp_out[0].pe(pe)
                    mlp_out[1].pe(pe)

                @block.scalar
                def _(act):
                    second.act(act)
                    norms[0].act(act)
                    norms[1].act(act)
                    for n in range(2 * F):
                        act.wait_ge(product.sem, pr0 + n + 1)
                        nc.scalar.activation(hidden[:, n // F, n % F, :], ps[:, 4 + n % 4, :], ACT.Gelu_apprx_tanh,
                                             bias=vcol("mlp_b1", n % F)).then_inc(moved.sem, 1)

                @block.vector
                def _(dve):
                    for u in range(2):
                        cols = slice(u * HALF, (u + 1) * HALF)
                        nc.vector.reciprocal(sums[:, :, cols], sums[:, :, cols]).then_inc(recip_done.sem, 1)
                        dve.wait_ge(recip_done.sem, rd0 + u + 1)
                        nc.vector.tensor_tensor(xT[:, :, cols], xT[:, :, cols], sums[:, :, cols], ALU.mult)\
                            .then_inc(normed.sem, 1)
                    self_out[0].dve(dve)
                    self_out[1].dve(dve)
                    second.dve(dve)
                    norms[0].dve(dve)
                    norms[1].dve(dve)
                    mlp_out[0].dve(dve)
                    mlp_out[1].dve(dve)

                @block.gpsimd
                def _(pool):
                    pad_v(nc.gpsimd, 0, v_ctx[:, bass.ds(b, 1), 1, :].rearrange("p o d -> p (o d)"))
                    second.pool(pool)
                    norms[0].pool(pool)
                    norms[1].pool(pool)
                    rows[0].pool(pool)
                    rows[1].pool(pool)

                @block.sync
                def _(sp):
                    second.sp(sp)
                    for u in range(2):
                        sp.wait_ge(x_ready.sem, mlp_out[u].done)
                        sp.dma_start(out[b, u * HALF:(u + 1) * HALF, :].rearrange("(t p) d -> p t d", p=P),
                                     x[:, 4 * u:4 * u + 4, :]).then_inc(stored.sem, 16)
                    sp.wait_ge(stored.sem, 32)
            clear_signals()


_NAMES = {
    "x": "x", "ctx": "ctx_1024", "cond": "cond_1024", "ctx_mask": "mask_BxS2_bf1", "mask": "mask_SxS_bk0",
    "Wq": "L0_xcond_Wq", "bq": "L0_xcond_bq", "Wkv": "L0_xcond_Wkv", "bkv": "L0_xcond_bkv", "Wp": "L0_xcond_Wp",
    "bp": "L0_xcond_bp", "Wss_q": "L0_xcond_Wss_q", "bss_q": "L0_xcond_bss_q", "Wss_kv": "L0_xcond_Wss_kv",
    "bss_kv": "L0_xcond_bss_kv", "adaLN_W": "L1_xcond_adaLN_W", "adaLN_b": "L1_xcond_adaLN_b",
    "norm1_w": "L1_xcond_norm1_w", "qkv_W": "L1_xcond_qkv_W", "attn_out_W": "L1_xcond_attn_out_W",
    "normc_w": "L1_xcond_normc_w", "cq_W": "L1_xcond_cq_W", "ck_W": "L1_xcond_ck_W", "cv_W": "L1_xcond_cv_W",
    "co_W": "L1_xcond_co_W", "norm2_w": "L1_xcond_norm2_w", "mlp_W1": "L1_xcond_mlp_W1",
    "mlp_b1": "L1_xcond_mlp_b1", "mlp_W2": "L1_xcond_mlp_W2", "mlp_b2": "L1_xcond_mlp_b2",
}


def by_component(v):
    import numpy as np
    shape = v.shape
    return np.ascontiguousarray(v.reshape(-1, shape[-1] // P, HPC, HD).swapaxes(2, 3)).reshape(shape)


def shape_consts():
    import numpy as np
    t = np.zeros((P, CONST_N), np.float32)

    def put(name, v):
        at, n = CONST_COLS[name]
        t[:v.shape[0], at:at + n] = v
    put("ident", np.eye(P, dtype=np.float32))
    inv_freq = 1.0 / 10000.0 ** (np.arange(0, HD, 2, dtype=np.float32) / HD)
    angle = np.outer(np.arange(S // 2, dtype=np.float32), inv_freq).T
    feature = np.arange(P) // HPC
    put("cos", np.cos(angle)[feature % (HD // 2)].astype(np.float32))
    sign = np.where(feature < HD // 2, 1.0, -1.0)[:, None]
    put("sin", (sign * np.sin(angle)[feature % (HD // 2)]).astype(np.float32))
    i = np.arange(T)
    put("before", (i[:, None] < i[None, :]).astype(np.float32))
    put("iota", np.tile(i.astype(np.float32), (T, 1)))
    put("tile", i[:, None].astype(np.float32))
    return t


def kernel(**inputs):
    import numpy as np
    import concourse.bacc as bacc
    from concourse.bass_utils import run_bass_kernel_spmd

    nc = bacc.Bacc("TRN2", target_bir_lowering=False, num_devices=1, dynamic_dma_scratch_size=1024)
    arrays, aps = {}, {}
    given = {short: np.ascontiguousarray(inputs[name]) for short, name in _NAMES.items()}
    for short in ("Wq", "bq", "cq_W", "ck_W"):
        given[short] = by_component(given[short])
    for short, n in (("Wkv", D), ("bkv", D), ("qkv_W", 2 * D)):
        given[short] = np.concatenate([by_component(given[short][..., :n]), given[short][..., n:]], axis=-1)
    given["shape_consts"] = shape_consts()
    for short, v in given.items():
        arrays[f"in_{short}"] = v
        aps[short] = nc.dram_tensor(f"in_{short}", v.shape, mybir.dt.from_np(v.dtype), kind="ExternalInput").ap()
    out = nc.dram_tensor("out_0", (B, S, D), F32, kind="ExternalOutput").ap()
    build(nc, aps, out)
    r = run_bass_kernel_spmd(nc, [arrays], core_ids=[0])
    return r.results[0]["out_0"]
```

```python
from contextlib import ExitStack

import concourse.bass as bass
from concourse import mybir

F32 = mybir.dt.float32
BF16 = mybir.dt.bfloat16
U8 = mybir.dt.uint8
I32 = mybir.dt.int32
ALU = mybir.AluOpType
ACT = mybir.ActivationFunctionType
AX_X = mybir.AxisListType.X

P = 128
B, S, D = 4, 1024, 256
C = D // P
T = S // P
HALF = 512
NH, HD = 16, 16
LC = 77
FF = 4 * D
EPS = 1e-5
SCALE = HD ** -0.5
MASKED = -1e30
N_SLOT = 6
Q_SLOTS = (0, 0, 1, 0, 2, 1)
K_SLOTS = (0, 1, 0, 2, 0, 1)
BIAS_ROW = N_SLOT * HD
MAX_ROWS = BIAS_ROW + 1
STACK = MAX_ROWS + 3

CONST_COLS = dict(ident=(0, P), cos=(P, S // 2), sin=(P + S // 2, S // 2),
                  before=(P + S, T), iota=(P + S + T, T), tile=(P + S + 2 * T, 1))
CONST_N = P + S + 2 * T + 1

VEC_ROWS = {}
_at = 0
for _name, _n in (("bss_q", 4), ("bss_kv", 4), ("adaLN_b", 18), ("bq", 2), ("bkv", 4), ("norm1_w", 2),
                  ("normc_w", 2), ("norm2_w", 2), ("mlp_b1", 8), ("bp", 2), ("mlp_b2", 2)):
    VEC_ROWS[_name] = (_at, _n)
    _at += _n
N_VEC = _at
N_MOD = 26
NORMS = dict(q0=(0, 2), kv0=(4, 6), n1=(10, 8), nc=(16, 14), n2=(22, 20))
GATES = dict(msa=12, x=18, mlp=24)


class Stage:

    def __init__(self, pe=None, act=None, dve=None, pool=None, sp=None, act_high=None, act_middle=None, dve_low=None,
                 done=None, xhat_done=None, transposed=None, read=None, x_done=None, ready=None):
        self.pe, self.act, self.dve, self.pool, self.sp = pe, act, dve, pool, sp
        self.act_high, self.act_middle, self.dve_low = act_high, act_middle, dve_low
        self.transposed = transposed
        self.done, self.xhat_done, self.read, self.x_done, self.ready = done, xhat_done, read, x_done, ready


class Signal:

    def __init__(self, sem):
        self.sem, self.at = sem, 0

    def reserve(self, n):
        start = self.at
        self.at += n
        return start


def build(nc, a, out):
    ctx = ExitStack()
    with ctx:
        def sb(name, shape, dt=F32):
            return ctx.enter_context(nc.sbuf_tensor(name, shape, dt))

        const = sb("const", [P, CONST_N])

        def constant(name):
            at, n = CONST_COLS[name]
            return const[:, at:at + n]

        ident, cos_k, sin_k = constant("ident"), constant("cos"), constant("sin")
        ident_bf = sb("ident_bf", [P, P], BF16)
        rope_q = sb("rope_q", [P, 2, S])
        w_q = sb("w_q", [P, C, D])
        w_p = sb("w_p", [P, C, D])
        w_qkv = sb("w_qkv", [P, C, 3 * D])
        w_out = sb("w_out", [P, C, D])
        w_cq = sb("w_cq", [P, C, D])
        w_co = sb("w_co", [P, C, D])
        w_1 = sb("w_1", [P, C, FF])
        w_2 = sb("w_2", [P, FF // P, D])
        w_gated = sb("w_gated", [P, 2 * C + FF // P, D])
        vec = sb("vec", [P, N_VEC])
        affine = sb("affine", [P, B, 5, 2, C])
        gates = sb("gates", [P, B, 4, C])
        affine_b = sb("affine_b", [P, 5, 2, C])
        gates_b = sb("gates_b", [P, 4, C])
        bp_row = sb("bp_row", [P, D])
        gb2_row = sb("gb2_row", [P, D])
        spread = sb("spread", [P, 2, P])
        x = sb("x", [P, T, D])
        xT = sb("xT", [P, C, S])
        xhat = sb("xhat", [P, T, D])
        arena_a = sb("arena_a", [P, 8192])
        arena_r = sb("arena_r", [P, 10240])
        k_parts = sb("k_parts", [P, 3, C, S], BF16)
        v_self = sb("v_self", [P, T, D])
        v_ctx = sb("v_ctx", [P, B, 2, D])
        v_pad = sb("v_pad", [P, 2, NH, 2 * HD])
        ones_pad = sb("ones_pad", [P, 2, 2 * HD])
        k_ctx = sb("k_ctx", [P, NH, 2 * P], BF16)
        k_self = sb("k_self", [P, NH, P], BF16)
        mask_bias = sb("mask_bias", [P, T, S], BF16)
        ones_row = sb("ones_row", [NH, S], BF16)
        tile_list = sb("tile_list", [1, 1 + T], I32)
        stats = sb("stats", [P, T, 6])
        mean_var = sb("mean_var", [P, T, 2])
        var_eps = sb("var_eps", [P, T])
        rstd = sb("rstd", [P, T])
        minus_half = sb("minus_half", [P, T])
        neg_max = sb("neg_max", [P, 2, NH, T // 2])
        tile_max = sb("tile_max", [P, 2, NH, T // 2])
        max_rest = spread
        max_parts = sb("max_parts", [P, 2, 3, P], BF16)

        q_stack = arena_a[:, :].bitcast(BF16).rearrange("p (h s) -> p h s", h=NH)
        q_stack = arena_a[:, :].bitcast(BF16).rearrange("p (u h s) -> p u h s", u=2, h=NH)
        hidden = arena_a[:, :].rearrange("p (u f s) -> p u f s", u=2, f=FF // P)
        probs = arena_r[:, 0:4096].rearrange("p (n k s) -> p n k s", n=4, k=2)
        k_rest = arena_r[:, 0:C * S].rearrange("p (c s) -> p c s", c=C)
        q_rest = arena_r[:, 4096:6144].rearrange("p (c s) -> p c s", c=C)
        q_parts = arena_r[:, 6144:9216].bitcast(BF16).rearrange("p (i c s) -> p i c s", i=3, c=C)
        inverse = arena_r[:, 9216:10240].rearrange("p (g s) -> p g s", g=C)
        turned = inverse
        sums = xhat[:].rearrange("p t d -> p (t d)").rearrange("p (c s) -> p c s", c=C)
        k_ctx_dram = nc.dram_tensor("k_ctx_stacks", (STACK, NH, B * 2 * P), BF16, kind="Internal").ap()

        ps = ctx.enter_context(nc.psum_tensor("ps", [P, 8, HALF], F32))

        signals = []

        def signal(name):
            s = Signal(ctx.enter_context(nc.semaphore(name)))
            signals.append(s)
            return s

        loads = signal("loads")
        late_loads = signal("late_loads")
        x_loaded = [signal("x_loaded_0"), signal("x_loaded_1")]
        stored = signal("stored")
        k_stacked = signal("k_stacked")
        q_stacked = [signal("q_stacked_0"), signal("q_stacked_1")]
        pe_done = signal("pe_done")
        act_done = signal("act_done")
        dve_done = signal("dve_done")
        pool_done = signal("pool_done")
        stats_ready = signal("stats_ready")
        var_ready = signal("var_ready")
        rstd_ready = signal("rstd_ready")
        xhat_ready = signal("xhat_ready")
        xT_transposed = signal("xT_transposed")
        xT_ready = signal("xT_ready")
        xT_dve = signal("xT_dve")
        biased = signal("biased")
        x_ready = signal("x_ready")
        gate_spread = signal("gate_spread")
        gate_rows = signal("gate_rows")
        gated = signal("gated")
        product = signal("product")
        out_product = signal("out_product")
        moved = signal("moved")
        high_ready = signal("high_ready")
        rest_ready = signal("rest_ready")
        middle_ready = signal("middle_ready")
        low_ready = signal("low_ready")
        k_low_ready = signal("k_low_ready")
        rope_step = signal("rope_step")
        rope_added = signal("rope_added")
        scores_ready = signal("scores_ready")
        max_taken = signal("max_taken")
        max_turned = signal("max_turned")
        max_high = signal("max_high")
        max_rest1 = signal("max_rest1")
        max_middle = signal("max_middle")
        max_low = signal("max_low")
        keyed_ready = signal("keyed_ready")
        exp_done = signal("exp_done")
        pv_done = signal("pv_done")
        recip_done = signal("recip_done")
        normed = signal("normed")
        o_read = signal("o_read")

        def clear_signals():
            for s in signals:
                nc.sync.sem_clear(s.sem)
                s.at = 0
            nc.all_engine_barrier()


        def vcol(name, i=0):
            at = VEC_ROWS[name][0] + i
            return vec[:, at:at + 1]

        def pad_v(engine, slot, of):
            src = of.rearrange("p (g two d) -> p g two d", two=2, d=HD)
            dst = v_pad[:, slot].rearrange("p (g two) (z d) -> p g two z d", two=2, z=2)
            engine.tensor_copy(dst[:, :, 0, 0, :], src[:, :, 0, :])
            return engine.tensor_copy(dst[:, :, 1, 1, :], src[:, :, 1, :])

        def context_norm(x_tiles, n_tiles, norm_scale, norm_shift, dst, n_groups, group_cols):
            per_group = n_tiles // n_groups
            st0, va0, rs0 = stats_ready.reserve(2), var_ready.reserve(1), rstd_ready.reserve(1)
            xh0, xt0 = xhat_ready.reserve(n_tiles), xT_transposed.reserve(2 * n_groups)
            xa0, xd0 = xT_ready.reserve(n_groups), xT_dve.reserve(n_groups)
            with nc.Block() as block:
                @block.vector
                def _(dve):
                    for t in range(n_tiles):
                        last = nc.vector.bn_stats(stats[:, t, :], x_tiles(t))
                    last.then_inc(stats_ready.sem, 1)
                    dve.wait_ge(stats_ready.sem, st0 + 1)
                    for t in range(n_tiles):
                        last = nc.vector.bn_aggr(mean_var[:, t, :], stats[:, t, :])
                    last.then_inc(stats_ready.sem, 1)
                    dve.wait_ge(stats_ready.sem, st0 + 2)
                    nc.vector.tensor_scalar(var_eps[:, 0:n_tiles], mean_var[:, 0:n_tiles, 1], EPS, None,
                                            ALU.add).then_inc(var_ready.sem, 1)
                    dve.wait_ge(rstd_ready.sem, rs0 + 1)
                    for t in range(n_tiles):
                        nc.vector.tensor_scalar(xhat[:, t, :], x_tiles(t), mean_var[:, t, 0:1],
                                                rstd[:, t:t + 1], ALU.subtract, ALU.mult)\
                            .then_inc(xhat_ready.sem, 1)
                    for g in range(n_groups):
                        dve.wait_ge(xT_transposed.sem, xt0 + 2 * g + 2)
                        nc.vector.tensor_scalar(dst[:, 1, g * group_cols:(g + 1) * group_cols],
                                                ps[:, 2 * g + 1, 0:group_cols], norm_scale(1, g),
                                                norm_shift(1, g), ALU.mult, ALU.add)\
                            .then_inc(xT_dve.sem, 1)

                @block.gpsimd
                def _(pool):
                    pool.wait_ge(var_ready.sem, va0 + 1)
                    nc.gpsimd.tensor_tensor(rstd[:, 0:n_tiles], var_eps[:, 0:n_tiles],
                                            minus_half[:, 0:n_tiles], ALU.pow).then_inc(rstd_ready.sem, 1)

                @block.tensor
                def _(pe):
                    for g in range(n_groups):
                        for c in range(C):
                            for t in range(per_group):
                                if c == 0:
                                    pe.wait_ge(xhat_ready.sem, xh0 + g * per_group + t + 1)
                                last = nc.tensor.transpose(ps[:, 2 * g + c, t * P:(t + 1) * P],
                                                           xhat[:, g * per_group + t, c * P:(c + 1) * P],
                                                           ident)
                            last.then_inc(xT_transposed.sem, 1)

                @block.scalar
                def _(act):
                    for g in range(n_groups):
                        act.wait_ge(xT_transposed.sem, xt0 + 2 * g + 1)
                        nc.scalar.activation(dst[:, 0, g * group_cols:(g + 1) * group_cols],
                                             ps[:, 2 * g, 0:group_cols], ACT.Identity,
                                             bias=norm_shift(0, g), scale=norm_scale(0, g))\
                            .then_inc(xT_ready.sem, 1)

        def stack_dmas(sp, stack, parts, slot, part, signal):
            for m in range(C):
                row = slot * HD + m * HD // 2
                sp.dma_start(stack[row:row + HD // 2], parts(part, m))\
                    .then_inc(signal.sem, 16)


        def norm(half, i, x_wait):
            st0, va0, rs0 = stats_ready.reserve(2), var_ready.reserve(1), rstd_ready.reserve(1)
            xh0, xt0, xr0 = xhat_ready.reserve(4), xT_transposed.reserve(1), xT_ready.reserve(2)
            tiles = range(4 * half, 4 * half + 4)
            four = slice(4 * half, 4 * half + 4)

            def dve(dve):
                if x_wait is not None:
                    dve.wait_ge(x_ready.sem, x_wait)
                for t in tiles:
                    last = nc.vector.bn_stats(stats[:, t, :], x[:, t, :])
                last.then_inc(stats_ready.sem, 1)
                dve.wait_ge(stats_ready.sem, st0 + 1)
                for t in tiles:
                    last = nc.vector.bn_aggr(mean_var[:, t, :], stats[:, t, :])
                last.then_inc(stats_ready.sem, 1)
                dve.wait_ge(stats_ready.sem, st0 + 2)
                nc.vector.tensor_scalar(var_eps[:, four], mean_var[:, four, 1], EPS, None, ALU.add)\
                    .then_inc(var_ready.sem, 1)
                dve.wait_ge(rstd_ready.sem, rs0 + 1)
                for t in tiles:
                    nc.vector.tensor_scalar(xhat[:, t, :], x[:, t, :], mean_var[:, t, 0:1], rstd[:, t:t + 1],
                                            ALU.subtract, ALU.mult).then_inc(xhat_ready.sem, 1)

            def pool(pool):
                pool.wait_ge(var_ready.sem, va0 + 1)
                nc.gpsimd.tensor_tensor(rstd[:, four], var_eps[:, four], minus_half[:, four], ALU.pow)\
                    .then_inc(rstd_ready.sem, 1)

            def pe(pe):
                for k, t in enumerate(tiles):
                    pe.wait_ge(xhat_ready.sem, xh0 + k + 1)
                    for c in range(C):
                        last = nc.tensor.transpose(ps[:, 2 * half + c, k * P:(k + 1) * P],
                                                   xhat[:, t, c * P:(c + 1) * P], ident)
                last.then_inc(xT_transposed.sem, 1)

            def act(act):
                act.wait_ge(xT_transposed.sem, xt0 + 1)
                for c in range(C):
                    nc.scalar.activation(xT[:, c, half * HALF:(half + 1) * HALF], ps[:, 2 * half + c, :],
                                         ACT.Identity, bias=affine_b[:, i, 1, c:c + 1],
                                         scale=affine_b[:, i, 0, c:c + 1]).then_inc(xT_ready.sem, 1)
            return Stage(dve=dve, pool=pool, pe=pe, act=act, done=xr0 + 2, xhat_done=xh0 + 4,
                         transposed=xt0 + 1)

        def add_bias(half, after, row):
            bi0 = biased.reserve(1)

            def pool(pool):
                pool.wait_ge(xhat_ready.sem, after.xhat_done)
                nc.gpsimd.tensor_tensor(x[:, 4 * half:4 * half + 4, :], x[:, 4 * half:4 * half + 4, :],
                                        row[:].rearrange("p (o d) -> p o d", o=1).to_broadcast([P, 4, D]), ALU.add)\
                    .then_inc(biased.sem, 1)
            return Stage(pool=pool, done=bi0 + 1)

        def parts_of(half, rest, parts, source):
            hi0, re0, mi0 = (s.reserve(C) for s in (high_ready, rest_ready, middle_ready))
            low = k_low_ready if parts is k_parts else low_ready
            lo0 = low.reserve(C)
            cols = slice(half * HALF, (half + 1) * HALF)

            def act_high(act, wait):
                for m in range(C):
                    wait(act, m)
                    bank, bias = source(m) if source else (rest[:, m, cols], 0.0)
                    nc.scalar.activation(parts[:, 0, m, cols], bank, ACT.Identity, bias=bias)\
                        .then_inc(high_ready.sem, 1)

            def act_middle(act):
                for m in range(C):
                    act.wait_ge(rest_ready.sem, re0 + m + 1)
                    nc.scalar.activation(parts[:, 1, m, cols], rest[:, m, cols], ACT.Copy)\
                        .then_inc(middle_ready.sem, 1)

            def dve(dve):
                for m in range(C):
                    dve.wait_ge(high_ready.sem, hi0 + m + 1)
                    if source:
                        bank, bias = source(m)
                        nc.vector.scalar_tensor_tensor(rest[:, m, cols], bank, bias, parts[:, 0, m, cols],
                                                       ALU.add, ALU.subtract).then_inc(rest_ready.sem, 1)
                    else:
                        nc.vector.tensor_tensor(rest[:, m, cols], rest[:, m, cols], parts[:, 0, m, cols],
                                                ALU.subtract).then_inc(rest_ready.sem, 1)

            def pool(pool):
                for m in range(C):
                    pool.wait_ge(middle_ready.sem, mi0 + m + 1)
                    nc.gpsimd.tensor_tensor(parts[:, 2, m, cols], rest[:, m, cols], parts[:, 1, m, cols],
                                            ALU.subtract).then_inc(k_low_ready.sem, 1)

            def dve_low(dve):
                for m in range(C):
                    dve.wait_ge(middle_ready.sem, mi0 + m + 1)
                    nc.vector.tensor_tensor(parts[:, 2, m, cols], rest[:, m, cols], parts[:, 1, m, cols],
                                            ALU.subtract).then_inc(low_ready.sem, 1)
            ready = ((high_ready.sem, hi0 + C), (middle_ready.sem, mi0 + C), (low.sem, lo0 + C))
            return Stage(act_high=act_high, act_middle=act_middle, dve=dve, dve_low=dve_low, pool=pool,
                         ready=ready)

        def stack_q(sp, half, parts):
            cols = slice(half * HALF, (half + 1) * HALF)
            for part, ready in enumerate(parts.ready):
                sp.wait_ge(*ready)
                for s in range(N_SLOT):
                    if Q_SLOTS[s] == part:
                        stack_dmas(sp, q_stack[:, half], lambda i, g: q_parts[:, i, g, cols], s, part,
                                   q_stacked[half])

        def query(half, w, bias, after):
            pr0 = product.reserve(C)
            sk0 = q_stacked[half].reserve(16 * N_SLOT * C)
            parts = parts_of(half, q_rest, q_parts, lambda m: (ps[:, 4 + 2 * half + m, :], bias(m)))

            def pe(pe):
                pe.wait_ge(xT_ready.sem, after.done)
                for m in range(C):
                    for c in range(C):
                        last = nc.tensor.matmul(ps[:, 4 + 2 * half + m, :], w[:, c, m * P:(m + 1) * P],
                                                xT[:, c, half * HALF:(half + 1) * HALF],
                                                start=(c == 0), stop=(c == C - 1))
                    last.then_inc(product.sem, 1)

            def act_high(act):
                parts.act_high(act, lambda act, m: act.wait_ge(product.sem, pr0 + m + 1))
            return Stage(pe=pe, act_high=act_high, act_middle=parts.act_middle, dve=parts.dve, dve_low=parts.dve_low,
                                   sp=lambda sp: stack_q(sp, half, parts), done=sk0 + 16 * N_SLOT * C)

        def scores_max(half, k_of, keys, mask_tile, running, free):
            n = 8
            sc0, mt0 = scores_ready.reserve(n), max_taken.reserve(n)
            view = ps[:].rearrange("p (u b) (h k) -> p u (b h) k", u=4, h=4)
            dst = tile_max if running else neg_max

            def pe(pe, first, end):
                if first == 0:
                    free(pe)
                for k in range(first, end):
                    t = 4 * half + k // 2
                    if mt0 + k >= 2:
                        pe.wait_ge(max_taken.sem, mt0 + k - 1)
                    for i in range(8):
                        h = k % 2 * 8 + i
                        o = view[:, k % 2, i, 0:keys]
                        if mask_tile is not None:
                            nc.tensor.matmul(o, mask_tile(slice(t * P, (t + 1) * P)), ident_bf[:],
                                             start=True, stop=False)
                        last = nc.tensor.matmul(o, q_stack[0:BIAS_ROW + 1, half, h, k // 2 * P:(k // 2 + 1) * P],
                                                k_of(h, BIAS_ROW + 1), start=mask_tile is None, stop=True)
                    last.then_inc(scores_ready.sem, 1)

            def dve(dve, first, end):
                for k in range(first, end):
                    dve.wait_ge(scores_ready.sem, sc0 + k + 1)
                    nc.vector.tensor_reduce(dst[:, half, k % 2 * 8:k % 2 * 8 + 8, k // 2],
                                            view[:, k % 2, :, 0:keys], AX_X, ALU.max, negate=True)\
                        .then_inc(max_taken.sem, 1)
            return Stage(pe=pe, dve=dve, done=mt0 + n)

        def turn_max(half, taken):
            tu0, hi0 = max_turned.reserve(1), max_high.reserve(1)
            re0, mi0, lo0 = max_rest1.reserve(1), max_middle.reserve(1), max_low.reserve(1)
            sk0 = q_stacked[half].reserve(48)
            rows = NH * T // 2
            bank = ps[0:rows, 4 + 2 * half, 0:P]

            def pe(pe):
                if taken is not None:
                    pe.wait_ge(max_taken.sem, taken)
                nc.tensor.transpose(bank, neg_max[:, half].rearrange("p h t -> p (h t)"), ident)\
                    .then_inc(max_turned.sem, 1)

            def act(act):
                act.wait_ge(max_turned.sem, tu0 + 1)
                nc.scalar.activation(max_parts[0:rows, half, 0, :], bank, ACT.Copy).then_inc(max_high.sem, 1)
                act.wait_ge(max_rest1.sem, re0 + 1)
                nc.scalar.activation(max_parts[0:rows, half, 1, :], max_rest[0:rows, half, :], ACT.Copy)\
                    .then_inc(max_middle.sem, 1)

            def dve(dve):
                dve.wait_ge(max_high.sem, hi0 + 1)
                nc.vector.tensor_tensor(max_rest[0:rows, half, :], bank, max_parts[0:rows, half, 0, :],
                                        ALU.subtract).then_inc(max_rest1.sem, 1)

            def pool(pool):
                pool.wait_ge(max_middle.sem, mi0 + 1)
                nc.gpsimd.tensor_tensor(max_parts[0:rows, half, 2, :], max_rest[0:rows, half, :],
                                        max_parts[0:rows, half, 1, :], ALU.subtract).then_inc(max_low.sem, 1)

            def sp(sp):
                for i, ready in enumerate(((max_high.sem, hi0 + 1), (max_middle.sem, mi0 + 1),
                                           (max_low.sem, lo0 + 1))):
                    sp.wait_ge(*ready)
                    row = q_stack[MAX_ROWS + i:MAX_ROWS + i + 1, half]
                    sp.dma_start(row.rearrange("o h (t q) -> o (h t) q", q=P), max_parts[0:rows, half, i, :])\
                        .then_inc(q_stacked[half].sem, 16)
            return Stage(pe=pe, act=act, dve=dve, pool=pool, sp=sp, read=re0 + 1, done=sk0 + 48)

        def weigh(half, k_of, v, mask_tile, add_to, q_ready, free):
            ke0, ex0, pv0 = keyed_ready.reserve(NH // 2), exp_done.reserve(NH // 2), pv_done.reserve(4)
            rd0, no0 = recip_done.reserve(2 * C if add_to == "last" else C), normed.reserve(C)
            or0 = o_read.reserve(C if add_to == "last" else 0)
            read, read0 = (o_read, or0) if add_to == "last" else (normed, no0)
            cols = slice(half * HALF, (half + 1) * HALF)

            def pe(pe):
                def products(quad):
                    g, sub = quad // 2, quad % 2
                    pe.wait_ge(exp_done.sem, ex0 + 2 * quad + 2)
                    if sub == 0:
                        free(pe, g)
                        if half == 1:
                            pe.wait_ge(read.sem, read0 - C + g + 1)
                    for what in range(2):
                        for j in range(4):
                            n = 4 * quad + j
                            w = v[:, 8 * g + 2 * j + sub, :] if what == 0 else ones_pad[:, sub, :]
                            last = nc.tensor.matmul(ps[32 * j:32 * j + 32, 4 + 2 * g + what, :], w,
                                                    probs[:, n // 2 % 4, n % 2, :],
                                                    start=(sub == 0), stop=(sub == 1), skip_group_check=True)
                    last.then_inc(pv_done.sem, 1)

                if q_ready is not None:
                    pe.wait_ge(q_stacked[half].sem, q_ready)
                for n in range(NH):
                    quad, j = n // 4, n % 4
                    h = 8 * (quad // 2) + 2 * j + quad % 2
                    if n % 2 == 0 and n >= 4:
                        pe.wait_ge(exp_done.sem, ex0 + n // 2 - 1)
                    o = ps[:, n % 4, :]
                    if mask_tile is not None:
                        nc.tensor.matmul(o, ident_bf[:], mask_tile(cols), start=True, stop=False)
                    last = nc.tensor.matmul(o, k_of(h, STACK), q_stack[0:STACK, half, h, :],
                                            start=mask_tile is None, stop=True)
                    if n % 2 == 1:
                        last.then_inc(keyed_ready.sem, 1)
                    if j == 3 and quad >= 1:
                        products(quad - 1)
                products(3)

            def act(act):
                for p in range(NH // 2):
                    act.wait_ge(keyed_ready.sem, ke0 + p + 1)
                    if 8 * half + p >= 4:
                        act.wait_ge(pv_done.sem, pv0 + p // 2 - 1)
                    nc.scalar.activation(probs[:, p % 4].rearrange("p k s -> p (k s)"),
                                         ps[:, 2 * (p % 2):2 * (p % 2) + 2, :].rearrange("p a b -> p (a b)"),
                                         ACT.Exp, scale=SCALE).then_inc(exp_done.sem, 1)

            def dve(dve):
                for g in range(C):
                    dve.wait_ge(pv_done.sem, pv0 + 2 * g + 2)
                    o, total = ps[:, 4 + 2 * g, :], ps[:, 5 + 2 * g, :]
                    if add_to == "last":
                        nc.vector.tensor_tensor(sums[:, g, cols], sums[:, g, cols], total, ALU.add)\
                            .then_inc(recip_done.sem, 1)
                        nc.vector.tensor_tensor(xT[:, g, cols], xT[:, g, cols], o, ALU.add)\
                            .then_inc(o_read.sem, 1)
                        dve.wait_ge(recip_done.sem, rd0 + 2 * g + 1)
                        nc.vector.reciprocal(sums[:, g, cols], sums[:, g, cols]).then_inc(recip_done.sem, 1)
                        dve.wait_ge(o_read.sem, or0 + g + 1)
                        dve.wait_ge(recip_done.sem, rd0 + 2 * g + 2)
                        nc.vector.tensor_tensor(xT[:, g, cols], xT[:, g, cols], sums[:, g, cols], ALU.mult)\
                            .then_inc(normed.sem, 1)
                    elif add_to:
                        nc.vector.tensor_tensor(sums[:, g, cols], sums[:, g, cols], total, ALU.add)\
                            .then_inc(recip_done.sem, 1)
                        nc.vector.tensor_tensor(xT[:, g, cols], xT[:, g, cols], o, ALU.add)\
                            .then_inc(normed.sem, 1)
                    else:
                        nc.vector.reciprocal(inverse[:, g, :], total).then_inc(recip_done.sem, 1)
                        dve.wait_ge(recip_done.sem, rd0 + g + 1)
                        nc.vector.tensor_tensor(xT[:, g, cols], o, inverse[:, g, :], ALU.mult)\
                            .then_inc(normed.sem, 1)
            return Stage(pe=pe, act=act, dve=dve, done=no0 + C)

        def project_back(half, act_in, weights, n_chunks, wait_input, wait_bias):
            pr0, xr0 = out_product.reserve(2), x_ready.reserve(2)

            def pe(pe):
                wait_input(pe)
                for k in range(2):
                    for r in range(2):
                        for c in range(n_chunks):
                            last = nc.tensor.matmul(ps[:, 2 * half + k, r * D:(r + 1) * D], act_in(c, 2 * k + r),
                                                    weights[:, c, :], start=(c == 0), stop=(c == n_chunks - 1))
                    last.then_inc(out_product.sem, 1)

            def dve(dve):
                if wait_bias is not None:
                    dve.wait_ge(biased.sem, wait_bias)
                for k in range(2):
                    dve.wait_ge(out_product.sem, pr0 + k + 1)
                    two = x[:, 4 * half + 2 * k:4 * half + 2 * k + 2, :].rearrange("p t d -> p (t d)")
                    nc.vector.tensor_tensor(two, two, ps[:, 2 * half + k, :], ALU.add).then_inc(x_ready.sem, 1)
            return Stage(pe=pe, dve=dve, done=xr0 + 2)

        def xT_tile(half):
            return lambda c, k: xT[:, c, half * HALF + k * P:half * HALF + (k + 1) * P]

        def load_x(sp, batch, half):
            sp.dma_start(x[:, 4 * half:4 * half + 4, :],
                         a["x"][batch, half * HALF:(half + 1) * HALF, :].rearrange("(t p) d -> p t d", p=P))\
                .then_inc(x_loaded[half].sem, 16)

        ada_w = arena_a[:, 0:C * 18 * P].rearrange("p (c n) -> p c n", c=C)
        ss_q = arena_a[:, 4608:5632].rearrange("p (c n) -> p c n", c=C)
        ss_kv = arena_a[:, 5632:6656].rearrange("p (c n) -> p c n", c=C)
        w_kv = arena_r[:, 0:1024].rearrange("p (c n) -> p c n", c=C)
        w_ck = arena_r[:, 1024:1536].rearrange("p (c n) -> p c n", c=C)
        w_cv = arena_r[:, 1536:2048].rearrange("p (c n) -> p c n", c=C)
        cT_norm = arena_r[:, 2048:3072].rearrange("p (c n) -> p c n", c=C)
        cT_raw = arena_r[:, 3072:4096].rearrange("p (c n) -> p c n", c=C)
        kc = arena_r[:, 4096:6144].rearrange("p (c b l k) -> p c b l k", c=C, b=B, l=2)
        kc_flat = arena_r[:, 4096:6144].rearrange("p (c n) -> p c n", c=C)
        kc_parts = k_parts
        mask_raw = arena_r[:, 6144:8192].bitcast(U8).rearrange("p (t k) -> p t k", t=T)
        k_ctx_all = arena_a[:, :].bitcast(BF16).rearrange("p (h k) -> p h k", h=NH)
        ctx_tok = x[:, 0:B, :]
        temps = arena_r[:, 8192:10240].rearrange("p (c s) -> p c s", c=C)
        vec_rows = temps[0:N_VEC, 0, 0:P]
        cond = temps[0:B, 0, 128:128 + D]
        ctx_mask = temps[:, 1, 0:B * LC // 4].bitcast(U8).rearrange("p (b k) -> p b k", b=B)
        condT = temps[:, 0, 512:512 + C * B].rearrange("p (c b) -> p c b", c=C)
        siluT = temps[:, 0, 544:544 + C * B].rearrange("p (c b) -> p c b", c=C)
        expT = temps[:, 0, 576:576 + C * B].rearrange("p (c b) -> p c b", c=C)
        mod = temps[:, 0, 640:640 + N_MOD * B].rearrange("p (j b) -> p j b", j=N_MOD)
        bv_row = temps[:, 0, 768:768 + D]
        any_ctx = temps[:, 1, 128:128 + B]
        key_bias = temps[:, 1, 256:768].bitcast(BF16).rearrange("p (b l k) -> p b l k", b=B, l=2)
        any_q = temps[:, 1, 800:800 + T]
        none_q = temps[:, 1, 816:816 + T]
        keep = temps[:, 1, 832:832 + T]
        seen = temps[:, 1, 848:848 + T * T].rearrange("p (t k) -> p t k", t=T)
        list_tmp = temps[:, 1, 920:920 + 24]
        bias_nat = xT[:].rearrange("p c s -> p (c s)").bitcast(BF16).rearrange("p (t k) -> p t k", t=4)

        with nc.Block() as block:
            @block.sync
            def _(sp):
                def load(dst, src, signal=loads):
                    sp.dma_start(dst[:], src).then_inc(signal.sem, 16)
                    signal.at += 16
                load(const[:], a["shape_consts"])
                for name, (at, n) in VEC_ROWS.items():
                    load(vec_rows[at:at + n, :], a[name].rearrange("(j p) -> j p", p=P))
                load(cond, a["cond"])
                load(ctx_mask, a["ctx_mask"].rearrange("(o b) k -> o b k", o=1).to_broadcast([P, B, LC]))
                for dst, name in ((ss_q, "Wss_q"), (ss_kv, "Wss_kv"), (ada_w, "adaLN_W"), (w_kv, "Wkv"),
                                  (w_ck, "ck_W"), (w_cv, "cv_W")):
                    load(dst, a[name].rearrange("(c p) n -> p c n", p=P))
                sp.wait_ge(pool_done.sem, 1)
                load(ctx_tok[0:LC], a["ctx"].rearrange("b k d -> k b d"))
                load(mask_raw, a["mask"].rearrange("(t p) k -> p t k", p=P), late_loads)
                for dst, name in ((w_q, "Wq"), (w_p, "Wp"), (w_qkv, "qkv_W"), (w_out, "attn_out_W"), (w_cq, "cq_W"),
                                  (w_co, "co_W"), (w_1, "mlp_W1"), (w_2, "mlp_W2")):
                    load(dst, a[name].rearrange("(c p) n -> p c n", p=P), late_loads)
                sp.wait_ge(loads.sem, loads.at)

            @block.gpsimd
            def _(pool):
                nc.gpsimd.memset(ctx_tok[:], 0.0).then_inc(pool_done.sem, 1)
                nc.gpsimd.memset(minus_half[:], -0.5)
                nc.gpsimd.memset(ones_row[:], 1.0)
                nc.gpsimd.memset(v_pad[:], 0.0)
                nc.gpsimd.memset(ones_pad[:], 0.0).then_inc(pool_done.sem, 1)
                pool.wait_ge(pool_done.sem, 2)
                nc.gpsimd.memset(ones_pad[:, 0, 0:HD], 1.0)
                nc.gpsimd.memset(ones_pad[:, 1, HD:2 * HD], 1.0)
                pool_done.at = 2

            @block.vector
            def _(dve):
                nc.vector.memset(key_bias[0:1], MASKED)
                nc.vector.memset(k_self[BIAS_ROW:P], 1.0).then_inc(dve_done.sem, 1)
                dve.wait_ge(dve_done.sem, 1)
                nc.vector.memset(key_bias[0:1, :, 0, 0:LC], 0.0)
                nc.vector.memset(k_self[BIAS_ROW:BIAS_ROW + 1], 0.0)

        with nc.Block() as block:
            @block.tensor
            def _(pe):
                nc.tensor.transpose(ps[:, 0, 0:N_VEC], vec_rows, ident[0:N_VEC, 0:N_VEC])
                for c in range(C):
                    last = nc.tensor.transpose(ps[:, 1, c * B:(c + 1) * B], cond[:, c * P:(c + 1) * P],
                                               ident[0:B, 0:B])
                last.then_inc(pe_done.sem, 1)

            @block.scalar
            def _(act):
                act.wait_ge(dve_done.sem, 2)
                nc.scalar.activation(expT, condT, ACT.Exp, scale=-1.0).then_inc(act_done.sem, 1)

            @block.vector
            def _(dve):
                nc.vector.tensor_copy(ident_bf[:], ident)
                dve.wait_ge(pe_done.sem, 1)
                nc.vector.tensor_copy(vec[:], ps[:, 0, 0:N_VEC])
                nc.vector.tensor_copy(condT, ps[:, 1, 0:C * B].rearrange("p (c b) -> p c b", c=C))\
                    .then_inc(dve_done.sem, 1)
                dve.wait_ge(act_done.sem, 1)
                nc.vector.tensor_scalar(expT, expT, 1.0, None, ALU.add).then_inc(dve_done.sem, 1)
                dve.wait_ge(dve_done.sem, 3)
                nc.vector.reciprocal(siluT, expT).then_inc(dve_done.sem, 1)
                dve.wait_ge(dve_done.sem, 4)
                nc.vector.tensor_tensor(siluT, siluT, condT, ALU.mult)
                nc.vector.tensor_reduce(any_ctx, ctx_mask, AX_X, ALU.max).then_inc(dve_done.sem, 1)
                dve.wait_ge(dve_done.sem, 5)
                nc.vector.tensor_scalar(list_tmp[0:1, 0:B], any_ctx[0:1, :], -MASKED, None, ALU.mult)\
                    .then_inc(dve_done.sem, 1)
                dve.wait_ge(dve_done.sem, 6)
                for b in range(B):
                    last = nc.vector.tensor_scalar(key_bias[0:1, b, 1, 0:LC], ctx_mask[0:1, b, :], 1.0,
                                                   list_tmp[0:1, b:b + 1], ALU.subtract, ALU.mult)
                last.then_inc(dve_done.sem, 1)
                dve_done.at = 7
            act_done.at = pe_done.at = 1

        with nc.Block() as block:
            @block.tensor
            def _(pe):
                for j in range(N_MOD):
                    w, at, c_in = (ss_q, j, siluT) if j < 4 else (ss_kv, j - 4, siluT) if j < 8 else (ada_w, j - 8, condT)
                    for c in range(C):
                        last = nc.tensor.matmul(ps[:, 0, j * B:(j + 1) * B], w[:, c, at * P:(at + 1) * P],
                                                c_in[:, c, :], start=(c == 0), stop=(c == C - 1))
                last.then_inc(pe_done.sem, 1)
                for c in range(C):
                    for k, name in enumerate(("bp", "bkv")):
                        pe.wait_ge(act_done.sem, 1 + 2 * c + k + 1)
                        last = nc.tensor.matmul(ps[:, 1 + k, c * P:(c + 1) * P], spread[:, k, :], ident,
                                                start=True, stop=True)
                    last.then_inc(pe_done.sem, 1)

            @block.scalar
            def _(act):
                for c in range(C):
                    if c:
                        act.wait_ge(pe_done.sem, 3)
                    for k, col in enumerate((vcol("bp", c), vcol("bkv", 2 + c))):
                        nc.scalar.activation(spread[:, k, :], col.to_broadcast([P, P]), ACT.Copy)\
                            .then_inc(act_done.sem, 1)

            @block.vector
            def _(dve):
                dve.wait_ge(pe_done.sem, 2)
                for b in range(B):
                    last = nc.vector.tensor_tensor(mod[:, :, b],
                                                   ps[:, 0, 0:N_MOD * B].rearrange("p (j b) -> p j b", j=N_MOD)[:, :, b],
                                                   vec[:, 0:N_MOD], ALU.add)
                last.then_inc(dve_done.sem, 1)
                dve.wait_ge(dve_done.sem, 8)
                for i, (norm, (sc, sh)) in enumerate(NORMS.items()):
                    for c in range(C):
                        nc.vector.tensor_scalar(affine[:, :, i, 0, c], mod[:, sc + c, :], 1.0, None, ALU.add)
                        last = nc.vector.tensor_copy(affine[:, :, i, 1, c], mod[:, sh + c, :])
                for c in range(C):
                    for i, j in enumerate((GATES["msa"], GATES["x"], GATES["mlp"])):
                        nc.vector.tensor_copy(gates[:, :, i, c], mod[:, j + c, :])
                    last = nc.vector.tensor_scalar(gates[:, :, 3, c], mod[:, GATES["mlp"] + c, :], vcol("mlp_b2", c),
                                                   None, ALU.mult)
                last.then_inc(dve_done.sem, 1)
                dve.wait_ge(dve_done.sem, 9)
                for i, name in ((2, "norm1_w"), (3, "normc_w"), (4, "norm2_w")):
                    for c in range(C):
                        last = nc.vector.tensor_scalar(affine[:, :, i, 0, c], affine[:, :, i, 0, c], vcol(name, c),
                                                       None, ALU.mult)
                dve.wait_ge(pe_done.sem, 4)
                nc.vector.tensor_copy(bp_row[:], ps[:, 1, 0:D])
                nc.vector.tensor_copy(bv_row, ps[:, 2, 0:D]).then_inc(dve_done.sem, 1)
                dve_done.at = 10
            act_done.at, pe_done.at = 5, 4

        with nc.Block() as block:
            @block.tensor
            def _(pe):
                for c in range(C):
                    for b in range(B):
                        last = nc.tensor.transpose(ps[:, c, b * P:(b + 1) * P], ctx_tok[:, b, c * P:(c + 1) * P], ident)
                last.then_inc(pe_done.sem, 1)

            @block.vector
            def _(dve):
                dve.wait_ge(pe_done.sem, 5)
                for c in range(C):
                    last = nc.vector.tensor_copy(cT_raw[:, c, :], ps[:, c, :])
                last.then_inc(dve_done.sem, 1)
            dve_done.at, pe_done.at = 11, 5
        context_norm(lambda t: ctx_tok[:, t, :], B, lambda c, g: affine[:, g, 1, 0, c:c + 1],
                   lambda c, g: affine[:, g, 1, 1, c:c + 1], cT_norm, B, P)

        with nc.Block() as block:
            @block.tensor
            def _(pe):
                for layer, (w, src) in enumerate(((w_kv, cT_norm), (w_ck, cT_raw))):
                    for m in range(C):
                        for c in range(C):
                            last = nc.tensor.matmul(ps[:, 2 * layer + m, :], w[:, c, m * P:(m + 1) * P],
                                                    src[:, c, :],
                                                    start=(c == 0), stop=(c == C - 1))
                last.then_inc(pe_done.sem, 1)
                for layer in range(2):
                    for b in range(B):
                        src, w = (cT_norm, w_kv[:, :, D:2 * D]) if layer == 0 else (cT_raw, w_cv)
                        for c in range(C):
                            last = nc.tensor.matmul(ps[:, 4 + b, layer * D:(layer + 1) * D],
                                                    src[:, c, b * P:(b + 1) * P], w[:, c, :],
                                                    start=(c == 0), stop=(c == C - 1))
                last.then_inc(pe_done.sem, 1)

            @block.vector
            def _(dve):
                dve.wait_ge(pe_done.sem, 6)
                for c in range(C):
                    for b in range(B):
                        nc.vector.tensor_scalar(kc[:, c, b, 0, :], ps[:, c, b * P:(b + 1) * P], vcol("bkv", c), None,
                                                ALU.add)
                        last = nc.vector.tensor_scalar(kc[:, c, b, 1, :], ps[:, 2 + c, b * P:(b + 1) * P],
                                                       any_ctx[:, b:b + 1], None, ALU.mult)
                last.then_inc(dve_done.sem, 1)
                dve.wait_ge(pe_done.sem, 7)
                for b in range(B):
                    nc.vector.tensor_tensor(v_ctx[:, b, 0, :], ps[:, 4 + b, 0:D], bv_row, ALU.add)
                    last = nc.vector.tensor_copy(v_ctx[:, b, 1, :], ps[:, 4 + b, D:2 * D])
                dve.wait_ge(dve_done.sem, 12)
                nc.vector.tensor_copy(kc_parts[:, 0], kc_flat).then_inc(dve_done.sem, 1)
                dve.wait_ge(dve_done.sem, 13)
                nc.vector.tensor_tensor(kc_flat, kc_flat, kc_parts[:, 0], ALU.subtract).then_inc(dve_done.sem, 1)
                dve.wait_ge(dve_done.sem, 14)
                nc.vector.tensor_copy(kc_parts[:, 1], kc_flat).then_inc(dve_done.sem, 1)
                dve.wait_ge(dve_done.sem, 15)
                nc.vector.tensor_tensor(kc_parts[:, 2], kc_flat, kc_parts[:, 1], ALU.subtract)\
                    .then_inc(dve_done.sem, 1)
                dve_done.at = 16

            @block.gpsimd
            def _(pool):
                nc.gpsimd.memset(k_ctx_all[BIAS_ROW:P], 1.0)

            @block.sync
            def _(sp):
                sp.wait_ge(late_loads.sem, late_loads.at)
            pe_done.at = 7

        with nc.Block() as block:
            @block.sync
            def _(sp):
                for h in range(NH):
                    sp.dma_start(k_ctx_all[BIAS_ROW:BIAS_ROW + 1, h, :],
                                 key_bias[0:1].rearrange("o b l k -> o (b l k)")).then_inc(k_stacked.sem, 16)
                for s, part in enumerate(K_SLOTS):
                    stack_dmas(sp, k_ctx_all, lambda i, g: kc_parts[:, i, g, :], s, part, k_stacked)
                k_stacked.at = 16 * (N_SLOT * C + NH)

            @block.vector
            def _(dve):
                nc.vector.tensor_reduce(seen, mask_raw.rearrange("p t (j k) -> p t j k", k=P), AX_X, ALU.max)\
                    .then_inc(dve_done.sem, 1)
                dve.wait_ge(dve_done.sem, 17)
                nc.vector.tensor_reduce(any_q, seen, AX_X, ALU.max).then_inc(dve_done.sem, 1)
                dve.wait_ge(dve_done.sem, 18)
                nc.vector.tensor_reduce(keep, seen.rearrange("p t k -> p k t"), AX_X, ALU.max)
                nc.vector.tensor_scalar(none_q, any_q, -MASKED, None, ALU.mult)
                nc.vector.tensor_reduce(list_tmp[:, 0:1], any_q, AX_X, ALU.min).then_inc(dve_done.sem, 1)
                dve.wait_ge(dve_done.sem, 19)
                nc.vector.tensor_scalar(list_tmp[:, 0:1], list_tmp[:, 0:1], -1.0, 1.0, ALU.mult, ALU.add)\
                    .then_inc(dve_done.sem, 1)
                dve.wait_ge(dve_done.sem, 20)
                nc.vector.tensor_scalar(keep, keep, list_tmp[:, 0:1], None, ALU.max).then_inc(dve_done.sem, 1)
                dve.wait_ge(pe_done.sem, 8)
                nc.vector.tensor_reduce(list_tmp[0:T, 1:2], ps[0:T, 0, 0:P], AX_X, ALU.max)\
                    .then_inc(dve_done.sem, 1)
                dve.wait_ge(pe_done.sem, 9)
                nc.vector.tensor_copy(list_tmp[0:T, 2:3], ps[0:T, 1, 0:1]).then_inc(dve_done.sem, 1)
                dve.wait_ge(dve_done.sem, 23)
                nc.vector.tensor_scalar(list_tmp[0:T, 8:8 + T], constant("iota")[0:T, :], list_tmp[0:T, 2:3],
                                        list_tmp[0:T, 1:2], ALU.is_equal, ALU.mult).then_inc(dve_done.sem, 1)
                dve.wait_ge(pe_done.sem, 10)
                nc.vector.tensor_copy(tile_list[0:1, :], ps[0:1, 2, 0:1 + T]).then_inc(dve_done.sem, 1)

            @block.tensor
            def _(pe):
                pe.wait_ge(dve_done.sem, 21)
                nc.tensor.transpose(ps[0:T, 0, 0:P], keep, ident).then_inc(pe_done.sem, 1)
                pe.wait_ge(dve_done.sem, 22)
                nc.tensor.matmul(ps[0:T, 1, 0:1], constant("before")[0:T, :], list_tmp[0:T, 1:2], start=True, stop=True)\
                    .then_inc(pe_done.sem, 1)
                pe.wait_ge(dve_done.sem, 24)
                nc.tensor.matmul(ps[0:1, 2, 0:1], constant("iota")[0:T, 1:2], list_tmp[0:T, 1:2], start=True, stop=True)
                nc.tensor.matmul(ps[0:1, 2, 1:1 + T], constant("tile")[0:T, :], list_tmp[0:T, 8:8 + T], start=True,
                                 stop=True).then_inc(pe_done.sem, 1)
            dve_done.at, pe_done.at = 25, 10
        for q4 in range(2):
            with nc.Block() as block:
                d0, p0 = dve_done.reserve(3), pe_done.reserve(8)

                @block.vector
                def _(dve):
                    for t in range(4):
                        tt = 4 * q4 + t
                        last = nc.vector.tensor_scalar(bias_nat[:, t, :], mask_raw[:, tt, :], 1.0, none_q[:, tt:tt + 1],
                                                       ALU.subtract, ALU.mult)
                    last.then_inc(dve_done.sem, 1)
                    for j in range(T):
                        dve.wait_ge(pe_done.sem, p0 + j + 1)
                        last = nc.vector.tensor_copy(mask_bias[:, j, q4 * HALF:(q4 + 1) * HALF],
                                                     ps[:, j % 8, :].bitcast(BF16)[:, 0:HALF])

                @block.tensor
                def _(pe):
                    pe.wait_ge(dve_done.sem, d0 + 1)
                    for j in range(T):
                        for t in range(4):
                            last = nc.tensor.transpose(ps[:, j % 8, :].bitcast(BF16)[:, t * P:(t + 1) * P],
                                                       bias_nat[:, t, j * P:(j + 1) * P], ident_bf[:])
                        last.then_inc(pe_done.sem, 1)
                dve_done.at = d0 + 1
        with nc.Block() as block:
            d0, p0, a0 = dve_done.at, pe_done.at, act_done.at

            @block.sync
            def _(sp):
                sp.wait_ge(k_stacked.sem, k_stacked.at)
                sp.dma_start(k_ctx_dram, k_ctx_all[0:STACK]).then_inc(stored.sem, 16)
                load_x(sp, 0, 0)
                sp.wait_ge(stored.sem, 16)
                sp.wait_ge(x_loaded[0].sem, 16)

            @block.scalar
            def _(act):
                for t in range(T):
                    if t >= 2:
                        act.wait_ge(pe_done.sem, p0 + t - 1)
                    nc.scalar.activation(spread[:, t % 2, :], any_q[:, t:t + 1].to_broadcast([P, P]), ACT.Copy)\
                        .then_inc(act_done.sem, 1)

            @block.tensor
            def _(pe):
                for t in range(T):
                    pe.wait_ge(act_done.sem, a0 + t + 1)
                    nc.tensor.matmul(ps[:, t // 4, (t % 4) * P:(t % 4 + 1) * P], spread[:, t % 2, :], ident, start=True,
                                     stop=True).then_inc(pe_done.sem, 1)

            @block.vector
            def _(dve):
                dve.wait_ge(pe_done.sem, p0 + T)
                for half in range(2):
                    for k, table in enumerate((cos_k, sin_k)):
                        nc.vector.tensor_tensor(rope_q[:, k, half * HALF:(half + 1) * HALF], ps[:, half, :], table,
                                                ALU.mult)
        clear_signals()
        first_tile = nc.values_load(tile_list[0:1, 1:2], min_val=0, max_val=T - 1)
        n_tiles = nc.values_load(tile_list[0:1, 0:1], min_val=1, max_val=T)

        with nc.Fori(0, B) as b:
            def gate_weights():
                gs0, gr0, ga0 = gate_spread.reserve(8), gate_rows.reserve(4), gated.reserve(4)

                def act(act):
                    for i in range(4):
                        for c in range(C):
                            if i >= 1:
                                act.wait_ge(gate_rows.sem, gr0 + i)
                            nc.scalar.activation(spread[:, c, :], gates_b[:, i, c:c + 1].to_broadcast([P, P]),
                                                 ACT.Copy).then_inc(gate_spread.sem, 1)

                def pe(pe):
                    for i in range(4):
                        for c in range(C):
                            pe.wait_ge(gate_spread.sem, gs0 + C * i + c + 1)
                            at = c * P
                            last = nc.tensor.matmul(ps[:, i, at:at + P], spread[:, c, :], ident,
                                                    start=True, stop=True)
                        last.then_inc(gate_rows.sem, 1)

                def dve(dve):
                    for i, (w, at, n) in enumerate(((w_out, 0, C), (w_co, C, C), (w_2, 2 * C, FF // P), (None, 0, 0))):
                        dve.wait_ge(gate_rows.sem, gr0 + i + 1)
                        row = ps[:, i, 0:D]
                        if w is None:
                            nc.vector.tensor_copy(gb2_row[:], row).then_inc(gated.sem, 1)
                        else:
                            nc.vector.tensor_tensor(w_gated[:, at:at + n, :], w[:],
                                                    row.rearrange("p (o d) -> p o d", o=1).to_broadcast([P, n, D]),
                                                    ALU.mult).then_inc(gated.sem, 1)
                return Stage(act=act, pe=pe, dve=dve, done=ga0 + 4)

            def finish(weighs, outs, norms):
                def pe(pe):
                    weighs[0].pe(pe)
                    weighs[1].pe(pe)
                    outs[0].pe(pe)
                    outs[1].pe(pe)

                def dve(dve):
                    weighs[0].dve(dve)
                    weighs[1].dve(dve)
                    outs[0].dve(dve)
                    norms[0].dve(dve)
                    outs[1].dve(dve)
                    norms[1].dve(dve)
                return Stage(pe=pe, dve=dve)

            def cross_attention(layer, norms, w_query, bias, weights, row, extra, next_norm):
                rows = [add_bias(u, norms[u], row) for u in range(2)] if row is not None else [None, None]
                queries = [query(u, w_query, bias, norms[u]) for u in range(2)]

                def k_of(h, rows, n):
                    return k_ctx[0:rows, h, layer * P:layer * P + n]

                def free_max(u):
                    def wait(pe):
                        pe.wait_ge(q_stacked[u].sem, queries[u].done)
                        if u == 0 and extra is not None:
                            pe.wait_ge(gated.sem, extra.done)
                            pe.wait_ge(loads.sem, 32)
                    return wait
                maxes = [scores_max(u, lambda h, rows: k_of(h, rows, LC), LC, None, False, free_max(u))
                         for u in range(2)]
                turns = [turn_max(u, maxes[u].done) for u in range(2)]

                def free_out(u):
                    def wait(pe, g):
                        if u == 0:
                            pe.wait_ge(max_rest1.sem, turns[g].read)
                    return wait
                sums_ = [weigh(u, lambda h, rows: k_of(h, rows, P), v_pad[:, 0], None, False,
                               turns[u].done, free_out(u)) for u in range(2)]
                outs = [project_back(u, xT_tile(u), weights, C,
                                     lambda pe, u=u: pe.wait_ge(normed.sem, sums_[u].done),
                                     rows[u].done if rows[u] else None) for u in range(2)]
                after = [norm(u, next_norm, outs[u].done) for u in range(2)]
                end = finish(sums_, outs, after)

                def pe(pe):
                    norms[0].pe(pe)
                    queries[0].pe(pe)
                    norms[1].pe(pe)
                    queries[1].pe(pe)
                    if extra is not None:
                        extra.pe(pe)
                    maxes[0].pe(pe, 0, 8)
                    maxes[1].pe(pe, 0, 4)
                    turns[0].pe(pe)
                    maxes[1].pe(pe, 4, 8)
                    pe.wait_ge(max_taken.sem, maxes[1].done)
                    turns[1].pe(pe)
                    end.pe(pe)

                def act(act):
                    norms[0].act(act)
                    queries[0].act_high(act)
                    norms[1].act(act)
                    queries[0].act_middle(act)
                    queries[1].act_high(act)
                    queries[1].act_middle(act)
                    if extra is not None:
                        extra.act(act)
                    turns[0].act(act)
                    turns[1].act(act)
                    sums_[0].act(act)
                    sums_[1].act(act)

                def dve(dve):
                    queries[0].dve(dve)
                    queries[0].dve_low(dve)
                    queries[1].dve(dve)
                    queries[1].dve_low(dve)
                    if extra is not None:
                        extra.dve(dve)
                    maxes[0].dve(dve, 0, 8)
                    maxes[1].dve(dve, 0, 4)
                    turns[0].dve(dve)
                    maxes[1].dve(dve, 4, 8)
                    turns[1].dve(dve)
                    end.dve(dve)

                def pool(pool):
                    for u in range(2):
                        if rows[u] is not None:
                            rows[u].pool(pool)
                    turns[0].pool(pool)
                    turns[1].pool(pool)
                    after[0].pool(pool)
                    after[1].pool(pool)

                def sp(sp):
                    for stage in (queries[0], queries[1], turns[0], turns[1]):
                        stage.sp(sp)
                return Stage(pe=pe, act=act, dve=dve, pool=pool, sp=sp), after

            def biases(j):
                return lambda cols: mask_bias[:, bass.ds(j, 1), cols].rearrange("p o q -> p (o q)")

            def stack_key_tile(sp, j, sets=None):
                for part in range(3):
                    if sets is not None:
                        sp.wait_ge(*sets[0].ready[part])
                        sp.wait_ge(*sets[1].ready[part])
                    for s in range(N_SLOT):
                        if K_SLOTS[s] == part:
                            stack_dmas(sp, k_self, lambda i, g: k_parts[:, i, g, bass.ds(j * P, P)], s, part, k_stacked)

            def key_stack(h, rows):
                return k_self[0:rows, h, :]

            def self_inputs(norms):
                ro0, ra0, mo0 = rope_step.reserve(8), rope_added.reserve(8), moved.reserve(4)
                pr0 = product.reserve(12)
                k_sets = [parts_of(u, k_rest, k_parts, None) for u in range(2)]
                q_sets = [parts_of(u, q_rest, q_parts, None) for u in range(2)]

                def chunks(pe, u, at):
                    for m in range(C):
                        for c in range(C):
                            last = nc.tensor.matmul(ps[:, 4 + 2 * u + m, :], w_qkv[:, c, at + m * P:at + (m + 1) * P],
                                                    xT[:, c, u * HALF:(u + 1) * HALF],
                                                    start=(c == 0), stop=(c == C - 1))
                        last.then_inc(product.sem, 1)

                def values(pe, u):
                    for k in (2 * u, 2 * u + 1):
                        for t in (2 * k, 2 * k + 1):
                            for c in range(C):
                                last = nc.tensor.matmul(ps[:, k, (t % 2) * D:(t % 2 + 1) * D],
                                                        xT[:, c, t * P:(t + 1) * P], w_qkv[:, c, 2 * D:3 * D],
                                                        start=(c == 0), stop=(c == C - 1))
                        last.then_inc(product.sem, 1)

                k_at, v_at, q_at = (0, 4), (2, 8), (6, 10)

                def pe(pe):
                    norms[0].pe(pe)
                    pe.wait_ge(xT_ready.sem, norms[0].done)
                    chunks(pe, 0, D)
                    values(pe, 0)
                    norms[1].pe(pe)
                    pe.wait_ge(xT_ready.sem, norms[1].done)
                    chunks(pe, 1, D)
                    pe.wait_ge(rope_step.sem, ro0 + 2)
                    chunks(pe, 0, 0)
                    values(pe, 1)
                    pe.wait_ge(rope_step.sem, ro0 + 4)
                    chunks(pe, 1, 0)

                def rope(dve, n):
                    is_q, u, m = n // 4, n // 2 % 2, n % 2
                    cols = slice(u * HALF, (u + 1) * HALF)
                    dst = (q_rest if is_q else k_rest)[:, m, cols]
                    cos, sin = (rope_q[:, 0, cols], rope_q[:, 1, cols]) if is_q else (cos_k, sin_k)
                    dve.wait_ge(product.sem, pr0 + (q_at if is_q else k_at)[u] + m + 1)
                    nc.vector.tensor_tensor(dst, ps[:, 4 + 2 * u + m, :], cos, ALU.mult)
                    if n >= 2:
                        dve.wait_ge(rope_added.sem, ra0 + n - 1)
                    if m == 0:
                        dve.wait_ge(product.sem, pr0 + (q_at if is_q else k_at)[u] + 2)
                    nc.vector.tensor_tensor(turned[:, m, :], ps[:, 5 + 2 * u - m, :], sin, ALU.mult)\
                        .then_inc(rope_step.sem, 1)

                def rope_add(pool, n):
                    is_q, u, m = n // 4, n // 2 % 2, n % 2
                    dst = (q_rest if is_q else k_rest)[:, m, u * HALF:(u + 1) * HALF]
                    pool.wait_ge(rope_step.sem, ro0 + n + 1)
                    nc.gpsimd.tensor_tensor(dst, dst, turned[:, m, :], ALU.subtract if m == 0 else ALU.add)\
                        .then_inc(rope_added.sem, 1)

                def turned_wait(first):
                    return lambda act, m: act.wait_ge(rope_added.sem, ra0 + first + m + 1)

                def dve(dve):
                    for n in range(4):
                        rope(dve, n)
                    k_sets[0].dve(dve)
                    rope(dve, 4)
                    rope(dve, 5)
                    k_sets[1].dve(dve)
                    q_sets[0].dve(dve)
                    rope(dve, 6)
                    rope(dve, 7)
                    q_sets[0].dve_low(dve)
                    q_sets[1].dve(dve)
                    q_sets[1].dve_low(dve)

                def pool(pool):
                    for n in range(4):
                        rope_add(pool, n)
                    k_sets[0].pool(pool)
                    rope_add(pool, 4)
                    rope_add(pool, 5)
                    k_sets[1].pool(pool)
                    rope_add(pool, 6)
                    rope_add(pool, 7)
                    nc.gpsimd.memset(sums[:], 0.0)
                    pool.wait_ge(moved.sem, mo0 + 4)
                    pad_v(nc.gpsimd, 1, v_self[:, bass.ds(first_tile, 1), :].rearrange("p o d -> p (o d)"))
                    pool.wait_ge(product.sem, pr0 + 12)
                    nc.gpsimd.memset(xT[:], 0.0)

                def move_v(act, u):
                    for k in (2 * u, 2 * u + 1):
                        act.wait_ge(product.sem, pr0 + v_at[u] + k % 2 + 1)
                        nc.scalar.activation(v_self[:, 2 * k:2 * k + 2, :].rearrange("p t d -> p (t d)"),
                                             ps[:, k, :], ACT.Copy).then_inc(moved.sem, 1)

                def act(act):
                    norms[0].act(act)
                    move_v(act, 0)
                    norms[1].act(act)
                    k_sets[0].act_high(act, turned_wait(0))
                    k_sets[1].act_high(act, turned_wait(2))
                    k_sets[0].act_middle(act)
                    q_sets[0].act_high(act, turned_wait(4))
                    k_sets[1].act_middle(act)
                    move_v(act, 1)
                    q_sets[0].act_middle(act)
                    q_sets[1].act_high(act, turned_wait(6))
                    q_sets[1].act_middle(act)

                def sp(sp):
                    stack_key_tile(sp, first_tile, k_sets)
                    for u in range(2):
                        stack_q(sp, u, q_sets[u])

                def free_max(u):
                    def wait(pe):
                        pe.wait_ge(k_stacked.sem, 16 * N_SLOT * C)
                        pe.wait_ge(q_stacked[u].sem, stacks_at[u])
                        if u == 0:
                            pe.wait_ge(moved.sem, mo0 + 4)
                    return wait
                stacks_at = [q_stacked[u].reserve(16 * N_SLOT * C) + 16 * N_SLOT * C for u in range(2)]
                maxes = [scores_max(u, key_stack, P, biases(first_tile), False, free_max(u)) for u in range(2)]
                return Stage(pe=pe, act=act, dve=dve, pool=pool, sp=sp), maxes

            with nc.Block() as block:
                gates_of = gate_weights()
                norms = [norm(u, 0, None) for u in range(2)]
                x_loaded[1].reserve(16)
                loads.reserve(32)
                first, after = cross_attention(0, norms, w_q, lambda m: vcol("bq", m), w_p, bp_row,
                                                     gates_of, 2)
                inputs, first_max = self_inputs(after)
                turns = [turn_max(u, first_max[u].done) for u in range(2)]

                @block.tensor
                def _(pe):
                    first.pe(pe)
                    inputs.pe(pe)
                    first_max[0].pe(pe, 0, 8)
                    first_max[1].pe(pe, 0, 4)
                    turns[0].pe(pe)
                    first_max[1].pe(pe, 4, 8)
                    turns[1].pe(pe)

                @block.scalar
                def _(act):
                    first.act(act)
                    inputs.act(act)
                    turns[0].act(act)
                    turns[1].act(act)

                @block.vector
                def _(dve):
                    nc.vector.tensor_copy(affine_b[:].rearrange("p n k c -> p (n k c)"),
                                          affine[:, bass.ds(b, 1)].rearrange("p o n k c -> p (o n k c)"))
                    nc.vector.tensor_copy(gates_b[:].rearrange("p n c -> p (n c)"),
                                          gates[:, bass.ds(b, 1)].rearrange("p o n c -> p (o n c)"))
                    norms[0].dve(dve)
                    dve.wait_ge(x_loaded[1].sem, 16)
                    norms[1].dve(dve)
                    first.dve(dve)
                    inputs.dve(dve)
                    first_max[0].dve(dve, 0, 8)
                    first_max[1].dve(dve, 0, 4)
                    turns[0].dve(dve)
                    first_max[1].dve(dve, 4, 8)
                    turns[1].dve(dve)

                @block.gpsimd
                def _(pool):
                    pad_v(nc.gpsimd, 0, v_ctx[:, bass.ds(b, 1), 0, :].rearrange("p o d -> p (o d)"))
                    norms[0].pool(pool)
                    norms[1].pool(pool)
                    first.pool(pool)
                    inputs.pool(pool)
                    turns[0].pool(pool)
                    turns[1].pool(pool)

                @block.sync
                def _(sp):
                    load_x(sp, b, 1)
                    sp.dma_start(q_stack[BIAS_ROW:BIAS_ROW + 1].rearrange("o u h s -> o (u h s)"), ones_row[:])\
                        .then_inc(loads.sem, 16)
                    sp.dma_start(k_ctx[0:STACK], k_ctx_dram[:, :, bass.ds(b * (2 * P), 2 * P)]).then_inc(loads.sem, 16)
                    first.sp(sp)
                    inputs.sp(sp)
                    for u in range(2):
                        turns[u].sp(sp)
                    for u in range(2):
                        sp.wait_ge(q_stacked[u].sem, turns[u].done)
            clear_signals()

            with nc.If(n_tiles > 1):
                with nc.Fori(1, n_tiles) as i:
                    j = nc.values_load(tile_list[0:1, bass.ds(i + 1, 1)], min_val=0, max_val=T - 1)
                    with nc.Block() as block:
                        maxes = [scores_max(u, key_stack, P, biases(j), True,
                                            lambda pe: pe.wait_ge(k_stacked.sem, 16 * N_SLOT * C)) for u in range(2)]

                        @block.sync
                        def _(sp):
                            stack_key_tile(sp, j)

                        @block.tensor
                        def _(pe):
                            maxes[0].pe(pe, 0, 8)
                            maxes[1].pe(pe, 0, 8)

                        @block.vector
                        def _(dve):
                            for u in range(2):
                                maxes[u].dve(dve, 0, 8)
                                dve.wait_ge(max_taken.sem, maxes[u].done)
                                nc.vector.tensor_tensor(neg_max[:, u], neg_max[:, u], tile_max[:, u], ALU.min)
                    clear_signals()
                with nc.Block() as block:
                    turns = [turn_max(u, None) for u in range(2)]

                    @block.tensor
                    def _(pe):
                        turns[0].pe(pe)
                        turns[1].pe(pe)

                    @block.scalar
                    def _(act):
                        turns[0].act(act)
                        turns[1].act(act)

                    @block.vector
                    def _(dve):
                        turns[0].dve(dve)
                        turns[1].dve(dve)

                    @block.gpsimd
                    def _(pool):
                        turns[0].pool(pool)
                        turns[1].pool(pool)

                    @block.sync
                    def _(sp):
                        turns[0].sp(sp)
                        turns[1].sp(sp)
                        for u in range(2):
                            sp.wait_ge(q_stacked[u].sem, q_stacked[u].at)
                clear_signals()
                with nc.Fori(1, n_tiles) as i:
                    j = nc.values_load(tile_list[0:1, bass.ds(i + 1, 1)], min_val=0, max_val=T - 1)
                    with nc.Block() as block:
                        pa0 = pool_done.reserve(1)
                        weighs = [weigh(u, key_stack, v_pad[:, 1], biases(j), True, None, lambda pe, g: None)
                                  for u in range(2)]

                        @block.sync
                        def _(sp):
                            stack_key_tile(sp, j)

                        @block.gpsimd
                        def _(pool):
                            pad_v(nc.gpsimd, 1, v_self[:, bass.ds(j, 1), :].rearrange("p o d -> p (o d)"))\
                                .then_inc(pool_done.sem, 1)

                        @block.tensor
                        def _(pe):
                            pe.wait_ge(k_stacked.sem, 16 * N_SLOT * C)
                            pe.wait_ge(pool_done.sem, pa0 + 1)
                            weighs[0].pe(pe)
                            weighs[1].pe(pe)

                        @block.scalar
                        def _(act):
                            weighs[0].act(act)
                            weighs[1].act(act)

                        @block.vector
                        def _(dve):
                            weighs[0].dve(dve)
                            weighs[1].dve(dve)
                    clear_signals()
                with nc.Block() as block:
                    @block.sync
                    def _(sp):
                        stack_key_tile(sp, first_tile)
                        sp.wait_ge(k_stacked.sem, 16 * N_SLOT * C)

                    @block.gpsimd
                    def _(pool):
                        pad_v(nc.gpsimd, 1, v_self[:, bass.ds(first_tile, 1), :].rearrange("p o d -> p (o d)"))
                clear_signals()

            with nc.Block() as block:
                weighs = [weigh(u, key_stack, v_pad[:, 1], biases(first_tile), "last", None, lambda pe, g: None)
                          for u in range(2)]
                self_out = [project_back(u, xT_tile(u), w_gated[:, 0:C], C,
                                         lambda pe, u=u: pe.wait_ge(normed.sem, weighs[u].done), None)
                            for u in range(2)]
                after = [norm(u, 3, self_out[u].done) for u in range(2)]
                self_end = finish(weighs, self_out, after)
                second, norms = cross_attention(1, after, w_cq, lambda m: 0.0,
                                                      w_gated[:, C:2 * C], None, None, 4)
                rows = [add_bias(u, norms[u], gb2_row) for u in range(2)]
                F = FF // P
                pr0, mo0 = product.reserve(2 * F), moved.reserve(2 * F)
                mlp_out = [project_back(u, lambda c, k, u=u: hidden[:, u, c, k * P:(k + 1) * P],
                                        w_gated[:, 2 * C:2 * C + F], F,
                                        lambda pe, u=u: pe.wait_ge(moved.sem, mo0 + (u + 1) * F), rows[u].done)
                           for u in range(2)]

                @block.tensor
                def _(pe):
                    self_end.pe(pe)
                    second.pe(pe)
                    norms[0].pe(pe)
                    for n in range(2 * F):
                        u, f = n // F, n % F
                        if n == F - 2:
                            norms[1].pe(pe)
                        if f == 0:
                            pe.wait_ge(xT_ready.sem, norms[u].done)
                        if n >= 4:
                            pe.wait_ge(moved.sem, mo0 + n - 3)
                        for c in range(C):
                            last = nc.tensor.matmul(ps[:, 4 + n % 4, :], w_1[:, c, f * P:(f + 1) * P],
                                                    xT[:, c, u * HALF:(u + 1) * HALF],
                                                    start=(c == 0), stop=(c == C - 1))
                        last.then_inc(product.sem, 1)
                    mlp_out[0].pe(pe)
                    mlp_out[1].pe(pe)

                @block.scalar
                def _(act):
                    weighs[0].act(act)
                    weighs[1].act(act)
                    second.act(act)
                    norms[0].act(act)
                    for n in range(2 * F):
                        if n == F - 2:
                            norms[1].act(act)
                        act.wait_ge(product.sem, pr0 + n + 1)
                        nc.scalar.activation(hidden[:, n // F, n % F, :], ps[:, 4 + n % 4, :], ACT.Gelu_apprx_tanh,
                                             bias=vcol("mlp_b1", n % F)).then_inc(moved.sem, 1)

                @block.vector
                def _(dve):
                    self_end.dve(dve)
                    second.dve(dve)
                    mlp_out[0].dve(dve)
                    mlp_out[1].dve(dve)

                @block.gpsimd
                def _(pool):
                    pad_v(nc.gpsimd, 0, v_ctx[:, bass.ds(b, 1), 1, :].rearrange("p o d -> p (o d)"))
                    after[0].pool(pool)
                    after[1].pool(pool)
                    second.pool(pool)
                    rows[0].pool(pool)
                    rows[1].pool(pool)

                @block.sync
                def _(sp):
                    second.sp(sp)
                    for u in range(2):
                        sp.wait_ge(x_ready.sem, mlp_out[u].done)
                        sp.dma_start(out[b, u * HALF:(u + 1) * HALF, :].rearrange("(t p) d -> p t d", p=P),
                                     x[:, 4 * u:4 * u + 4, :]).then_inc(stored.sem, 16)
                        sp.wait_ge(stored.sem, 16 * (u + 1))
                        if u == 0:
                            load_x(sp, (b + 1) % B, 0)
                    sp.wait_ge(x_loaded[0].sem, 16)
            clear_signals()


_NAMES = {
    "x": "x", "ctx": "ctx_1024", "cond": "cond_1024", "ctx_mask": "mask_BxS2_bf1", "mask": "mask_SxS_bk0",
    "Wq": "L0_xcond_Wq", "bq": "L0_xcond_bq", "Wkv": "L0_xcond_Wkv", "bkv": "L0_xcond_bkv", "Wp": "L0_xcond_Wp",
    "bp": "L0_xcond_bp", "Wss_q": "L0_xcond_Wss_q", "bss_q": "L0_xcond_bss_q", "Wss_kv": "L0_xcond_Wss_kv",
    "bss_kv": "L0_xcond_bss_kv", "adaLN_W": "L1_xcond_adaLN_W", "adaLN_b": "L1_xcond_adaLN_b",
    "norm1_w": "L1_xcond_norm1_w", "qkv_W": "L1_xcond_qkv_W", "attn_out_W": "L1_xcond_attn_out_W",
    "normc_w": "L1_xcond_normc_w", "cq_W": "L1_xcond_cq_W", "ck_W": "L1_xcond_ck_W", "cv_W": "L1_xcond_cv_W",
    "co_W": "L1_xcond_co_W", "norm2_w": "L1_xcond_norm2_w", "mlp_W1": "L1_xcond_mlp_W1",
    "mlp_b1": "L1_xcond_mlp_b1", "mlp_W2": "L1_xcond_mlp_W2", "mlp_b2": "L1_xcond_mlp_b2",
}


def by_component(v):
    import numpy as np
    return np.ascontiguousarray(v.reshape(-1, NH, HD).swapaxes(1, 2)).reshape(v.shape)


def shape_consts():
    import numpy as np
    t = np.zeros((P, CONST_N), np.float32)

    def put(name, v):
        at, n = CONST_COLS[name]
        t[:v.shape[0], at:at + n] = v
    put("ident", np.eye(P, dtype=np.float32))
    inv_freq = 1.0 / 10000.0 ** (np.arange(0, HD, 2, dtype=np.float32) / HD)
    angle = np.outer(np.arange(S // 2, dtype=np.float32), inv_freq).T
    component = np.arange(P) // NH
    put("cos", np.cos(angle)[component].astype(np.float32))
    put("sin", np.sin(angle)[component].astype(np.float32))
    i = np.arange(T)
    put("before", (i[:, None] < i[None, :]).astype(np.float32))
    put("iota", np.tile(i.astype(np.float32), (T, 1)))
    put("tile", i[:, None].astype(np.float32))
    return t


def kernel(**inputs):
    import numpy as np
    import concourse.bacc as bacc
    from concourse.bass_utils import run_bass_kernel_spmd

    nc = bacc.Bacc("TRN2", target_bir_lowering=False, num_devices=1, dynamic_dma_scratch_size=1024)
    arrays, aps = {}, {}
    given = {short: np.ascontiguousarray(inputs[name]) for short, name in _NAMES.items()}
    for short in ("Wq", "bq", "cq_W", "ck_W"):
        given[short] = by_component(given[short])
    for short, n in (("Wkv", D), ("bkv", D), ("qkv_W", 2 * D)):
        given[short] = np.concatenate([by_component(given[short][..., :n]), given[short][..., n:]], axis=-1)
    given["shape_consts"] = shape_consts()
    for short, v in given.items():
        arrays[f"in_{short}"] = v
        aps[short] = nc.dram_tensor(f"in_{short}", v.shape, mybir.dt.from_np(v.dtype), kind="ExternalInput").ap()
    out = nc.dram_tensor("out_0", (B, S, D), F32, kind="ExternalOutput").ap()
    build(nc, aps, out)
    r = run_bass_kernel_spmd(nc, [arrays], core_ids=[0])
    return r.results[0]["out_0"]
```
